# Optimizing a Trainium2 kernel written in Bass

```python
import numpy as np
import jax
import jax.numpy as jnp

def _softmax(x, axis=-1):
    return jax.nn.softmax(x, axis=axis)

def _gelu(x):
    return jax.nn.gelu(x, approximate=True)

def _silu(x):
    return jax.nn.silu(x)

def _sigmoid(x):
    return jax.nn.sigmoid(x)

def _layernorm(x, axis=-1, eps=1e-05):
    m = jnp.mean(x, axis=axis, keepdims=True)
    v = jnp.var(x, axis=axis, keepdims=True)
    return (x - m) / jnp.sqrt(v + eps)

def _scatter_add(tgt, idx, src, axis=0):
    return tgt.at[idx].add(src)

def _segment_sum(src, seg, n):
    return jax.ops.segment_sum(src, seg, n)
kernel_name = 'mk_audio_tower_d2_tok_audfeat1024_r4_9b015f'

def setup_inputs(seed: int=0):
    np.random.seed(seed)
    _w = jnp.asarray

    def _rec_inputs():
        import jax
        import jax.numpy as jnp
        _rk = jax.random.key(seed)
        x = -0.000392918 + 0.999932 * jax.random.normal(jax.random.fold_in(_rk, 1), (64, 125, 128), jnp.float32)
        return x
    x = _rec_inputs()

    def _L0_tok_setup():
        import jax, jax.numpy as jnp
        import numpy as np
        K = 8
        H = 8
        L = 2
        D = 256

        def _ln(x, s, b, eps=1e-12):
            m = jnp.mean(x, axis=-1, keepdims=True)
            v = jnp.mean((x - m) ** 2, axis=-1, keepdims=True)
            return (x - m) / jnp.sqrt(v + eps) * s + b
        key = jax.random.key(seed)
        keys = iter(jax.random.split(key, 16))

        def w(shape, scale=0.02):
            return jax.random.normal(next(keys), shape, jnp.float32) * scale
        return dict(x=jax.random.normal(next(keys), (8, 1024, 128), jnp.float32), w1=w((512, 1024)), b1=jnp.zeros((512,), jnp.float32), w2=w((256, 512)), b2=jnp.zeros((256,), jnp.float32), ln1_s=jnp.ones((L, D), jnp.float32), ln1_b=jnp.zeros((L, D), jnp.float32), wq=w((L, D, D)), bq=jnp.zeros((L, D), jnp.float32), wk=w((L, D, D)), bk=jnp.zeros((L, D), jnp.float32), wv=w((L, D, D)), bv=jnp.zeros((L, D), jnp.float32), wo=w((L, D, D)), bo=jnp.zeros((L, D), jnp.float32), ln2_s=jnp.ones((L, D), jnp.float32), ln2_b=jnp.zeros((L, D), jnp.float32), ffw1=w((L, D // 4, D)), ffb1=jnp.zeros((L, D // 4), jnp.float32), ffw2=w((L, D, D // 4)), ffb2=jnp.zeros((L, D), jnp.float32))
    _L0_tok_all = _L0_tok_setup()
    _L0_tok_in = {k: v for k, v in _L0_tok_all.items() if k in ('w1', 'b1', 'w2', 'b2', 'ln1_s', 'ln1_b', 'wq', 'bq', 'wk', 'bk', 'wv', 'bv', 'wo', 'bo', 'ln2_s', 'ln2_b', 'ffw1', 'ffb1', 'ffw2', 'ffb2')}
    del _L0_tok_all

    def _L0_attn_setup():
        import jax, jax.numpy as jnp
        import numpy as np
        from math import sqrt
        N_HEAD = 16
        W_SCALE = 0.02

        def _reference_tuple_inner(x, W_dq, W_uq, W_dkv, W_uk, W_uv, W_o):
            B, T, C = x.shape
            nh = N_HEAD
            hs = C // nh
            n_kvl = W_dkv.shape[0]
            k_eff = (W_dq.T @ W_uq.T @ W_uk).reshape(nh, hs, n_kvl)
            v_eff = jnp.transpose((W_uv.T @ W_o.T).reshape(n_kvl, nh, hs), (1, 0, 2))
            c_kv = x @ W_dkv.T
            q = x @ W_dq.T @ W_uq.T
            q = q.reshape(B, T, nh, hs)
            q_lat = jnp.einsum('bqhd,hdl->bhql', q, k_eff)
            attn = jnp.einsum('bhql,bkl->bhqk', q_lat, c_kv) / sqrt(hs)
            causal = jnp.tril(jnp.ones((T, T), dtype=bool))
            attn = jnp.where(causal[None, None], attn, -jnp.inf)
            attn = jax.nn.softmax(attn, axis=-1)
            y_lat = jnp.einsum('bhqk,bkl->bhql', attn, c_kv)
            y = jnp.einsum('bhql,hld->bqhd', y_lat, v_eff).reshape(B, T, C)
            return (y, c_kv)
        key = jax.random.key(seed)
        ks = jax.random.split(key, 7)
        B, T, C = (2, 512, 256)
        QL, KVL = (128, 128)
        return {'x': jax.random.normal(ks[0], (B, T, C), dtype=jnp.float32), 'W_dq': jax.random.normal(ks[1], (QL, C), dtype=jnp.float32) * W_SCALE, 'W_uq': jax.random.normal(ks[2], (C, QL), dtype=jnp.float32) * W_SCALE, 'W_dkv': jax.random.normal(ks[3], (KVL, C), dtype=jnp.float32) * W_SCALE, 'W_uk': jax.random.normal(ks[4], (C, KVL), dtype=jnp.float32) * W_SCALE, 'W_uv': jax.random.normal(ks[5], (C, KVL), dtype=jnp.float32) * W_SCALE, 'W_o': jax.random.normal(ks[6], (C, C), dtype=jnp.float32) * W_SCALE}
    _L0_attn_all = _L0_attn_setup()
    _L0_attn_in = {k: v for k, v in _L0_attn_all.items() if k in ('W_dq', 'W_uq', 'W_dkv', 'W_uk', 'W_uv', 'W_o')}
    del _L0_attn_all

    def _L0_ffn_setup():
        import jax, jax.numpy as jnp
        import numpy as np
        QP = 127.0
        MIN_RANGE = 1e-06

        def _ste_round(x):
            return x + jax.lax.stop_gradient(jnp.round(x) - x)

        def _quant_per_tensor(x):
            scale = jnp.maximum(jnp.max(jnp.abs(x)), MIN_RANGE) / QP
            return (_ste_round(x / scale), scale)

        def _qlinear(x2d, w, b):
            xq, sx = _quant_per_tensor(x2d)
            wq, sw = _quant_per_tensor(w)
            out = jnp.matmul(xq, wq.T) + b[None, :]
            return out * (sw * sx)
        key = jax.random.key(seed)
        k = jax.random.split(key, 5)
        B, N, D, H = (8, 256, 256, 1024)
        return {'x': jax.random.normal(k[0], (B, N, D), dtype=jnp.float32), 'w1': jax.random.normal(k[1], (H, D), dtype=jnp.float32) * 0.02, 'b1': jax.random.normal(k[2], (H,), dtype=jnp.float32) * 0.02, 'w2': jax.random.normal(k[3], (D, H), dtype=jnp.float32) * 0.02, 'b2': jax.random.normal(k[4], (D,), dtype=jnp.float32) * 0.02}
    _L0_ffn_all = _L0_ffn_setup()
    _L0_ffn_in = {k: v for k, v in _L0_ffn_all.items() if k in ('w1', 'b1', 'w2', 'b2')}
    del _L0_ffn_all

    def _L1_attn_setup():
        import jax, jax.numpy as jnp
        import numpy as np
        EPS = 1e-05

        def rmsnorm(x, w):
            return x * jax.lax.rsqrt(jnp.mean(x * x, axis=-1, keepdims=True) + EPS) * w

        def depthwise_conv1d(x, w, b):
            k = w.shape[-1]
            p = (k - 1) // 2
            y = jax.lax.conv_general_dilated(x, w, window_strides=(1,), padding=[(p, p)], feature_group_count=x.shape[1], dimension_numbers=('NCH', 'OIH', 'NCH'))
            return y + b[None, :, None]

        def selective_scan(u, delta, A, B, C, D):

            def step(h, inp):
                d_t, B_t, C_t, u_t = inp
                dA = jnp.exp(d_t[..., None] * A)
                h = dA * h + (d_t * u_t)[..., None] * B_t[:, None, :]
                y = jnp.einsum('bdn,bn->bd', h, C_t)
                return (h, y)
            b, l, d_in = u.shape
            n = A.shape[1]
            h0 = jnp.zeros((b, d_in, n), u.dtype)
            xs = (jnp.moveaxis(delta, 1, 0), jnp.moveaxis(B, 1, 0), jnp.moveaxis(C, 1, 0), jnp.moveaxis(u, 1, 0))
            _, ys = jax.lax.scan(step, h0, xs)
            return jnp.moveaxis(ys, 0, 1) + u * D

        def mamba_block(x, Wi, bi, cw, cb, Wx, Wdt, bdt, A_log, D, Wo, bo, dt_rank, n):
            d_inner = A_log.shape[0]
            xr = x @ Wi.T + bi
            xs, res = jnp.split(xr, 2, axis=-1)
            xs = depthwise_conv1d(jnp.swapaxes(xs, 1, 2), cw, cb)
            xs = jax.nn.silu(jnp.swapaxes(xs, 1, 2))
            x_dbl = xs @ Wx.T
            dlt, B, C = jnp.split(x_dbl, [dt_rank, dt_rank + n], axis=-1)
            delta = jax.nn.softplus(dlt @ Wdt.T + bdt)
            A = -jnp.exp(A_log)
            y = selective_scan(xs, delta, A, B, C, D)
            y = y * jax.nn.silu(res)
            return y @ Wo.T + bo
        key = jax.random.key(seed)
        L, b, l, d, di, n, dtr, k = (2, 4, 256, 256, 512, 16, 64, 5)
        ks = jax.random.split(key, 12)
        s = lambda kk, shape, scale: jax.random.normal(kk, shape, jnp.float32) * scale
        inp = {'x': s(ks[0], (b, l, d), 1.0), 'in_proj_w': s(ks[1], (L, 2 * di, d), d ** (-0.5)), 'in_proj_b': s(ks[2], (L, 2 * di), 0.02), 'conv_w': s(ks[3], (L, di, 1, k), k ** (-0.5)), 'conv_b': s(ks[4], (L, di), 0.02), 'x_proj_w': s(ks[5], (L, dtr + 2 * n, di), di ** (-0.5)), 'dt_proj_w': s(ks[6], (L, di, dtr), dtr ** (-0.5)), 'dt_proj_b': s(ks[7], (L, di), 0.02), 'A_log': jnp.broadcast_to(jnp.log(jnp.arange(1, n + 1, dtype=jnp.float32)), (L, di, n)) * 1.0, 'D': jnp.ones((L, di), jnp.float32), 'out_proj_w': s(ks[8], (L, d, di), di ** (-0.5)), 'out_proj_b': s(ks[9], (L, d), 0.02), 'norm_w': jnp.ones((L, d), jnp.float32), 'norm_f_w': jnp.ones((d,), jnp.float32)}
        return inp
    _L1_attn_all = _L1_attn_setup()
    _L1_attn_in = {k: v for k, v in _L1_attn_all.items() if k in ('in_proj_w', 'in_proj_b', 'conv_w', 'conv_b', 'x_proj_w', 'dt_proj_w', 'dt_proj_b', 'A_log', 'D', 'out_proj_w', 'out_proj_b', 'norm_w', 'norm_f_w')}
    del _L1_attn_all

    def _L1_ffn_setup():
        import jax, jax.numpy as jnp
        import numpy as np
        CAPACITY_FACTOR = 0.5
        key = jax.random.key(seed)
        ks = jax.random.split(key, 5)
        B, S, D, F = (4, 1024, 256, 1024)
        scale_in = 1.0 / np.sqrt(D)
        scale_ff = 1.0 / np.sqrt(F)
        return {'hidden_states': jax.random.normal(ks[0], (B, S, D), dtype=jnp.float32), 'w_router': jax.random.normal(ks[1], (D,), dtype=jnp.float32) * scale_in, 'W1': jax.random.normal(ks[2], (D, F), dtype=jnp.float32) * scale_in, 'b1': jnp.zeros((F,), dtype=jnp.float32), 'W2': jax.random.normal(ks[3], (F, D), dtype=jnp.float32) * scale_ff, 'b2': jnp.zeros((D,), dtype=jnp.float32)}
    _L1_ffn_all = _L1_ffn_setup()
    _L1_ffn_in = {k: v for k, v in _L1_ffn_all.items() if k in ('w_router', 'W1', 'b1', 'W2', 'b2')}
    del _L1_ffn_all
    return {'x': x, 'L0_tok_w1': _L0_tok_in['w1'], 'L0_tok_b1': _L0_tok_in['b1'], 'L0_tok_w2': _L0_tok_in['w2'], 'L0_tok_b2': _L0_tok_in['b2'], 'L0_tok_ln1_s': _L0_tok_in['ln1_s'], 'L0_tok_ln1_b': _L0_tok_in['ln1_b'], 'L0_tok_wq': _L0_tok_in['wq'], 'L0_tok_bq': _L0_tok_in['bq'], 'L0_tok_wk': _L0_tok_in['wk'], 'L0_tok_bk': _L0_tok_in['bk'], 'L0_tok_wv': _L0_tok_in['wv'], 'L0_tok_bv': _L0_tok_in['bv'], 'L0_tok_wo': _L0_tok_in['wo'], 'L0_tok_bo': _L0_tok_in['bo'], 'L0_tok_ln2_s': _L0_tok_in['ln2_s'], 'L0_tok_ln2_b': _L0_tok_in['ln2_b'], 'L0_tok_ffw1': _L0_tok_in['ffw1'], 'L0_tok_ffb1': _L0_tok_in['ffb1'], 'L0_tok_ffw2': _L0_tok_in['ffw2'], 'L0_tok_ffb2': _L0_tok_in['ffb2'], 'L0_attn_W_dq': _L0_attn_in['W_dq'], 'L0_attn_W_uq': _L0_attn_in['W_uq'], 'L0_attn_W_dkv': _L0_attn_in['W_dkv'], 'L0_attn_W_uk': _L0_attn_in['W_uk'], 'L0_attn_W_uv': _L0_attn_in['W_uv'], 'L0_attn_W_o': _L0_attn_in['W_o'], 'L0_ffn_w1': _L0_ffn_in['w1'], 'L0_ffn_b1': _L0_ffn_in['b1'], 'L0_ffn_w2': _L0_ffn_in['w2'], 'L0_ffn_b2': _L0_ffn_in['b2'], 'L1_attn_in_proj_w': _L1_attn_in['in_proj_w'], 'L1_attn_in_proj_b': _L1_attn_in['in_proj_b'], 'L1_attn_conv_w': _L1_attn_in['conv_w'], 'L1_attn_conv_b': _L1_attn_in['conv_b'], 'L1_attn_x_proj_w': _L1_attn_in['x_proj_w'], 'L1_attn_dt_proj_w': _L1_attn_in['dt_proj_w'], 'L1_attn_dt_proj_b': _L1_attn_in['dt_proj_b'], 'L1_attn_A_log': _L1_attn_in['A_log'], 'L1_attn_D': _L1_attn_in['D'], 'L1_attn_out_proj_w': _L1_attn_in['out_proj_w'], 'L1_attn_out_proj_b': _L1_attn_in['out_proj_b'], 'L1_attn_norm_w': _L1_attn_in['norm_w'], 'L1_attn_norm_f_w': _L1_attn_in['norm_f_w'], 'L1_ffn_w_router': _L1_ffn_in['w_router'], 'L1_ffn_W1': _L1_ffn_in['W1'], 'L1_ffn_b1': _L1_ffn_in['b1'], 'L1_ffn_W2': _L1_ffn_in['W2'], 'L1_ffn_b2': _L1_ffn_in['b2']}

def reference(x, L0_tok_w1, L0_tok_b1, L0_tok_w2, L0_tok_b2, L0_tok_ln1_s, L0_tok_ln1_b, L0_tok_wq, L0_tok_bq, L0_tok_wk, L0_tok_bk, L0_tok_wv, L0_tok_bv, L0_tok_wo, L0_tok_bo, L0_tok_ln2_s, L0_tok_ln2_b, L0_tok_ffw1, L0_tok_ffb1, L0_tok_ffw2, L0_tok_ffb2, L0_attn_W_dq, L0_attn_W_uq, L0_attn_W_dkv, L0_attn_W_uk, L0_attn_W_uv, L0_attn_W_o, L0_ffn_w1, L0_ffn_b1, L0_ffn_w2, L0_ffn_b2, L1_attn_in_proj_w, L1_attn_in_proj_b, L1_attn_conv_w, L1_attn_conv_b, L1_attn_x_proj_w, L1_attn_dt_proj_w, L1_attn_dt_proj_b, L1_attn_A_log, L1_attn_D, L1_attn_out_proj_w, L1_attn_out_proj_b, L1_attn_norm_w, L1_attn_norm_f_w, L1_ffn_w_router, L1_ffn_W1, L1_ffn_b1, L1_ffn_W2, L1_ffn_b2):
    import jax
    import jax.numpy as jnp

    def _L0_tok_ref(x, w1, b1, w2, b2, ln1_s, ln1_b, wq, bq, wk, bk, wv, bv, wo, bo, ln2_s, ln2_b, ffw1, ffb1, ffw2, ffb2):
        import jax, jax.numpy as jnp
        import numpy as np
        K = 8
        H = 8
        L = 2
        D = 256

        def _ln(x, s, b, eps=1e-12):
            m = jnp.mean(x, axis=-1, keepdims=True)
            v = jnp.mean((x - m) ** 2, axis=-1, keepdims=True)
            return (x - m) / jnp.sqrt(v + eps) * s + b
        B, S, Dm = x.shape
        chunk = (S - 1) // K + 1
        pad = chunk * K - S
        x = jnp.pad(x, ((0, 0), (0, pad), (0, 0)))
        x = x.reshape(B, chunk, Dm * K)
        x = jax.nn.relu(x @ w1.T + b1) @ w2.T + b2
        dk = D // H
        scale = 1.0 / jnp.sqrt(jnp.float32(dk))
        for i in range(L):
            h = _ln(x, ln1_s[i], ln1_b[i])
            q = (h @ wq[i].T + bq[i]).reshape(B, chunk, H, dk)
            k = (h @ wk[i].T + bk[i]).reshape(B, chunk, H, dk)
            v = (h @ wv[i].T + bv[i]).reshape(B, chunk, H, dk)
            scores = jnp.einsum('bqhd,bkhd->bhqk', q, k) * scale
            attn = jax.nn.softmax(scores, axis=-1)
            o = jnp.einsum('bhqk,bkhd->bqhd', attn, v).reshape(B, chunk, D)
            x = x + (o @ wo[i].T + bo[i])
            h = _ln(x, ln2_s[i], ln2_b[i])
            x = x + jax.nn.relu(h @ ffw1[i].T + ffb1[i]) @ ffw2[i].T + ffb2[i]
        return x

    def _L0_attn_ref(x, W_dq, W_uq, W_dkv, W_uk, W_uv, W_o):
        import jax, jax.numpy as jnp
        import numpy as np
        from math import sqrt
        N_HEAD = 16
        W_SCALE = 0.02

        def _reference_tuple_inner(x, W_dq, W_uq, W_dkv, W_uk, W_uv, W_o):
            B, T, C = x.shape
            nh = N_HEAD
            hs = C // nh
            n_kvl = W_dkv.shape[0]
            k_eff = (W_dq.T @ W_uq.T @ W_uk).reshape(nh, hs, n_kvl)
            v_eff = jnp.transpose((W_uv.T @ W_o.T).reshape(n_kvl, nh, hs), (1, 0, 2))
            c_kv = x @ W_dkv.T
            q = x @ W_dq.T @ W_uq.T
            q = q.reshape(B, T, nh, hs)
            q_lat = jnp.einsum('bqhd,hdl->bhql', q, k_eff)
            attn = jnp.einsum('bhql,bkl->bhqk', q_lat, c_kv) / sqrt(hs)
            causal = jnp.tril(jnp.ones((T, T), dtype=bool))
            attn = jnp.where(causal[None, None], attn, -jnp.inf)
            attn = jax.nn.softmax(attn, axis=-1)
            y_lat = jnp.einsum('bhqk,bkl->bhql', attn, c_kv)
            y = jnp.einsum('bhql,hld->bqhd', y_lat, v_eff).reshape(B, T, C)
            return (y, c_kv)
        return _reference_tuple_inner(x, W_dq, W_uq, W_dkv, W_uk, W_uv, W_o)[0]

    def _L0_ffn_ref(x, w1, b1, w2, b2):
        import jax, jax.numpy as jnp
        import numpy as np
        QP = 127.0
        MIN_RANGE = 1e-06

        def _ste_round(x):
            return x + jax.lax.stop_gradient(jnp.round(x) - x)

        def _quant_per_tensor(x):
            scale = jnp.maximum(jnp.max(jnp.abs(x)), MIN_RANGE) / QP
            return (_ste_round(x / scale), scale)

        def _qlinear(x2d, w, b):
            xq, sx = _quant_per_tensor(x2d)
            wq, sw = _quant_per_tensor(w)
            out = jnp.matmul(xq, wq.T) + b[None, :]
            return out * (sw * sx)
        B, N, D = x.shape
        h = _qlinear(x.reshape(-1, D), w1, b1)
        h = jax.nn.gelu(h, approximate=False)
        o = _qlinear(h, w2, b2)
        return o.reshape(B, N, -1)

    def _L1_attn_ref(x, in_proj_w, in_proj_b, conv_w, conv_b, x_proj_w, dt_proj_w, dt_proj_b, A_log, D, out_proj_w, out_proj_b, norm_w, norm_f_w):
        import jax, jax.numpy as jnp
        import numpy as np
        EPS = 1e-05

        def rmsnorm(x, w):
            return x * jax.lax.rsqrt(jnp.mean(x * x, axis=-1, keepdims=True) + EPS) * w

        def depthwise_conv1d(x, w, b):
            k = w.shape[-1]
            p = (k - 1) // 2
            y = jax.lax.conv_general_dilated(x, w, window_strides=(1,), padding=[(p, p)], feature_group_count=x.shape[1], dimension_numbers=('NCH', 'OIH', 'NCH'))
            return y + b[None, :, None]

        def selective_scan(u, delta, A, B, C, D):

            def step(h, inp):
                d_t, B_t, C_t, u_t = inp
                dA = jnp.exp(d_t[..., None] * A)
                h = dA * h + (d_t * u_t)[..., None] * B_t[:, None, :]
                y = jnp.einsum('bdn,bn->bd', h, C_t)
                return (h, y)
            b, l, d_in = u.shape
            n = A.shape[1]
            h0 = jnp.zeros((b, d_in, n), u.dtype)
            xs = (jnp.moveaxis(delta, 1, 0), jnp.moveaxis(B, 1, 0), jnp.moveaxis(C, 1, 0), jnp.moveaxis(u, 1, 0))
            _, ys = jax.lax.scan(step, h0, xs)
            return jnp.moveaxis(ys, 0, 1) + u * D

        def mamba_block(x, Wi, bi, cw, cb, Wx, Wdt, bdt, A_log, D, Wo, bo, dt_rank, n):
            d_inner = A_log.shape[0]
            xr = x @ Wi.T + bi
            xs, res = jnp.split(xr, 2, axis=-1)
            xs = depthwise_conv1d(jnp.swapaxes(xs, 1, 2), cw, cb)
            xs = jax.nn.silu(jnp.swapaxes(xs, 1, 2))
            x_dbl = xs @ Wx.T
            dlt, B, C = jnp.split(x_dbl, [dt_rank, dt_rank + n], axis=-1)
            delta = jax.nn.softplus(dlt @ Wdt.T + bdt)
            A = -jnp.exp(A_log)
            y = selective_scan(xs, delta, A, B, C, D)
            y = y * jax.nn.silu(res)
            return y @ Wo.T + bo
        n = A_log.shape[-1]
        dt_rank = x_proj_w.shape[1] - 2 * n
        h = x
        for i in range(in_proj_w.shape[0]):
            h = h + mamba_block(rmsnorm(h, norm_w[i]), in_proj_w[i], in_proj_b[i], conv_w[i], conv_b[i], x_proj_w[i], dt_proj_w[i], dt_proj_b[i], A_log[i], D[i], out_proj_w[i], out_proj_b[i], dt_rank, n)
        return rmsnorm(h, norm_f_w)

    def _L1_ffn_ref(hidden_states, w_router, W1, b1, W2, b2):
        import jax, jax.numpy as jnp
        import numpy as np
        CAPACITY_FACTOR = 0.5
        'Mixture-of-Depths block: route top-k tokens through an FFN inner block,\n            scatter back with sigmoid router weights; bypassed tokens pass through.'
        B, S, D = hidden_states.shape
        k = int(S * CAPACITY_FACTOR)
        scores = jnp.einsum('bsd,d->bs', hidden_states, w_router)
        top_scores, top_idx = jax.lax.top_k(scores, k)
        weights = jax.nn.sigmoid(top_scores)
        selected = jnp.take_along_axis(hidden_states, top_idx[:, :, None], axis=1)
        h = jax.nn.gelu(jnp.einsum('bkd,df->bkf', selected, W1) + b1)
        processed = jnp.einsum('bkf,fd->bkd', h, W2) + b2
        update = weights[:, :, None] * processed

        def scatter_one(xb, ib, ub):
            return xb.at[ib].add(ub)
        output = jax.vmap(scatter_one)(hidden_states, top_idx, update)
        return output
    h = _L0_tok_ref(x, L0_tok_w1, L0_tok_b1, L0_tok_w2, L0_tok_b2, L0_tok_ln1_s, L0_tok_ln1_b, L0_tok_wq, L0_tok_bq, L0_tok_wk, L0_tok_bk, L0_tok_wv, L0_tok_bv, L0_tok_wo, L0_tok_bo, L0_tok_ln2_s, L0_tok_ln2_b, L0_tok_ffw1, L0_tok_ffb1, L0_tok_ffw2, L0_tok_ffb2)
    h = h + _L0_attn_ref(_layernorm(h, axis=-1), L0_attn_W_dq, L0_attn_W_uq, L0_attn_W_dkv, L0_attn_W_uk, L0_attn_W_uv, L0_attn_W_o)
    h = h + _L0_ffn_ref(_layernorm(h, axis=-1), L0_ffn_w1, L0_ffn_b1, L0_ffn_w2, L0_ffn_b2)
    h = h + _L1_attn_ref(_layernorm(h, axis=-1), L1_attn_in_proj_w, L1_attn_in_proj_b, L1_attn_conv_w, L1_attn_conv_b, L1_attn_x_proj_w, L1_attn_dt_proj_w, L1_attn_dt_proj_b, L1_attn_A_log, L1_attn_D, L1_attn_out_proj_w, L1_attn_out_proj_b, L1_attn_norm_w, L1_attn_norm_f_w)
    h = h + _L1_ffn_ref(_layernorm(h, axis=-1), L1_ffn_w_router, L1_ffn_W1, L1_ffn_b1, L1_ffn_W2, L1_ffn_b2)
    return h

_drawn_inputs = setup_inputs


def setup_inputs(seed=0):
    import zlib

    import numpy as np

    out = dict(_drawn_inputs(seed))
    spreads = {'L0_tok_b1': (0.0, 0.1),
     'L0_tok_b2': (0.0, 0.1),
     'L0_tok_ln1_s': (1.0, 0.2),
     'L0_tok_ln1_b': (0.0, 0.1),
     'L0_tok_bq': (0.0, 0.8),
     'L0_tok_bk': (0.0, 0.8),
     'L0_tok_bv': (0.0, 0.1),
     'L0_tok_bo': (0.0, 0.1),
     'L0_tok_ln2_s': (1.0, 0.2),
     'L0_tok_ln2_b': (0.0, 0.308),
     'L0_tok_ffb1': (0.0, 0.1),
     'L0_tok_ffb2': (0.0, 0.1),
     'L1_attn_D': (1.0, 0.2),
     'L1_attn_norm_w': (1.0, 0.2),
     'L1_attn_norm_f_w': (1.0, 0.2),
     'L1_ffn_b1': (0.0, 0.731),
     'L1_ffn_b2': (0.0, 0.499)}
    factors = {'L0_tok_wq': 4.419,
     'L0_tok_wk': 4.059,
     'L0_attn_W_dq': 8.0,
     'L0_attn_W_uq': 8.0,
     'L0_attn_W_uk': 8.0,
     'L0_ffn_b1': 8.0,
     'L0_ffn_b2': 8.0,
     'L1_attn_in_proj_b': 2.896,
     'L1_attn_dt_proj_b': 7.676}
    for name, (base, spread) in spreads.items():
        noise = np.random.default_rng([zlib.crc32(name.encode()), seed]).standard_normal(out[name].shape)
        drawn = base * np.exp(spread * noise) if base else spread * noise
        out[name] = jnp.asarray(drawn.astype(out[name].dtype))
    for name, factor in factors.items():
        out[name] = (out[name] * factor).astype(out[name].dtype)
    return out
```

```python
from contextlib import ExitStack

import concourse.bass as bass
from concourse import mybir

F32 = mybir.dt.float32
BF16 = mybir.dt.bfloat16
ALU = mybir.AluOpType
ACT = mybir.ActivationFunctionType
AX = mybir.AxisListType.X
RMAX = bass.bass_isa.ReduceOp.max

P = 128
SEQS, T, D = 64, 16, 256
TOKENS = SEQS * T
GROUP = 512
GROUPS = TOKENS // GROUP
TILES = GROUP // P
DT = D // P
EPS = 1e-5
TOK_EPS = 1e-12
LAYERS = 2
MLP_IN, MLP_HID = 1024, 512
TOK_HEADS, TOK_DK = 8, 32
TOK_FF = D // 4
MLA_HEADS, MLA_HS, LATENT = 16, 16, 128
FFN = 1024
SEMAPHORES = 64
ROUND = 12582912.0
INNER, STATE, RANK, CONV = 512, 16, 64, 5
TOP = 8


class Memory:
    pass


class Steps:

    def __init__(self, eng, sem):
        self.eng, self.sem, self.n = eng, sem, 0

    def step(self, ins):
        ins.then_inc(self.sem, 1)
        self.n += 1
        return self.n

    def settle(self):
        if self.n:
            self.eng.wait_ge(self.sem, self.n)


def named(mem, names):
    names = names.split()
    return dict(zip(names, mem.pool[:len(names)], strict=True))


def end_block(nc, mem):
    nc.gpsimd.sem_clear(mem.numbers)
    nc.all_engine_barrier()


class Arena:

    def __init__(self, tensor, size):
        self.tensor, self.size, self.at = tensor, size, 0

    def take(self, *shape, dtype=F32, rows=P):
        n = 1
        for x in shape:
            n *= x
        words = n if dtype == F32 else (n + 1) // 2
        view = self.tensor[0:rows, self.at:self.at + words]
        self.at += words
        assert self.at <= self.size, (self.at, self.size)
        if dtype != F32:
            view = view.bitcast(dtype)
        if len(shape) > 1:
            names = " ".join(f"d{i}" for i in range(len(shape)))
            sizes = {f"d{i}": x for i, x in enumerate(shape) if i}
            view = view.rearrange(f"p ({names}) -> p {names}", **sizes)
        return view


def spread(ap, axis, n):
    shape = list(ap.shape)
    shape.insert(axis, n)
    return ap.unsqueeze(axis).broadcast_to(shape)


def norm_stats(v, own, src, stats, mv, stats_ready):
    for t in range(TILES):
        own.step(v.bn_stats(stats[:, t, :], src[:, t, :]))
    own.settle()
    for t in range(TILES):
        ins = v.bn_aggr(mv[:, t, :], stats[:, t, :])
        if t < TILES - 1:
            own.step(ins)
    own.settle()
    ins.then_inc(stats_ready, 1)


def norm_rstd(pool, own, var, rstd, minus_half, eps, rstd_ready, n):
    own.settle()
    own.step(pool.tensor_scalar(rstd, var, 1.0, eps, ALU.mult, ALU.add))
    own.settle()
    pool.tensor_tensor(rstd, rstd, minus_half, ALU.pow).then_inc(rstd_ready, 1)
    pool.wait_ge(rstd_ready, n)


def norm_apply(v, src, mv, rstd, z, z_ready):
    for t in range(TILES):
        v.tensor_scalar(z[:, t, :], src[:, t, :], mv[:, t, 0:1], rstd[:, t:t + 1],
                        ALU.subtract, ALU.mult).then_inc(z_ready, 1)


def turn_tiles(pe, z, ident, banks, turned):
    for f in range(DT):
        for t in range(TILES):
            ins = pe.transpose(banks[:, f, t * P:(t + 1) * P], z[:, t, f * P:(f + 1) * P], ident)
        ins.then_inc(turned, 1)


def token_mlp(nc, ctx, mem, dram):
    s = named(mem, " ".join(f"slice{k}" for k in range(8)) +
                      " small hid_sum hid_ready out_sum out_ready")
    slices = [s["slice0"], s["slice1"], s["slice2"], s["slice3"], s["slice4"], s["slice5"], s["slice6"], s["slice7"]]
    KT, HT = MLP_IN // P, MLP_HID // P
    a = mem.fresh()
    w1 = a.take(KT, MLP_HID)
    x = a.take(KT, TOKENS)
    w2 = a.take(HT, D)
    b1 = a.take(HT)
    b2 = a.take(D)
    hid = a.take(GROUPS, HT, GROUP)
    ps, res = mem.ps, mem.res

    with nc.Block() as block:
        @block.sync
        def _(sp):
            for k in range(KT):
                sp.dma_start(w1[:, k, :], dram["tok_w1"][:, k, :]).then_inc(slices[k], 16)
                sp.dma_start(x[:, k, :], dram["tok_x"][:, k, :]).then_inc(slices[k], 16)

        @block.scalar
        def _(act):
            act.dma_start(mem.consts, dram["consts"]).then_inc(s["small"], 16)
            act.dma_start(b1, dram["tok_b1"]).then_inc(s["small"], 16)
            act.dma_start(b2, dram["tok_b2"]).then_inc(s["small"], 16)
            act.dma_start(w2, dram["tok_w2"]).then_inc(s["small"], 16)
            act.wait_ge(s["small"], 64)
            for g in range(GROUPS):
                for m in range(HT):
                    act.wait_ge(s["hid_sum"], g * HT + m + 1)
                    act.activation(hid[:, g, m, :], ps[:, 4 * g + m, :], ACT.Relu,
                                   bias=b1[:, m:m + 1]).then_inc(s["hid_ready"], 1)

        @block.tensor
        def _(pe):
            for k in range(KT):
                pe.wait_ge(slices[k], 32)
                for g in range(GROUPS):
                    for m in range(HT):
                        ins = pe.matmul(ps[:, 4 * g + m, :], w1[:, k, m * P:(m + 1) * P],
                                        x[:, k, g * GROUP:(g + 1) * GROUP],
                                        start=(k == 0), stop=(k == KT - 1))
                        if k == KT - 1:
                            ins.then_inc(s["hid_sum"], 1)
            pe.wait_ge(s["small"], 64)
            for g in range(GROUPS):
                pe.wait_ge(s["hid_ready"], (g + 1) * HT)
                for t in range(TILES):
                    for k in range(HT):
                        ins = pe.matmul(ps[:, 4 * g + t // 2, (t % 2) * D:(t % 2 + 1) * D],
                                        hid[:, g, k, t * P:(t + 1) * P], w2[:, k, :],
                                        start=(k == 0), stop=(k == HT - 1))
                    if t % 2:
                        ins.then_inc(s["out_sum"], 1)

        @block.vector
        def _(v):
            v.wait_ge(s["small"], 64)
            for g in range(GROUPS):
                for h in range(2):
                    v.wait_ge(s["out_sum"], 2 * g + h + 1)
                    t = TILES * g + 2 * h
                    v.tensor_tensor(res[:, t:t + 2, :],
                                    ps[:, 4 * g + h, :].rearrange("p (t d) -> p t d", t=2),
                                    spread(b2, 1, 2), ALU.add).then_inc(s["out_ready"], 1)
    end_block(nc, mem)


def attention_layers(nc, ctx, mem, dram):
    s = named(mem, """cols_in qkv_in wo_in ff_in rows_in
        stats rstd z turned hT q_sum q k_sum k v_sum v s_sum s_ready e p o_sum o
        wo_sum bo_added res1 f_sum f f2_sum res2 v_own p_own""")
    a = mem.fresh()
    wqkv = a.take(DT, 3 * D)
    wo = a.take(DT, D)
    ff1 = a.take(DT, TOK_FF)
    ff2 = a.take(D, rows=TOK_FF + 1)
    cols = a.take(16)
    rows = a.take(2, D)
    stats, mv, rstd = a.take(GROUPS, TILES, 6), a.take(GROUPS, TILES, 2), a.take(GROUPS, TILES)
    z, hT = a.take(GROUPS, TILES, D), a.take(GROUPS, DT, GROUP)
    qT, kT = a.take(GROUPS, DT, GROUP), a.take(GROUPS, DT, GROUP)
    val = a.take(GROUPS, TILES, D)
    sc, pT = a.take(GROUPS, 4, 8 * 32), a.take(GROUPS, 4, 8 * 32)
    small = a.take(GROUPS, 2, 32)
    oT = a.take(GROUPS, DT, GROUP)
    fT = a.take(GROUPS, GROUP, rows=TOK_FF + 1)
    ps, res = mem.ps, mem.res
    SCALE = TOK_DK ** -0.5

    def tiles_of(g):
        return res[:, TILES * g:TILES * (g + 1), :]

    def two_tiles(g, b):
        return ps[:, 4 * g + b, :].rearrange("p (t d) -> p t d", t=2)

    with nc.Fori(0, LAYERS) as layer:
        with nc.Block() as block:
            @block.sync
            def _(sp):
                sp.dma_start(cols, dram["enc_cols"][layer, :, :]).then_inc(s["cols_in"], 16)
                sp.dma_start(wqkv, dram["enc_wqkv"][layer, :, :, :]).then_inc(s["qkv_in"], 16)
                sp.dma_start(rows, dram["enc_rows"][layer, :, :, :]).then_inc(s["rows_in"], 16)
                sp.dma_start(wo, dram["enc_wo"][layer, :, :, :]).then_inc(s["wo_in"], 16)
                sp.dma_start(ff1, dram["enc_ff1"][layer, :, :, :]).then_inc(s["ff_in"], 16)
                sp.dma_start(ff2, dram["enc_ff2"][layer, :, :]).then_inc(s["ff_in"], 16)

            @block.gpsimd
            def _(pool):
                own = Steps(pool, s["p_own"])
                own.step(pool.memset(fT[TOK_FF:TOK_FF + 1, :, :], 1.0))
                for j in range(2):
                    for g in range(GROUPS):
                        pool.wait_ge(s["stats"], 2 * j + g + 1)
                        norm_rstd(pool, own, mv[:, g, :, 1], rstd[:, g, :], mem.minus_half,
                                  TOK_EPS, s["rstd"], 2 * j + g + 1)
                    if j == 0:
                        pool.wait_ge(s["rows_in"], 16)
                        for g in range(GROUPS):
                            pool.wait_ge(s["z"], TILES * (g + 1))
                            pool.tensor_tensor(tiles_of(g), tiles_of(g), spread(rows[:, 1, :], 1, TILES),
                                               ALU.add).then_inc(s["bo_added"], 1)
                            pool.wait_ge(s["bo_added"], g + 1)

            @block.vector
            def _(v):
                own = Steps(v, s["v_own"])

                def norm(j):
                    for g in range(GROUPS):
                        norm_stats(v, own, tiles_of(g), stats[:, g], mv[:, g], s["stats"])
                    for g in range(GROUPS):
                        v.wait_ge(s["rstd"], 2 * j + g + 1)
                        norm_apply(v, tiles_of(g), mv[:, g], rstd[:, g], z[:, g], s["z"])

                norm(0)
                v.wait_ge(s["cols_in"], 16)
                for g in range(GROUPS):
                    for m in range(DT):
                        v.wait_ge(s["k_sum"], DT * g + m + 1)
                        v.tensor_scalar(kT[:, g, m, :], ps[:, 4 * g + m, :], cols[:, 6 + m:7 + m], None,
                                        ALU.add).then_inc(s["k"], 1)
                v.wait_ge(s["rows_in"], 16)
                for g in range(GROUPS):
                    for b in range(2):
                        v.wait_ge(s["v_sum"], 2 * g + b + 1)
                        v.tensor_tensor(val[:, g, 2 * b:2 * b + 2, :], two_tiles(g, 2 + b),
                                        spread(rows[:, 0, :], 1, 2), ALU.add).then_inc(s["v"], 1)
                for g in range(GROUPS):
                    v.wait_ge(s["s_sum"], g + 1)
                    rows32 = sc[:, g].rearrange("p r (j k) -> p (r j) k", k=32)
                    own.step(v.tensor_tensor(
                        sc[:, g].rearrange("p r (j k) -> p r j k", k=32),
                        ps[:, 4 * g:4 * g + 4, 0:256].rearrange("p r (j k) -> p r j k", k=32),
                        spread(spread(mem.same_seq, 1, 8), 1, 4), ALU.add))
                    own.settle()
                    own.step(v.tensor_reduce(small[:, g, 0, :], rows32, AX, ALU.max))
                    own.settle()
                    v.tensor_tensor(rows32, rows32, spread(small[:, g, 0, :], 2, 32),
                                    ALU.subtract).then_inc(s["s_ready"], 1)
                for g in range(GROUPS):
                    v.wait_ge(s["e"], g + 1)
                    rows32 = sc[:, g].rearrange("p r (j k) -> p (r j) k", k=32)
                    own.step(v.tensor_reduce(small[:, g, 1, :], rows32, AX, ALU.add))
                    own.settle()
                    own.step(v.reciprocal(small[:, g, 0, :], small[:, g, 1, :]))
                    own.settle()
                    own.step(v.tensor_tensor(rows32, rows32, spread(small[:, g, 0, :], 2, 32), ALU.mult))
                    own.settle()
                    v.transpose(pT[:, g].rearrange("p r c -> p (r c)"),
                                sc[:, g].rearrange("p r c -> p (r c)")).then_inc(s["p"], 1)
                for g in range(GROUPS):
                    v.wait_ge(s["bo_added"], g + 1)
                    for b in range(2):
                        v.wait_ge(s["wo_sum"], 2 * g + b + 1)
                        two = res[:, TILES * g + 2 * b:TILES * g + 2 * b + 2, :]
                        v.tensor_tensor(two, two, two_tiles(g, b), ALU.add).then_inc(s["res1"], 1)
                v.wait_ge(s["res1"], 2 * GROUPS)
                norm(1)
                for g in range(GROUPS):
                    for b in range(2):
                        v.wait_ge(s["f2_sum"], 2 * g + b + 1)
                        two = res[:, TILES * g + 2 * b:TILES * g + 2 * b + 2, :]
                        v.tensor_tensor(two, two, two_tiles(g, 2 + b), ALU.add).then_inc(s["res2"], 1)

            @block.scalar
            def _(act):
                act.wait_ge(s["cols_in"], 16)

                def turned(j, base):
                    for g in range(GROUPS):
                        for f in range(DT):
                            act.wait_ge(s["turned"], GROUPS * DT * j + DT * g + f + 1)
                            act.activation(hT[:, g, f, :], ps[:, 4 * g + 2 * j + f, :], ACT.Identity,
                                           bias=cols[:, base + 2 + f:base + 3 + f],
                                           scale=cols[:, base + f:base + f + 1]).then_inc(s["hT"], 1)

                turned(0, 0)
                for g in range(GROUPS):
                    for m in range(DT):
                        act.wait_ge(s["q_sum"], DT * g + m + 1)
                        act.activation(qT[:, g, m, :], ps[:, 4 * g + 2 + m, :], ACT.Identity,
                                       bias=cols[:, 4 + m:5 + m]).then_inc(s["q"], 1)
                for g in range(GROUPS):
                    act.wait_ge(s["s_ready"], g + 1)
                    both = sc[:, g].rearrange("p r c -> p (r c)")
                    act.activation(both, both, ACT.Exp, scale=SCALE).then_inc(s["e"], 1)
                for g in range(GROUPS):
                    act.wait_ge(s["o_sum"], g + 1)
                    for hh in range(2):
                        act.activation(
                            oT[:, g, hh, :].rearrange("p (t i q) -> p i t q", t=TILES, i=4),
                            ps[:, 4 * g:4 * g + 4, hh * P:(hh + 1) * P].rearrange("p i (t q) -> p i t q", q=32),
                            ACT.Copy).then_inc(s["o"], 1)
                turned(1, 8)
                for g in range(GROUPS):
                    act.wait_ge(s["f_sum"], g + 1)
                    act.activation(fT[0:TOK_FF, g, :], ps[0:TOK_FF, 4 * g, :], ACT.Relu,
                                   bias=cols[0:TOK_FF, 12:13]).then_inc(s["f"], 1)

            @block.tensor
            def _(pe):
                def turn(j):
                    for g in range(GROUPS):
                        if j == 1:
                            pe.wait_ge(s["o"], 2 * (g + 1))
                        pe.wait_ge(s["z"], GROUPS * TILES * j + TILES * (g + 1))
                        turn_tiles(pe, z[:, g], mem.ident, ps[:, 4 * g + 2 * j:4 * g + 2 * j + 2, :], s["turned"])

                def columns(g, bank, w, at, done):
                    for m in range(DT):
                        for k in range(DT):
                            ins = pe.matmul(ps[:, bank + m, :], w[:, k, at + m * P:at + (m + 1) * P],
                                            hT[:, g, k, :], start=(k == 0), stop=(k == DT - 1))
                        ins.then_inc(done, 1)

                def tokens(bank, src, w, done, K=DT):
                    for t in range(TILES):
                        for k in range(K):
                            ins = pe.matmul(ps[:, bank + t // 2, (t % 2) * D:(t % 2 + 1) * D],
                                            src(k)[:, t * P:(t + 1) * P], w(k),
                                            start=(k == 0), stop=(k == K - 1))
                        if t % 2:
                            ins.then_inc(done, 1)

                turn(0)
                pe.wait_ge(s["qkv_in"], 16)
                for g in range(GROUPS):
                    pe.wait_ge(s["hT"], DT * (g + 1))
                    columns(g, 4 * g + 2, wqkv, 0, s["q_sum"])
                    columns(g, 4 * g, wqkv, D, s["k_sum"])
                for g in range(GROUPS):
                    pe.wait_ge(s["q"], DT * (g + 1))
                    tokens(4 * g + 2, lambda k: hT[:, g, k, :], lambda k: wqkv[:, k, 2 * D:3 * D], s["v_sum"])
                for g in range(GROUPS):
                    pe.wait_ge(s["k"], DT * (g + 1))
                    pe.wait_ge(s["v"], 2 * (g + 1))
                    for t in range(TILES):
                        for hh in range(2):
                            for i in range(4):
                                for r in range(4):
                                    at = slice(t * P + 32 * i, t * P + 32 * i + 32)
                                    ins = pe.matmul(ps[32 * i:32 * i + 32, 4 * g + r, (2 * t + hh) * 32:(2 * t + hh + 1) * 32],
                                                    qT[32 * r:32 * r + 32, g, hh, at],
                                                    kT[32 * r:32 * r + 32, g, hh, at],
                                                    start=True, stop=True)
                    ins.then_inc(s["s_sum"], 1)
                for g in range(GROUPS):
                    pe.wait_ge(s["p"], g + 1)
                    for hh in range(2):
                        for t in range(TILES):
                            for r in range(4):
                                for i in range(4):
                                    rows_i = slice(32 * i, 32 * i + 32)
                                    ins = pe.matmul(ps[32 * r:32 * r + 32, 4 * g + i, hh * P + t * 32:hh * P + (t + 1) * 32],
                                                    val[rows_i, g, t, (4 * hh + r) * 32:(4 * hh + r + 1) * 32],
                                                    pT[rows_i, g, r, (2 * t + hh) * 32:(2 * t + hh + 1) * 32],
                                                    start=True, stop=True)
                    ins.then_inc(s["o_sum"], 1)
                pe.wait_ge(s["wo_in"], 16)
                for g in range(GROUPS):
                    pe.wait_ge(s["o"], 2 * (g + 1))
                    tokens(4 * g, lambda k: oT[:, g, k, :], lambda k: wo[:, k, :], s["wo_sum"])
                turn(1)
                pe.wait_ge(s["ff_in"], 32)
                for g in range(GROUPS):
                    pe.wait_ge(s["res1"], 2 * (g + 1))
                    pe.wait_ge(s["hT"], DT * GROUPS + DT * (g + 1))
                    for k in range(DT):
                        ins = pe.matmul(ps[0:TOK_FF, 4 * g, :], ff1[:, k, :], hT[:, g, k, :],
                                        start=(k == 0), stop=(k == DT - 1))
                    ins.then_inc(s["f_sum"], 1)
                pe.wait_ge(s["p_own"], 1)
                for g in range(GROUPS):
                    pe.wait_ge(s["f"], g + 1)
                    tokens(4 * g + 2, lambda k: fT[:, g, :], lambda k: ff2, s["f2_sum"], K=1)
        end_block(nc, mem)


def absolute_max(v, own, out, src):
    own.step(v.tensor_reduce(out, src, AX, ALU.max, apply_absolute_value=True))


def quantiser(v, own, most, scale, inverse):
    own.step(v.tensor_scalar(scale, most, 1e-6, 1.0 / 127.0, ALU.max, ALU.mult))
    own.settle()
    own.step(v.reciprocal(inverse, scale))
    own.settle()


def quantise(v, own, src, inverse, shifted, out, done):
    own.step(v.tensor_scalar(shifted, src, inverse, ROUND, ALU.mult, ALU.add))
    own.settle()
    v.tensor_scalar(out, shifted, -ROUND, None, ALU.add).then_inc(done, 1)


def latent_attention_and_ffn(nc, ctx, mem, dram):
    s = named(mem, """mla_in ffn_in stats rstd z turned hT
        m1_sum m1 keff_sum keff veff_sum veff d_sum d c_sum c q_sum q k_sum k v_sum v
        s_sum s_ready e p o_sum res1 w_most w_all w1_q w2_q x_most x_all x_q x_scale
        a_sum a a_most a_all a_q a_scale b2_added f_sum res2 v_own p_own""")
    a = mem.fresh()
    w = a.take(2048)
    dq = w[:, 0:256].rearrange("p (f n) -> p f n", f=DT)
    dq_rows = w[:, 256:512]
    uq = w[:, 512:768]
    uk = w[:, 768:1024].rearrange("p (f n) -> p f n", f=DT)
    dkv = w[:, 1024:1280].rearrange("p (f n) -> p f n", f=DT)
    uv = w[:, 1280:1536].rearrange("p (f n) -> p f n", f=DT)
    wo = w[:, 1536:2048].rearrange("p (f n) -> p f n", f=DT)
    m1, keff, veff = a.take(DT, D), a.take(D), a.take(D)
    stats, mv, rstd = a.take(GROUPS, TILES, 6), a.take(GROUPS, TILES, 2), a.take(GROUPS, TILES)
    z, hT = a.take(GROUPS, TILES, D), a.take(GROUPS, DT, GROUP)
    dT, cT = a.take(GROUPS, GROUP), a.take(GROUPS, GROUP)
    qT = a.take(GROUPS, DT, GROUP)
    kT = a.take(GROUPS, 2, DT, GROUP)
    val = a.take(GROUPS, TILES, D)
    sc, pT = a.take(GROUPS, 4, 512), a.take(GROUPS, 4, 512)
    small = a.take(GROUPS, 2, 64)
    w1, w2 = a.take(DT, FFN), a.take(FFN // P, D)
    w1q, w2q = a.take(DT, FFN, dtype=BF16), a.take(FFN // P, D, dtype=BF16)
    b1, b1s, b2 = a.take(FFN // P), a.take(FFN // P), a.take(D)
    most, alls, scale, inverse = a.take(4), a.take(4), a.take(4), a.take(4)
    parts = a.take(4)
    prod = a.take(2)
    xq = a.take(GROUPS, DT, GROUP, dtype=BF16)
    shifted = a.take(2048)
    hidden = a.take(GROUPS, FFN // P, GROUP)
    hq = a.take(GROUPS, FFN // P, GROUP, dtype=BF16)
    ps, res, h = mem.ps, mem.res, mem.h
    SCALE = MLA_HS ** -0.5
    M = FFN // P

    def flat(ap):
        return ap.rearrange("p a b -> p (a b)")

    def tiles_of(g):
        return res[:, TILES * g:TILES * (g + 1), :]

    def two_tiles(g, b):
        return ps[:, 4 * g + b, :].rearrange("p (t d) -> p t d", t=2)

    with nc.Block() as block:
        @block.sync
        def _(sp):
            sp.dma_start(w, dram["mla"]).then_inc(s["mla_in"], 16)
            sp.dma_start(w1, dram["ffn_w1"]).then_inc(s["ffn_in"], 16)
            sp.dma_start(w2, dram["ffn_w2"]).then_inc(s["ffn_in"], 16)
            sp.dma_start(b1, dram["ffn_b1"]).then_inc(s["ffn_in"], 16)
            sp.dma_start(b2, dram["ffn_b2"]).then_inc(s["ffn_in"], 16)

        @block.gpsimd
        def _(pool):
            own = Steps(pool, s["p_own"])
            for g in range(GROUPS):
                pool.wait_ge(s["stats"], g + 1)
                norm_rstd(pool, own, mv[:, g, :, 1], rstd[:, g, :], mem.minus_half, EPS, s["rstd"], g + 1)
            for n in range(2):
                pool.wait_ge(s["w_most"], n + 1)
                pool.partition_all_reduce(alls[:, n:n + 1], most[:, n:n + 1], P, RMAX).then_inc(s["w_all"], 1)
                pool.wait_ge(s["w_all"], n + 1)
            for g in range(GROUPS):
                n = GROUPS + g + 1
                pool.wait_ge(s["stats"], n)
                norm_rstd(pool, own, mv[:, g, :, 1], rstd[:, g, :], mem.minus_half, EPS, s["rstd"], n)
            pool.wait_ge(s["x_most"], 1)
            pool.partition_all_reduce(alls[:, 2:3], most[:, 2:3], P, RMAX).then_inc(s["x_all"], 1)
            pool.wait_ge(s["x_all"], 1)
            pool.wait_ge(s["a_most"], 1)
            pool.partition_all_reduce(alls[:, 3:4], most[:, 3:4], P, RMAX).then_inc(s["a_all"], 1)
            pool.wait_ge(s["a_all"], 1)
            pool.wait_ge(s["a_scale"], 1)
            own.step(pool.tensor_scalar(b2, b2, prod[:, 1:2], 1.0, ALU.mult, ALU.mult))
            for g in range(GROUPS):
                own.settle()
                if g:
                    pool.wait_ge(s["b2_added"], g)
                pool.tensor_tensor(tiles_of(g), tiles_of(g), spread(b2, 1, TILES), ALU.add).then_inc(s["b2_added"], 1)
            pool.wait_ge(s["b2_added"], GROUPS)
            for g in range(GROUPS):
                n = 2 * GROUPS + g + 1
                pool.wait_ge(s["stats"], n)
                norm_rstd(pool, own, mv[:, g, :, 1], rstd[:, g, :], mem.minus_half, EPS, s["rstd"], n)

        @block.vector
        def _(v):
            own = Steps(v, s["v_own"])

            def statistics():
                for g in range(GROUPS):
                    norm_stats(v, own, tiles_of(g), stats[:, g], mv[:, g], s["stats"])

            def apply(j, out):
                for g in range(GROUPS):
                    v.wait_ge(s["rstd"], GROUPS * j + g + 1)
                    norm_apply(v, tiles_of(g), mv[:, g], rstd[:, g], out(g), s["z"])

            statistics()
            v.wait_ge(s["ffn_in"], 64)
            for n, x in enumerate((w1, w2)):
                v.tensor_reduce(most[:, n:n + 1], flat(x), AX, ALU.max,
                                apply_absolute_value=True).then_inc(s["w_most"], 1)
            apply(0, lambda g: z[:, g])
            for n, (x, q, done) in enumerate(((w1, w1q, s["w1_q"]), (w2, w2q, s["w2_q"]))):
                v.wait_ge(s["w_all"], n + 1)
                quantiser(v, own, alls[:, n:n + 1], scale[:, n:n + 1], inverse[:, n:n + 1])
                if n:
                    v.wait_ge(s["w1_q"], 1)
                quantise(v, own, flat(x), inverse[:, n:n + 1], shifted, flat(q), done)
            for g in range(GROUPS):
                v.wait_ge(s["c_sum"], g + 1)
                v.tensor_copy(cT[:, g, :], ps[:, 4 * g + 3, :]).then_inc(s["c"], 1)
            for g in range(GROUPS):
                v.wait_ge(s["k_sum"], DT * (g + 1))
                for e in range(2):
                    v.tensor_scalar(kT[:, g, e, 1, :], ps[:, 4 * g + 3, :], mem.parity[:, e:e + 1], None,
                                    ALU.mult).then_inc(s["k"], 1)
            for g in range(GROUPS):
                for b in range(2):
                    v.wait_ge(s["v_sum"], 2 * g + b + 1)
                    v.tensor_copy(val[:, g, 2 * b:2 * b + 2, :], two_tiles(g, b)).then_inc(s["v"], 1)
            for g in range(GROUPS):
                v.wait_ge(s["s_sum"], g + 1)
                rows32 = sc[:, g].rearrange("p r (j k) -> p (r j) k", k=32)
                own.step(v.tensor_tensor(
                    sc[:, g].rearrange("p r (j k) -> p r j k", k=32),
                    ps[:, 4 * g:4 * g + 4, :].rearrange("p r (j k) -> p r j k", k=32),
                    spread(spread(mem.causal, 1, 16), 1, 4), ALU.add))
                own.settle()
                own.step(v.tensor_reduce(small[:, g, 0, :], rows32, AX, ALU.max))
                own.settle()
                v.tensor_tensor(rows32, rows32, spread(small[:, g, 0, :], 2, 32),
                                ALU.subtract).then_inc(s["s_ready"], 1)
            for g in range(GROUPS):
                v.wait_ge(s["e"], g + 1)
                rows32 = sc[:, g].rearrange("p r (j k) -> p (r j) k", k=32)
                own.step(v.tensor_reduce(small[:, g, 1, :], rows32, AX, ALU.add))
                own.settle()
                own.step(v.reciprocal(small[:, g, 0, :], small[:, g, 1, :]))
                own.settle()
                own.step(v.tensor_tensor(rows32, rows32, spread(small[:, g, 0, :], 2, 32), ALU.mult))
                own.settle()
                v.transpose(flat(pT[:, g]), flat(sc[:, g])).then_inc(s["p"], 1)
            for pair in range(2):
                for g in range(GROUPS):
                    v.wait_ge(s["o_sum"], GROUPS * pair + g + 1)
                    for i in range(4):
                        rows_i = slice(32 * i, 32 * i + 32)
                        t = TILES * g + 2 * pair
                        two = res[rows_i, t:t + 2, :]
                        v.tensor_tensor(two, two, ps[rows_i, 4 * g + i, :].rearrange("p (t d) -> p t d", t=2),
                                        ALU.add).then_inc(s["res1"], 1)
            v.wait_ge(s["res1"], 4 * GROUPS * 2)
            statistics()
            apply(1, lambda g: z[:, g])
            v.wait_ge(s["z"], 2 * GROUPS * TILES)
            absolute_max(v, own, parts[:, 0:1], z.rearrange("p g t d -> p (g t d)"))
            own.settle()
            v.tensor_copy(most[:, 2:3], parts[:, 0:1]).then_inc(s["x_most"], 1)
            v.wait_ge(s["x_all"], 1)
            quantiser(v, own, alls[:, 2:3], scale[:, 2:3], inverse[:, 2:3])
            own.step(v.tensor_tensor(prod[:, 0:1], scale[:, 0:1], scale[:, 2:3], ALU.mult))
            own.settle()
            v.tensor_scalar(b1s, b1, prod[:, 0:1], None, ALU.mult).then_inc(s["x_scale"], 1)
            for g in range(GROUPS):
                v.wait_ge(s["hT"], DT * GROUPS + DT * (g + 1))
                quantise(v, own, flat(hT[:, g]), inverse[:, 2:3], flat(hT[:, g]), flat(xq[:, g]), s["x_q"])
            for g in range(GROUPS):
                for b in range(2):
                    v.wait_ge(s["a"], M * g + 4 * b + 4)
                    n = 2 * g + b
                    absolute_max(v, own, parts[:, n:n + 1], flat(hidden[:, g, 4 * b:4 * b + 4, :]))
            own.settle()
            v.tensor_reduce(most[:, 3:4], parts, AX, ALU.max).then_inc(s["a_most"], 1)
            v.wait_ge(s["a_all"], 1)
            quantiser(v, own, alls[:, 3:4], scale[:, 3:4], inverse[:, 3:4])
            v.tensor_tensor(prod[:, 1:2], scale[:, 1:2], scale[:, 3:4], ALU.mult).then_inc(s["a_scale"], 1)
            for g in range(GROUPS):
                quantise(v, own, flat(hidden[:, g]), inverse[:, 3:4], flat(hidden[:, g]), flat(hq[:, g]), s["a_q"])
            v.wait_ge(s["a_scale"], 1)
            for g in range(GROUPS):
                v.wait_ge(s["b2_added"], g + 1)
                for b in range(2):
                    v.wait_ge(s["f_sum"], 2 * g + b + 1)
                    t = TILES * g + 2 * b
                    two = res[:, t:t + 2, :]
                    v.scalar_tensor_tensor(two, two_tiles(g, b), prod[:, 1:2], two, ALU.mult,
                                           ALU.add).then_inc(s["res2"], 1)
            v.wait_ge(s["res2"], 2 * GROUPS)
            statistics()
            apply(2, lambda g: h[:, TILES * g:TILES * (g + 1), :])

        @block.scalar
        def _(act):
            act.wait_ge(s["m1_sum"], 1)
            act.activation(flat(m1), ps[:, 6, :], ACT.Copy).then_inc(s["m1"], 1)
            act.wait_ge(s["veff_sum"], 1)
            act.activation(veff, ps[:, 7, 0:D], ACT.Copy).then_inc(s["veff"], 1)
            act.wait_ge(s["keff_sum"], 1)
            act.activation(keff, ps[:, 6, 0:D], ACT.Copy).then_inc(s["keff"], 1)

            def turned(j):
                for g in range(GROUPS):
                    for f in range(DT):
                        act.wait_ge(s["turned"], GROUPS * DT * j + DT * g + f + 1)
                        act.activation(hT[:, g, f, :], ps[:, 4 * g + f, :], ACT.Copy).then_inc(s["hT"], 1)

            turned(0)
            for g in range(GROUPS):
                act.wait_ge(s["d_sum"], g + 1)
                act.activation(dT[:, g, :], ps[:, 4 * g + 2, :], ACT.Copy).then_inc(s["d"], 1)
            for g in range(GROUPS):
                for m in range(DT):
                    act.wait_ge(s["q_sum"], DT * g + m + 1)
                    act.activation(qT[:, g, m, :], ps[:, 4 * g + m, :], ACT.Copy).then_inc(s["q"], 1)
            for g in range(GROUPS):
                act.wait_ge(s["k_sum"], DT * g + 1)
                for e in range(2):
                    act.activation(kT[:, g, e, 0, :], ps[:, 4 * g + 2, :], ACT.Identity, bias=0.0,
                                   scale=mem.parity[:, e:e + 1]).then_inc(s["k"], 1)
            for g in range(GROUPS):
                act.wait_ge(s["s_ready"], g + 1)
                act.activation(flat(sc[:, g]), flat(sc[:, g]), ACT.Exp, scale=SCALE).then_inc(s["e"], 1)
            turned(1)
            act.wait_ge(s["x_scale"], 1)
            for g in range(GROUPS):
                for m in range(M):
                    act.wait_ge(s["a_sum"], M * g + m + 1)
                    act.activation(hidden[:, g, m, :], ps[:, 4 * g + m % 4, :], ACT.Gelu,
                                   bias=b1s[:, m:m + 1], scale=prod[:, 0:1]).then_inc(s["a"], 1)

        @block.tensor
        def _(pe):
            pe.wait_ge(s["mla_in"], 16)
            for f in range(DT):
                ins = pe.matmul(ps[:, 6, f * D:(f + 1) * D], uq[:, f * P:(f + 1) * P], dq_rows,
                                start=True, stop=True)
            ins.then_inc(s["m1_sum"], 1)
            for f in range(DT):
                ins = pe.matmul(ps[:, 7, 0:D], uv[:, f, :], wo[:, f, :], start=(f == 0), stop=(f == DT - 1))
            ins.then_inc(s["veff_sum"], 1)
            pe.wait_ge(s["m1"], 1)
            for f in range(DT):
                ins = pe.matmul(ps[:, 6, 0:D], uk[:, f, :], m1[:, f, :], start=(f == 0), stop=(f == DT - 1))
            ins.then_inc(s["keff_sum"], 1)

            def turn(j):
                for g in range(GROUPS):
                    pe.wait_ge(s["z"], GROUPS * TILES * j + TILES * (g + 1))
                    turn_tiles(pe, z[:, g], mem.ident, ps[:, 4 * g:4 * g + 2, :], s["turned"])

            turn(0)
            pe.wait_ge(s["veff"], 1)
            pe.wait_ge(s["keff"], 1)
            for g in range(GROUPS):
                pe.wait_ge(s["hT"], DT * (g + 1))
                for w_in, bank, done in ((dq, 2, s["d_sum"]), (dkv, 3, s["c_sum"])):
                    for k in range(DT):
                        ins = pe.matmul(ps[:, 4 * g + bank, :], w_in[:, k, :], hT[:, g, k, :],
                                        start=(k == 0), stop=(k == DT - 1))
                    ins.then_inc(done, 1)
            for g in range(GROUPS):
                pe.wait_ge(s["d"], g + 1)
                for m in range(DT):
                    pe.matmul(ps[:, 4 * g + m, :], uq[:, m * P:(m + 1) * P], dT[:, g, :],
                              start=True, stop=True).then_inc(s["q_sum"], 1)
                pe.wait_ge(s["c"], g + 1)
                for m in range(DT):
                    pe.matmul(ps[:, 4 * g + 2 + m, :], keff[:, m * P:(m + 1) * P], cT[:, g, :],
                              start=True, stop=True).then_inc(s["k_sum"], 1)
            for g in range(GROUPS):
                pe.wait_ge(s["q"], DT * (g + 1))
                for t in range(TILES):
                    ins = pe.matmul(ps[:, 4 * g + t // 2, (t % 2) * D:(t % 2 + 1) * D],
                                    cT[:, g, t * P:(t + 1) * P], veff, start=True, stop=True)
                    if t % 2:
                        ins.then_inc(s["v_sum"], 1)
            pe.wait_ge(s["k"], 4 * GROUPS)
            for g in range(GROUPS):
                pe.wait_ge(s["v"], 2 * (g + 1))
                for t in range(TILES):
                    for f in range(DT):
                        for e in range(2):
                            col = t * P + (2 * f + e) * 32
                            for i in range(4):
                                for r in range(4):
                                    at = slice(t * P + 32 * i, t * P + 32 * i + 32)
                                    ins = pe.matmul(ps[32 * i:32 * i + 32, 4 * g + r, col:col + 32],
                                                    qT[32 * r:32 * r + 32, g, f, at],
                                                    kT[32 * r:32 * r + 32, g, e, f, at],
                                                    start=True, stop=True)
                ins.then_inc(s["s_sum"], 1)
            for pair in range(2):
                for g in range(GROUPS):
                    pe.wait_ge(s["p"], g + 1)
                    if pair:
                        pe.wait_ge(s["res1"], 4 * (g + 1))
                    for t in (2 * pair, 2 * pair + 1):
                        for f in range(DT):
                            for e in range(2):
                                col = t * P + (2 * f + e) * 32
                                for r in range(4):
                                    head = 8 * f + 2 * r + e
                                    for i in range(4):
                                        rows_i = slice(32 * i, 32 * i + 32)
                                        out_at = (t % 2) * D + head * MLA_HS
                                        ins = pe.matmul(ps[rows_i, 4 * g + i, out_at:out_at + MLA_HS],
                                                        pT[rows_i, g, r, col:col + 32],
                                                        val[rows_i, g, t, head * MLA_HS:(head + 1) * MLA_HS],
                                                        start=True, stop=True)
                    ins.then_inc(s["o_sum"], 1)
            turn(1)
            pe.wait_ge(s["w1_q"], 1)
            for g in range(GROUPS):
                pe.wait_ge(s["x_q"], g + 1)
                for m in range(M):
                    if m >= 4:
                        pe.wait_ge(s["a"], M * g + m - 3)
                    for k in range(DT):
                        ins = pe.matmul(ps[:, 4 * g + m % 4, :], w1q[:, k, m * P:(m + 1) * P], xq[:, g, k, :],
                                        start=(k == 0), stop=(k == DT - 1))
                    ins.then_inc(s["a_sum"], 1)
            pe.wait_ge(s["w2_q"], 1)
            for g in range(GROUPS):
                pe.wait_ge(s["a_q"], g + 1)
                for t in range(TILES):
                    for k in range(M):
                        ins = pe.matmul(ps[:, 4 * g + t // 2, (t % 2) * D:(t % 2 + 1) * D],
                                        hq[:, g, k, t * P:(t + 1) * P], w2q[:, k, :],
                                        start=(k == 0), stop=(k == M - 1))
                    if t % 2:
                        ins.then_inc(s["f_sum"], 1)
    end_block(nc, mem)


def mamba_layers(nc, ctx, mem, dram):
    s = named(mem, """cols_in in_in x_in dt_in out_in rows_in sel_in zeroed diag
        a_exp a_neg squares rstd z turned hT xs_sum xs gate_sum gate conv_sum u x_sum x bc3
        dt_sum dt_free soft delta du bc_sum bc decay scanned weighted reduced y_free y
        o_sum bo_added h_out v_own p_own""")
    KT = INNER // P
    CH, NC = 4, STATE // 4
    PAD = (CONV - 1) // 2
    SEQ = GROUP // T
    a = mem.fresh()
    w_in = a.take(DT, 2 * INNER)
    w_conv = a.take(KT * CONV, P)
    w_x = a.take(KT, RANK + 2 * STATE)
    w_dt = a.take(INNER, rows=RANK)
    w_out = a.take(KT, D)
    cols = a.take(48)
    b_in, b_conv, b_dt, skip, w_norm, taps = (cols[:, 0:8], cols[:, 8:12], cols[:, 12:16], cols[:, 16:20],
                                              cols[:, 20:22], cols[:, 24:44])
    decay_log, decay_exp, decay_rate = a.take(KT, STATE), a.take(KT, STATE), a.take(KT, STATE)
    b_out = a.take(D)
    squares, rstd = a.take(GROUPS, TILES), a.take(GROUPS, TILES)
    select = a.take(2 * STATE, P, dtype=BF16, rows=96)
    zh = a.take(4, GROUP)
    z = zh[:, 0:2, :].rearrange("p a (t d) -> p (a t) d", d=D)
    hT = zh[:, 2:4, :]
    soft = zh
    padded = a.take(KT, SEQ, T + 2 * PAD)
    u, gate = a.take(GROUPS, KT, GROUP), a.take(GROUPS, KT, GROUP)
    delta, du = a.take(GROUPS, KT, GROUP), a.take(GROUPS, KT, GROUP)
    xd = a.take(GROUP, rows=96)
    bc3 = a.take(GROUPS, GROUP, dtype=BF16, rows=96)
    rest = a.take(GROUP, rows=96)
    middle = a.take(GROUP, dtype=BF16, rows=96)
    bc = a.take(2, 2 * CH, GROUP)
    decay, work = a.take(2, CH, GROUP), a.take(2, CH, GROUP)
    ps, h = mem.ps, mem.h
    CHUNKS = NC * KT

    def flat(ap):
        return ap.rearrange("p a b -> p (a b)")

    def steps_of(ap):
        return ap.rearrange("p (b t) -> p b t", t=T)

    def tiles_of(g):
        return h[:, TILES * g:TILES * (g + 1), :]

    PREPARE = ["norm", "xs", "gate", "conv", "xproj", "dt"]
    BEFORE = {1: [("norm", 1)], 2: [("rows", 1), ("xs", 1)], 3: [("gate", 1)], 5: [("conv", 1)], 6: [("rows", 2)],
              7: [("xproj", 1)], 8: [("dt", 1)], 10: [("rows", 3)], 14: [("rows", 4)], 17: [("y", 0)],
              18: [("rows", 5)], 19: [("out", 0)], 22: [("rows", 6)], 26: [("rows", 7)]}
    ORDER = [(p, 0) for p in PREPARE] + [("rows", 0)]
    for c in range(GROUPS * CHUNKS):
        ORDER += BEFORE.get(c, []) + [("chunk", c)]
    ORDER += [("y", 1), ("out", 1)]

    with nc.Fori(0, LAYERS) as layer:
        with nc.Block() as block:
            @block.sync
            def _(sp):
                sp.dma_start(cols, dram["mam_cols"][layer, :, :]).then_inc(s["cols_in"], 16)
                sp.dma_start(decay_log, dram["mam_alog"][layer, :, :, :]).then_inc(s["cols_in"], 16)
                sp.dma_start(w_in, dram["mam_in"][layer, :, :, :]).then_inc(s["in_in"], 16)
                sp.dma_start(w_x, dram["mam_x"][layer, :, :, :]).then_inc(s["x_in"], 16)
                sp.dma_start(w_dt, dram["mam_dt"][layer, :, :]).then_inc(s["dt_in"], 16)
                sp.dma_start(select, dram["select"]).then_inc(s["sel_in"], 16)
                sp.dma_start(b_out, dram["mam_bo"][layer, :, :]).then_inc(s["rows_in"], 16)
                sp.dma_start(w_out, dram["mam_out"][layer, :, :, :]).then_inc(s["out_in"], 16)

            @block.gpsimd
            def _(pool):
                own = Steps(pool, s["p_own"])

                def scale_rows(g):
                    pool.wait_ge(s["squares"], TILES * (g + 1))
                    own.step(pool.tensor_scalar(rstd[:, g], squares[:, g], 1.0 / D, EPS, ALU.mult, ALU.add))
                    own.settle()
                    pool.tensor_tensor(rstd[:, g], rstd[:, g], mem.minus_half, ALU.pow).then_inc(s["rstd"], 1)
                    pool.wait_ge(s["rstd"], g + 1)

                scale_rows(0)
                own.step(pool.memset(padded, 0.0))
                own.settle()
                pool.wait_ge(s["cols_in"], 32)
                pool.tensor_tensor(w_conv, spread(mem.ident, 1, KT * CONV), spread(taps, 2, P),
                                   ALU.mult).then_inc(s["diag"], 1)
                pool.wait_ge(s["diag"], 1)
                own.step(pool.memset(decay, 0.0))
                own.settle()
                for g in range(GROUPS):
                    if g:
                        scale_rows(g)
                    pool.wait_ge(s["rows_in"], 16)
                    pool.wait_ge(s["z"], TILES * (g + 1))
                    pool.tensor_tensor(tiles_of(g), tiles_of(g), spread(b_out, 1, TILES),
                                       ALU.add).then_inc(s["bo_added"], 1)
                    pool.wait_ge(s["bo_added"], g + 1)

            @block.scalar
            def _(act):
                act.wait_ge(s["cols_in"], 32)
                for what, n in ORDER:
                    g = n
                    if what == "norm":
                        if g:
                            act.wait_ge(s["delta"], g)
                        for t in range(TILES):
                            act.activation(z[:, t, :], h[:, TILES * g + t, :], ACT.Square,
                                           accum_out=squares[:, g, t:t + 1]).then_inc(s["squares"], 1)
                        for f in range(DT):
                            act.wait_ge(s["turned"], DT * g + f + 1)
                            act.activation(hT[:, f, :], ps[:, 4 + f, :], ACT.Identity, bias=0.0,
                                           scale=w_norm[:, f:f + 1]).then_inc(s["hT"], 1)
                    if what == "xs":
                        act.wait_ge(s["p_own"], 2)
                        for m in range(KT):
                            act.wait_ge(s["xs_sum"], KT * g + m + 1)
                            act.activation(padded[:, m, :, PAD:PAD + T], steps_of(ps[:, 4 + m, :]), ACT.Identity,
                                           bias=b_in[:, m:m + 1]).then_inc(s["xs"], 1)
                    if what == "gate":
                        for m in range(KT):
                            act.wait_ge(s["gate_sum"], KT * g + m + 1)
                            act.activation(gate[:, g, m, :], ps[:, 4 + m, :], ACT.Silu,
                                           bias=b_in[:, KT + m:KT + m + 1]).then_inc(s["gate"], 1)
                    if what == "conv":
                        for m in range(KT):
                            act.wait_ge(s["conv_sum"], KT * g + m + 1)
                            act.activation(u[:, g, m, :], ps[:, 4 + m, :], ACT.Silu,
                                           bias=b_conv[:, m:m + 1]).then_inc(s["u"], 1)
                    if what == "dt":
                        if g == 0:
                            act.activation(decay_exp, decay_log, ACT.Exp).then_inc(s["a_exp"], 1)
                        for m in range(KT):
                            act.wait_ge(s["dt_sum"], KT * g + m + 1)
                            act.activation(soft[:, m, :], ps[:, 4 + m, :], ACT.Abs, bias=b_dt[:, m:m + 1])\
                               .then_inc(s["soft"], 1)
                            act.activation(delta[:, g, m, :], ps[:, 4 + m, :], ACT.Relu,
                                           bias=b_dt[:, m:m + 1]).then_inc(s["dt_free"], 1)
                        act.wait_ge(s["soft"], (KT + 2) * g + KT)
                        act.activation(flat(soft), flat(soft), ACT.Exp, scale=-1.0).then_inc(s["soft"], 1)
                        act.wait_ge(s["soft"], (KT + 2) * g + KT + 1)
                        act.activation(flat(soft), flat(soft), ACT.Ln, bias=1.0).then_inc(s["soft"], 1)
                    if what == "rows":
                        if n >= 2:
                            act.wait_ge(s["weighted"], KT * (n - 1))
                        for j in range(2 * CH):
                            act.wait_ge(s["bc_sum"], 2 * CH * n + j + 1)
                            act.activation(bc[:, n % 2, j, :], ps[:, 4 + j % 4, :], ACT.Copy).then_inc(s["bc"], 1)
                    if what == "chunk":
                        g, part, m = n // CHUNKS, n % CHUNKS // KT, n % KT
                        act.wait_ge(s["delta"], g + 1)
                        if n == 0:
                            act.wait_ge(s["a_neg"], 1)
                            act.wait_ge(s["p_own"], 3)
                        if n >= 2:
                            act.wait_ge(s["scanned"], n - 1)
                        for j in range(CH):
                            state = CH * part + j
                            act.activation(steps_of(decay[:, n % 2, j, :])[:, :, 1:T],
                                           steps_of(delta[:, g, m, :])[:, :, 1:T], ACT.Exp,
                                           scale=decay_rate[:, m, state:state + 1]).then_inc(s["decay"], 1)

            @block.vector
            def _(v):
                own = Steps(v, s["v_own"])
                v.wait_ge(s["cols_in"], 32)
                for what, n in ORDER:
                    g = n
                    if what == "norm":
                        v.wait_ge(s["rstd"], g + 1)
                        for t in range(TILES):
                            v.tensor_scalar(z[:, t, :], h[:, TILES * g + t, :], rstd[:, g, t:t + 1], None,
                                            ALU.mult).then_inc(s["z"], 1)
                    if what == "xproj":
                        lo, mid, hi = slice(0, 32), slice(32, 64), slice(64, 96)
                        v.wait_ge(s["x_sum"], g + 1)
                        v.tensor_copy(xd, ps[0:96, 4, :]).then_inc(s["x"], 1)
                        v.wait_ge(s["x"], g + 1)
                        own.step(v.tensor_copy(bc3[hi, g, :], xd[hi, :]))
                        own.settle()
                        own.step(v.tensor_tensor(rest[hi, :], xd[hi, :], bc3[hi, g, :], ALU.subtract))
                        own.settle()
                        own.step(v.tensor_copy(middle[hi, :], rest[hi, :]))
                        own.settle()
                        own.step(v.tensor_tensor(rest[hi, :], rest[hi, :], middle[hi, :], ALU.subtract))
                        own.step(v.tensor_copy(bc3[mid, g, :], middle[hi, :]))
                        own.settle()
                        v.tensor_copy(bc3[lo, g, :], rest[hi, :]).then_inc(s["bc3"], 1)
                    if what == "dt":
                        if g == 0:
                            v.wait_ge(s["a_exp"], 1)
                            v.tensor_scalar(flat(decay_rate), flat(decay_exp), -1.0, None, ALU.mult).then_inc(s["a_neg"], 1)
                        v.wait_ge(s["soft"], (KT + 2) * (g + 1))
                        v.wait_ge(s["dt_free"], KT * (g + 1))
                        v.tensor_tensor(flat(delta[:, g]), flat(delta[:, g]), flat(soft), ALU.add).then_inc(s["delta"], 1)
                        v.wait_ge(s["delta"], g + 1)
                        v.wait_ge(s["u"], KT * (g + 1))
                        v.tensor_tensor(flat(du[:, g]), flat(delta[:, g]), flat(u[:, g]), ALU.mult).then_inc(s["du"], 1)
                        v.wait_ge(s["du"], g + 1)
                    if what == "chunk":
                        g, part, m = n // CHUNKS, n % CHUNKS // KT, n % KT
                        rows = bc[:, (n // KT) % 2]
                        w = work[:, n % 2]
                        v.wait_ge(s["bc"], 2 * CH * (n // KT + 1))
                        if n >= 2:
                            v.wait_ge(s["reduced"], n - 1)
                        own.step(v.tensor_tensor(w, spread(du[:, g, m, :], 1, CH), rows[:, 0:CH, :], ALU.mult))
                        v.wait_ge(s["decay"], CH * (n + 1))
                        own.settle()
                        v.tensor_tensor_scan(flat(w), flat(decay[:, n % 2]), flat(w), 0.0, ALU.mult,
                                             ALU.add).then_inc(s["scanned"], 1)
                        v.wait_ge(s["scanned"], n + 1)
                        v.tensor_tensor(w, w, rows[:, CH:2 * CH, :], ALU.mult).then_inc(s["weighted"], 1)
                    if what == "y":
                        v.wait_ge(s["reduced"], CHUNKS * (g + 1))
                        v.wait_ge(s["gate"], KT * (g + 1))
                        for m in range(KT):
                            v.scalar_tensor_tensor(du[:, g, m, :], u[:, g, m, :], skip[:, m:m + 1], ps[:, m, :],
                                                   ALU.mult, ALU.add).then_inc(s["y_free"], 1)
                        for m in range(KT):
                            v.wait_ge(s["y_free"], KT * g + m + 1)
                            v.tensor_tensor(du[:, g, m, :], du[:, g, m, :], gate[:, g, m, :],
                                            ALU.mult).then_inc(s["y"], 1)
                    if what == "out":
                        v.wait_ge(s["bo_added"], g + 1)
                        for b in range(2):
                            v.wait_ge(s["o_sum"], 2 * g + b + 1)
                            t = TILES * g + 2 * b
                            v.tensor_tensor(h[:, t:t + 2, :], h[:, t:t + 2, :],
                                            ps[:, 4 + b, :].rearrange("p (t d) -> p t d", t=2),
                                            ALU.add).then_inc(s["h_out"], 1)

            @block.tensor
            def _(pe):
                read = None
                for what, n in ORDER:
                    g = n
                    if what not in ("chunk", "y") and read:
                        pe.wait_ge(*read)
                    if what == "norm":
                        pe.wait_ge(s["z"], TILES * (g + 1))
                        turn_tiles(pe, z, mem.ident, ps[:, 4:6, :], s["turned"])
                        read = (s["hT"], DT * (g + 1))
                    if what in ("xs", "gate"):
                        pe.wait_ge(s["in_in"], 16)
                        at = 0 if what == "xs" else INNER
                        for m in range(KT):
                            for k in range(DT):
                                ins = pe.matmul(ps[:, 4 + m, :], w_in[:, k, at + m * P:at + (m + 1) * P],
                                                hT[:, k, :], start=(k == 0), stop=(k == DT - 1))
                            ins.then_inc(s["xs_sum"] if what == "xs" else s["gate_sum"], 1)
                        read = (s["xs"] if what == "xs" else s["gate"], KT * (g + 1))
                    if what == "conv":
                        pe.wait_ge(s["diag"], 1)
                        for m in range(KT):
                            for k in range(CONV):
                                ins = pe.matmul(ps[:, 4 + m, :], w_conv[:, CONV * m + k, :],
                                                padded[:, m, :, k:k + T], start=(k == 0), stop=(k == CONV - 1))
                            ins.then_inc(s["conv_sum"], 1)
                        read = (s["u"], KT * (g + 1))
                    if what == "xproj":
                        pe.wait_ge(s["x_in"], 16)
                        for k in range(KT):
                            ins = pe.matmul(ps[0:96, 4, :], w_x[:, k, :], u[:, g, k, :],
                                            start=(k == 0), stop=(k == KT - 1))
                        ins.then_inc(s["x_sum"], 1)
                        read = (s["x"], g + 1)
                    if what == "dt":
                        pe.wait_ge(s["dt_in"], 16)
                        for m in range(KT):
                            pe.matmul(ps[:, 4 + m, :], w_dt[:, m * P:(m + 1) * P], xd[0:RANK, :],
                                      start=True, stop=True).then_inc(s["dt_sum"], 1)
                        read = (s["dt_free"], KT * (g + 1))
                    if what == "rows":
                        g, part = n // NC, n % NC
                        pe.wait_ge(s["sel_in"], 16)
                        pe.wait_ge(s["bc3"], g + 1)
                        for j in range(2 * CH):
                            if j >= 4:
                                pe.wait_ge(s["bc"], 2 * CH * n + j - 3)
                            row = (j // CH) * STATE + CH * part + j % CH
                            pe.matmul(ps[:, 4 + j % 4, :], select[:, row, :], bc3[:, g, :],
                                      start=True, stop=True).then_inc(s["bc_sum"], 1)
                        read = (s["bc"], 2 * CH * (n + 1))
                    if what == "chunk":
                        g, part, m = n // CHUNKS, n % CHUNKS // KT, n % KT
                        if g and part == 0:
                            pe.wait_ge(s["y_free"], KT * (g - 1) + m + 1)
                        pe.wait_ge(s["weighted"], n + 1)
                        for j in range(CH):
                            ins = pe.matmul(ps[:, m, :], mem.ident, work[:, n % 2, j, :],
                                            start=(part == 0 and j == 0), stop=(part == NC - 1 and j == CH - 1))
                        ins.then_inc(s["reduced"], 1)
                    if what == "out":
                        pe.wait_ge(s["out_in"], 16)
                        pe.wait_ge(s["y"], KT * (g + 1))
                        for t in range(TILES):
                            for k in range(KT):
                                ins = pe.matmul(ps[:, 4 + t // 2, (t % 2) * D:(t % 2 + 1) * D],
                                                du[:, g, k, t * P:(t + 1) * P], w_out[:, k, :],
                                                start=(k == 0), stop=(k == KT - 1))
                            if t % 2:
                                ins.then_inc(s["o_sum"], 1)
                        read = (s["h_out"], 2 * (g + 1))
        end_block(nc, mem)


def mixture_of_depths(nc, ctx, mem, dram):
    s = named(mem, """small_in w1_in w2_in squares rstd first stats rstd2 z turned hT
        score spread_in score_sum minus expo weight x_added a_sum a f_sum biased done stored v_own p_own""")
    M = FFN // P
    a = mem.fresh()
    w1, w2 = a.take(DT, FFN), a.take(M, D)
    b1 = a.take(M)
    rows = a.take(3, D)
    squares, rstd = a.take(GROUPS, TILES), a.take(GROUPS, TILES)
    stats, mv = a.take(GROUPS, TILES, 6), a.take(GROUPS, TILES, 2)
    first, z, hT = a.take(GROUPS, TILES, D), a.take(GROUPS, TILES, D), a.take(GROUPS, DT, GROUP)
    score = a.take(GROUPS, TILES)
    each, seen, tmp, tied = (a.take(GROUPS, TILES, T) for _ in range(4))
    mine, rank, expo, weight = (a.take(GROUPS, TILES) for _ in range(4))
    hidden = a.take(GROUPS, M, GROUP)
    biased = a.take(GROUPS, TILES, D)
    ps, res, h = mem.ps, mem.res, mem.h

    def tiles_of(x, g):
        return x[:, TILES * g:TILES * (g + 1), :]

    with nc.Block() as block:
        @block.sync
        def _(sp):
            sp.dma_start(rows, dram["mod_rows"]).then_inc(s["small_in"], 16)
            sp.dma_start(b1, dram["mod_b1"]).then_inc(s["small_in"], 16)
            sp.dma_start(w1, dram["mod_w1"]).then_inc(s["w1_in"], 16)
            sp.dma_start(w2, dram["mod_w2"]).then_inc(s["w2_in"], 16)
            for g in range(GROUPS):
                sp.wait_ge(s["done"], TILES * (g + 1))
                out = dram["out"][g * GROUP:(g + 1) * GROUP, :].rearrange("(t p) d -> p t d", p=P)
                sp.dma_start(out, tiles_of(res, g)).then_inc(s["stored"], 16)
            sp.wait_ge(s["stored"], 16 * GROUPS)

        @block.gpsimd
        def _(pool):
            own = Steps(pool, s["p_own"])
            for g in range(GROUPS):
                pool.wait_ge(s["squares"], TILES * (g + 1))
                own.settle()
                own.step(pool.tensor_scalar(rstd[:, g], squares[:, g], 1.0 / D, EPS, ALU.mult, ALU.add))
                own.settle()
                pool.tensor_tensor(rstd[:, g], rstd[:, g], mem.minus_half, ALU.pow).then_inc(s["rstd"], 1)
                pool.wait_ge(s["rstd"], g + 1)
            for g in range(GROUPS):
                pool.wait_ge(s["stats"], g + 1)
                norm_rstd(pool, own, mv[:, g, :, 1], rstd[:, g, :], mem.minus_half, EPS, s["rstd2"], g + 1)
            for g in range(GROUPS):
                pool.wait_ge(s["z"], TILES * (g + 1))
                pool.tensor_tensor(tiles_of(res, g), tiles_of(res, g), z[:, g], ALU.add).then_inc(s["x_added"], 1)
                pool.wait_ge(s["x_added"], g + 1)

        @block.scalar
        def _(act):
            for g in range(GROUPS):
                for t in range(TILES):
                    act.activation(z[:, g, t, :], h[:, TILES * g + t, :], ACT.Square,
                                   accum_out=squares[:, g, t:t + 1]).then_inc(s["squares"], 1)
            for g in range(GROUPS):
                for f in range(DT):
                    act.wait_ge(s["turned"], DT * g + f + 1)
                    act.activation(hT[:, g, f, :], ps[:, 4 * g + f, :], ACT.Copy).then_inc(s["hT"], 1)
            for g in range(GROUPS):
                act.wait_ge(s["minus"], g + 1)
                act.activation(expo[:, g], mine[:, g], ACT.Exp, scale=-1.0).then_inc(s["expo"], 1)
            act.wait_ge(s["small_in"], 32)
            for g in range(GROUPS):
                for m in range(M):
                    act.wait_ge(s["a_sum"], M * g + m + 1)
                    act.activation(hidden[:, g, m, :], ps[:, 4 * g + m % 4, :], ACT.Gelu_apprx_tanh,
                                   bias=b1[:, m:m + 1]).then_inc(s["a"], 1)

        @block.vector
        def _(v):
            own = Steps(v, s["v_own"])
            v.wait_ge(s["small_in"], 32)
            for g in range(GROUPS):
                v.wait_ge(s["rstd"], g + 1)
                for t in range(TILES):
                    v.scalar_tensor_tensor(first[:, g, t, :], h[:, TILES * g + t, :], rstd[:, g, t:t + 1],
                                           rows[:, 0, :], ALU.mult, ALU.mult).then_inc(s["first"], 1)
                v.wait_ge(s["first"], TILES * (g + 1))
                own.step(v.tensor_tensor(tiles_of(res, g), tiles_of(res, g), first[:, g], ALU.add))
                own.settle()
                norm_stats(v, own, tiles_of(res, g), stats[:, g], mv[:, g], s["stats"])
            for g in range(GROUPS):
                v.wait_ge(s["rstd2"], g + 1)
                norm_apply(v, tiles_of(res, g), mv[:, g], rstd[:, g], z[:, g], s["z"])
            for g in range(GROUPS):
                v.wait_ge(s["z"], TILES * (g + 1))
                for t in range(TILES):
                    own.step(v.tensor_tensor_reduce(first[:, g, t, :], z[:, g, t, :], rows[:, 1, :], 1.0, 0.0,
                                                    ALU.mult, ALU.add, score[:, g, t:t + 1]))
                own.settle()
                v.tensor_tensor(each[:, g], spread(mem.slot, 1, TILES), spread(score[:, g], 2, T),
                                ALU.mult).then_inc(s["spread_in"], 1)
            for g in range(GROUPS):
                v.wait_ge(s["score_sum"], g + 1)
                own.step(v.tensor_copy(seen[:, g], ps[:, 4 * g + 2, 0:TILES * T].rearrange("p (t j) -> p t j", j=T)))
                own.settle()
                own.step(v.tensor_tensor(tmp[:, g], seen[:, g], spread(mem.slot, 1, TILES), ALU.mult))
                own.settle()
                v.tensor_reduce(mine[:, g], tmp[:, g], AX, ALU.add).then_inc(s["minus"], 1)
                v.wait_ge(s["minus"], g + 1)
                own.step(v.tensor_tensor(tied[:, g], seen[:, g], spread(mine[:, g], 2, T), ALU.is_equal))
                own.step(v.tensor_tensor(tmp[:, g], seen[:, g], spread(mine[:, g], 2, T), ALU.is_gt))
                own.settle()
                own.step(v.tensor_tensor(tied[:, g], tied[:, g], spread(mem.before, 1, TILES), ALU.mult))
                own.settle()
                own.step(v.tensor_tensor(tmp[:, g], tmp[:, g], tied[:, g], ALU.add))
                own.settle()
                own.step(v.tensor_reduce(rank[:, g], tmp[:, g], AX, ALU.add))
                v.wait_ge(s["expo"], g + 1)
                own.step(v.tensor_scalar(weight[:, g], expo[:, g], 1.0, None, ALU.add))
                own.settle()
                own.step(v.reciprocal(weight[:, g], weight[:, g]))
                own.step(v.tensor_scalar(rank[:, g], rank[:, g], TOP - 0.5, None, ALU.is_lt))
                own.settle()
                v.tensor_tensor(weight[:, g], weight[:, g], rank[:, g], ALU.mult).then_inc(s["weight"], 1)
            for g in range(GROUPS):
                v.wait_ge(s["weight"], g + 1)
                v.wait_ge(s["x_added"], g + 1)
                for b in range(2):
                    v.wait_ge(s["f_sum"], 2 * g + b + 1)
                    v.tensor_tensor(biased[:, g, 2 * b:2 * b + 2, :],
                                    ps[:, 4 * g + b, :].rearrange("p (t d) -> p t d", t=2),
                                    spread(rows[:, 2, :], 1, 2), ALU.add).then_inc(s["biased"], 1)
                    v.wait_ge(s["biased"], 2 * g + b + 1)
                    for t in (2 * b, 2 * b + 1):
                        tile = res[:, TILES * g + t, :]
                        v.scalar_tensor_tensor(tile, biased[:, g, t, :], weight[:, g, t:t + 1], tile,
                                               ALU.mult, ALU.add).then_inc(s["done"], 1)

        @block.tensor
        def _(pe):
            for g in range(GROUPS):
                pe.wait_ge(s["z"], TILES * (g + 1))
                turn_tiles(pe, z[:, g], mem.ident, ps[:, 4 * g:4 * g + 2, :], s["turned"])
            for g in range(GROUPS):
                pe.wait_ge(s["spread_in"], g + 1)
                pe.matmul(ps[:, 4 * g + 2, 0:TILES * T], mem.seq_block,
                          each[:, g].rearrange("p t j -> p (t j)"), start=True, stop=True).then_inc(s["score_sum"], 1)
            pe.wait_ge(s["w1_in"], 16)
            for g in range(GROUPS):
                pe.wait_ge(s["hT"], DT * (g + 1))
                pe.wait_ge(s["minus"], g + 1)
                for m in range(M):
                    if m >= 4:
                        pe.wait_ge(s["a"], M * g + m - 3)
                    for k in range(DT):
                        ins = pe.matmul(ps[:, 4 * g + m % 4, :], w1[:, k, m * P:(m + 1) * P], hT[:, g, k, :],
                                        start=(k == 0), stop=(k == DT - 1))
                    ins.then_inc(s["a_sum"], 1)
            pe.wait_ge(s["w2_in"], 16)
            for g in range(GROUPS):
                pe.wait_ge(s["a"], M * (g + 1))
                for t in range(TILES):
                    for k in range(M):
                        ins = pe.matmul(ps[:, 4 * g + t // 2, (t % 2) * D:(t % 2 + 1) * D],
                                        hidden[:, g, k, t * P:(t + 1) * P], w2[:, k, :],
                                        start=(k == 0), stop=(k == M - 1))
                    if t % 2:
                        ins.then_inc(s["f_sum"], 1)


BLOCKS = [token_mlp, attention_layers, latent_attention_and_ffn, mamba_layers, mixture_of_depths]


def audio_tower(nc, dram):
    with ExitStack() as ctx:
        size = 53200
        tensor = ctx.enter_context(nc.sbuf_tensor("arena", [P, size], F32))
        ps = ctx.enter_context(nc.psum_tensor("banks", [P, 8, 512], F32))
        a = Arena(tensor, size)
        consts = a.take(CONSTS)
        mem = Memory()
        mem.ps, mem.consts = ps, consts
        mem.res = a.take(GROUPS * TILES, D)
        mem.h = a.take(GROUPS * TILES, D)
        at = 0
        parts = []
        for n in CONST_PARTS:
            parts.append(consts[:, at:at + n])
            at += n
        mem.ident, mem.same_seq, mem.causal, mem.parity, mem.minus_half, mem.seq_block, mem.slot, mem.before = parts
        start = a.at

        def fresh():
            b = Arena(tensor, size)
            b.at = start
            return b

        mem.fresh = fresh
        mem.pool = [ctx.enter_context(nc.semaphore(f"count{n}")) for n in range(SEMAPHORES)]
        mem.numbers = range(mem.pool[0].num, mem.pool[-1].num + 1)
        assert len(mem.numbers) == SEMAPHORES
        for block in BLOCKS:
            block(nc, ctx, mem, dram)


CONST_PARTS = [P, 32, 32, 2, TILES, P, T, T]
CONSTS = sum(CONST_PARTS)


def constants(np):
    p = np.arange(P)[:, None]
    k = np.arange(32)[None, :]
    same = (p % 32) // T == k // T
    causal = same & (k % T <= p % T)
    far = np.float32(-1e30)
    step = np.arange(T)[None, :]
    parts = [
        np.eye(P),
        np.where(same, 0, far),
        np.where(causal, 0, far),
        (p // MLA_HS) % 2 == np.arange(2)[None, :],
        np.full((P, TILES), -0.5),
        p // T == np.arange(P)[None, :] // T,
        p % T == step,
        step < p % T,
    ]
    return np.concatenate([np.asarray(x, np.float32) for x in parts], axis=1)


def by_rows(np, w):
    K, M = w.shape
    return w.reshape(K // P, P, M).transpose(1, 0, 2)


def by_partition(np, b):
    return b.reshape(-1, P).T


def every_token(np, b):
    return np.broadcast_to(b, (P, *b.shape))


def laid_out(np, i):
    x = np.pad(i["x"], ((0, 0), (0, T * MLP_IN // 128 - i["x"].shape[1]), (0, 0)))
    x = x.reshape(TOKENS, MLP_IN)
    a = {"consts": constants(np)}
    a["tok_x"] = by_rows(np, x.T)
    a["tok_w1"] = by_rows(np, i["L0_tok_w1"].T)
    a["tok_w2"] = by_rows(np, i["L0_tok_w2"].T)
    a["tok_b1"] = by_partition(np, i["L0_tok_b1"])
    a["tok_b2"] = every_token(np, i["L0_tok_b2"])
    e = {n[7:]: v for n, v in i.items() if n.startswith("L0_tok_")}
    layers = range(LAYERS)
    a["enc_wqkv"] = np.stack([by_rows(np, np.concatenate([e["wq"][l], e["wk"][l], e["wv"][l]]).T) for l in layers])
    a["enc_wo"] = np.stack([by_rows(np, e["wo"][l].T) for l in layers])
    a["enc_ff1"] = np.stack([by_rows(np, e["ffw1"][l].T) for l in layers])
    a["enc_ff2"] = np.stack([np.concatenate([e["ffw2"][l].T, e["ffb2"][l][None]]) for l in layers])
    a["enc_rows"] = np.stack([every_token(np, np.stack([e["bv"][l], e["bo"][l]])) for l in layers])
    a["enc_cols"] = np.stack([np.concatenate(
        [by_partition(np, e[n][l]) for n in ("ln1_s", "ln1_b", "bq", "bk", "ln2_s", "ln2_b")]
        + [np.pad(e["ffb1"][l], (0, P - TOK_FF))[:, None], np.zeros((P, 3), np.float32)], axis=1) for l in layers])
    m = {n[8:]: v for n, v in i.items() if n.startswith("L0_attn_")}

    def side(w):
        return by_rows(np, w).reshape(P, -1)

    a["mla"] = np.concatenate([side(m["W_dq"].T), m["W_dq"], m["W_uq"].T, side(m["W_uk"]), side(m["W_dkv"].T),
                               side(m["W_uv"]), side(m["W_o"].T)], axis=1)
    a["ffn_w1"] = by_rows(np, i["L0_ffn_w1"].T)
    a["ffn_w2"] = by_rows(np, i["L0_ffn_w2"].T)
    a["ffn_b1"] = by_partition(np, i["L0_ffn_b1"])
    a["ffn_b2"] = every_token(np, i["L0_ffn_b2"])
    q = {n[8:]: v for n, v in i.items() if n.startswith("L1_attn_")}
    a["mam_in"] = np.stack([by_rows(np, q["in_proj_w"][l].T) for l in layers])
    a["mam_x"] = np.stack([by_rows(np, q["x_proj_w"][l].T) for l in layers])
    a["mam_dt"] = np.stack([q["dt_proj_w"][l].T for l in layers])
    a["mam_out"] = np.stack([by_rows(np, q["out_proj_w"][l].T) for l in layers])
    a["mam_bo"] = np.stack([every_token(np, q["out_proj_b"][l]) for l in layers])
    a["mam_alog"] = np.stack([by_rows(np, q["A_log"][l]) for l in layers])
    a["mam_cols"] = np.stack([np.concatenate(
        [by_partition(np, q[n][l]) for n in ("in_proj_b", "conv_b", "dt_proj_b", "D", "norm_w")]
        + [np.zeros((P, 2), np.float32), by_rows(np, q["conv_w"][l][:, 0, :]).reshape(P, -1),
           np.zeros((P, 4), np.float32)], axis=1) for l in layers])
    a["select"] = np.broadcast_to((np.arange(96)[:, None] % 32 == np.arange(32)[None, :])[:, :, None],
                                  (96, 32, P)).astype(mybir.dt.np(BF16))
    f = {n[7:]: v for n, v in i.items() if n.startswith("L1_ffn_")}
    a["mod_rows"] = every_token(np, np.stack([q["norm_f_w"], f["w_router"], f["b2"]]))
    a["mod_b1"] = by_partition(np, f["b1"])
    a["mod_w1"] = by_rows(np, f["W1"])
    a["mod_w2"] = by_rows(np, f["W2"])
    return a


def kernel(**inputs):
    import numpy as np
    import concourse.bacc as bacc
    from concourse.bass_utils import run_bass_kernel_spmd

    arrays = {n: np.ascontiguousarray(v) for n, v in laid_out(np, {n: np.asarray(v) for n, v in inputs.items()}).items()}
    nc = bacc.Bacc("TRN2", target_bir_lowering=False, num_devices=1)
    handles = {n: nc.dram_tensor(n, v.shape, mybir.dt.from_np(v.dtype), kind="ExternalInput").ap()
               for n, v in arrays.items()}
    handles["out"] = nc.dram_tensor("out", (TOKENS, D), F32, kind="ExternalOutput").ap()
    audio_tower(nc, handles)
    got = run_bass_kernel_spmd(nc, [arrays], core_ids=[0])
    return got.results[0]["out"].reshape(SEQS, T, D)
```

```python
from contextlib import ExitStack

import concourse.bass as bass
from concourse import mybir

F32 = mybir.dt.float32
BF16 = mybir.dt.bfloat16
ALU = mybir.AluOpType
ACT = mybir.ActivationFunctionType
AX = mybir.AxisListType.X
RMAX = bass.bass_isa.ReduceOp.max

P = 128
SEQS, T, D = 64, 16, 256
TOKENS = SEQS * T
GROUP = 512
GROUPS = TOKENS // GROUP
TILES = GROUP // P
DT = D // P
EPS = 1e-5
TOK_EPS = 1e-12
LAYERS = 2
MLP_IN, MLP_HID = 1024, 512
TOK_HEADS, TOK_DK = 8, 32
TOK_FF = D // 4
MLA_HEADS, MLA_HS, LATENT = 16, 16, 128
FFN = 1024
SEMAPHORES = 64
ROUND = 12582912.0
INNER, STATE, RANK, CONV = 512, 16, 64, 5
KT = INNER // P
CH, NC = 4, STATE // 4
CHUNKS = NC * KT
TOP = 8


class Memory:
    pass


class Steps:

    def __init__(self, eng, sem):
        self.eng, self.sem, self.n = eng, sem, 0

    def step(self, ins):
        ins.then_inc(self.sem, 1)
        self.n += 1
        return self.n

    def settle(self):
        if self.n:
            self.eng.wait_ge(self.sem, self.n)


def named(mem, names):
    names = names.split()
    return dict(zip(names, mem.pool[:len(names)], strict=True))


def end_block(nc, mem):
    nc.gpsimd.sem_clear(mem.numbers)
    nc.all_engine_barrier()


class Arena:

    def __init__(self, tensor, size):
        self.tensor, self.size, self.at = tensor, size, 0

    def take(self, *shape, dtype=F32, rows=P):
        n = 1
        for x in shape:
            n *= x
        words = n if dtype == F32 else (n + 1) // 2
        view = self.tensor[0:rows, self.at:self.at + words]
        self.at += words
        assert self.at <= self.size, (self.at, self.size)
        if dtype != F32:
            view = view.bitcast(dtype)
        if len(shape) > 1:
            names = " ".join(f"d{i}" for i in range(len(shape)))
            sizes = {f"d{i}": x for i, x in enumerate(shape) if i}
            view = view.rearrange(f"p ({names}) -> p {names}", **sizes)
        return view


def spread(ap, axis, n):
    shape = list(ap.shape)
    shape.insert(axis, n)
    return ap.unsqueeze(axis).broadcast_to(shape)


def norm_stats(v, own, src, stats, mv, stats_ready):
    for t in range(TILES):
        own.step(v.bn_stats(stats[:, t, :], src[:, t, :]))
    own.settle()
    for t in range(TILES):
        ins = v.bn_aggr(mv[:, t, :], stats[:, t, :])
        if t < TILES - 1:
            own.step(ins)
    own.settle()
    ins.then_inc(stats_ready, 1)


def norm_rstd(pool, own, var, rstd, minus_half, eps, rstd_ready, n):
    own.settle()
    own.step(pool.tensor_scalar(rstd, var, 1.0, eps, ALU.mult, ALU.add))
    own.settle()
    pool.tensor_tensor(rstd, rstd, minus_half, ALU.pow).then_inc(rstd_ready, 1)
    pool.wait_ge(rstd_ready, n)


def norm_apply(v, src, mv, rstd, z, z_ready):
    for t in range(TILES):
        v.tensor_scalar(z[:, t, :], src[:, t, :], mv[:, t, 0:1], rstd[:, t:t + 1],
                        ALU.subtract, ALU.mult).then_inc(z_ready, 1)


def turn_tiles(pe, z, ident, banks, turned):
    for f in range(DT):
        for t in range(TILES):
            ins = pe.transpose(banks[:, f, t * P:(t + 1) * P], z[:, t, f * P:(f + 1) * P], ident)
        ins.then_inc(turned, 1)


def token_mlp(nc, ctx, mem, dram):
    s = named(mem, " ".join(f"slice{k}" for k in range(8)) +
                      " small hid_sum hid_ready out_sum out_ready")
    slices = [s["slice0"], s["slice1"], s["slice2"], s["slice3"], s["slice4"], s["slice5"], s["slice6"], s["slice7"]]
    KT, HT = MLP_IN // P, MLP_HID // P
    a = mem.fresh()
    w1 = a.take(KT, MLP_HID)
    x = a.take(KT, TOKENS)
    w2 = a.take(HT, D)
    b1 = a.take(HT)
    b2 = a.take(D)
    hid = a.take(GROUPS, HT, GROUP)
    ps, res = mem.ps, mem.res

    with nc.Block() as block:
        @block.sync
        def _(sp):
            for k in range(KT):
                sp.dma_start(w1[:, k, :], dram["tok_w1"][:, k, :]).then_inc(slices[k], 16)
                sp.dma_start(x[:, k, :], dram["tok_x"][:, k, :]).then_inc(slices[k], 16)

        @block.scalar
        def _(act):
            act.dma_start(mem.consts, dram["consts"]).then_inc(s["small"], 16)
            act.dma_start(b1, dram["tok_b1"]).then_inc(s["small"], 16)
            act.dma_start(b2, dram["tok_b2"]).then_inc(s["small"], 16)
            act.dma_start(w2, dram["tok_w2"]).then_inc(s["small"], 16)
            act.wait_ge(s["small"], 64)
            for g in range(GROUPS):
                for m in range(HT):
                    act.wait_ge(s["hid_sum"], g * HT + m + 1)
                    act.activation(hid[:, g, m, :], ps[:, 4 * g + m, :], ACT.Relu,
                                   bias=b1[:, m:m + 1]).then_inc(s["hid_ready"], 1)

        @block.tensor
        def _(pe):
            for k in range(KT):
                pe.wait_ge(slices[k], 32)
                for g in range(GROUPS):
                    for m in range(HT):
                        ins = pe.matmul(ps[:, 4 * g + m, :], w1[:, k, m * P:(m + 1) * P],
                                        x[:, k, g * GROUP:(g + 1) * GROUP],
                                        start=(k == 0), stop=(k == KT - 1))
                        if k == KT - 1:
                            ins.then_inc(s["hid_sum"], 1)
            pe.wait_ge(s["small"], 64)
            for g in range(GROUPS):
                pe.wait_ge(s["hid_ready"], (g + 1) * HT)
                for t in range(TILES):
                    for k in range(HT):
                        ins = pe.matmul(ps[:, 4 * g + t // 2, (t % 2) * D:(t % 2 + 1) * D],
                                        hid[:, g, k, t * P:(t + 1) * P], w2[:, k, :],
                                        start=(k == 0), stop=(k == HT - 1))
                    if t % 2:
                        ins.then_inc(s["out_sum"], 1)

        @block.vector
        def _(v):
            v.wait_ge(s["small"], 64)
            for g in range(GROUPS):
                for h in range(2):
                    v.wait_ge(s["out_sum"], 2 * g + h + 1)
                    t = TILES * g + 2 * h
                    v.tensor_tensor(res[:, t:t + 2, :],
                                    ps[:, 4 * g + h, :].rearrange("p (t d) -> p t d", t=2),
                                    spread(b2, 1, 2), ALU.add).then_inc(s["out_ready"], 1)
    end_block(nc, mem)


def attention_layers(nc, ctx, mem, dram):
    s = named(mem, """cols_in qkv_in wo_in ff_in rows_in
        stats rstd z turned hT q_sum q k_sum k v_sum v s_sum s_ready e p o_sum o
        wo_sum bo_added res1 f_sum f f2_sum res2 v_own p_own""")
    a = mem.fresh()
    wqkv = a.take(DT, 3 * D)
    wo = a.take(DT, D)
    ff1 = a.take(DT, TOK_FF)
    ff2 = a.take(D, rows=TOK_FF + 1)
    cols = a.take(16)
    rows = a.take(2, D)
    stats, mv, rstd = a.take(GROUPS, TILES, 6), a.take(GROUPS, TILES, 2), a.take(GROUPS, TILES)
    z, hT = a.take(GROUPS, TILES, D), a.take(GROUPS, DT, GROUP)
    qT, kT = a.take(GROUPS, DT, GROUP), a.take(GROUPS, DT, GROUP)
    val = a.take(GROUPS, TILES, D)
    sc, pT = a.take(GROUPS, 4, 8 * 32), a.take(GROUPS, 4, 8 * 32)
    small = a.take(GROUPS, 2, 32)
    oT = a.take(GROUPS, DT, GROUP)
    fT = a.take(GROUPS, GROUP, rows=TOK_FF + 1)
    ps, res = mem.ps, mem.res
    SCALE = TOK_DK ** -0.5

    def tiles_of(g):
        return res[:, TILES * g:TILES * (g + 1), :]

    def two_tiles(g, b):
        return ps[:, 4 * g + b, :].rearrange("p (t d) -> p t d", t=2)

    with nc.Fori(0, LAYERS) as layer:
        with nc.Block() as block:
            @block.sync
            def _(sp):
                sp.dma_start(cols, dram["enc_cols"][layer, :, :]).then_inc(s["cols_in"], 16)
                sp.dma_start(wqkv, dram["enc_wqkv"][layer, :, :, :]).then_inc(s["qkv_in"], 16)
                sp.dma_start(rows, dram["enc_rows"][layer, :, :, :]).then_inc(s["rows_in"], 16)
                sp.dma_start(wo, dram["enc_wo"][layer, :, :, :]).then_inc(s["wo_in"], 16)
                sp.dma_start(ff1, dram["enc_ff1"][layer, :, :, :]).then_inc(s["ff_in"], 16)
                sp.dma_start(ff2, dram["enc_ff2"][layer, :, :]).then_inc(s["ff_in"], 16)

            @block.gpsimd
            def _(pool):
                own = Steps(pool, s["p_own"])
                own.step(pool.memset(fT[TOK_FF:TOK_FF + 1, :, :], 1.0))
                for j in range(2):
                    for g in range(GROUPS):
                        pool.wait_ge(s["stats"], 2 * j + g + 1)
                        norm_rstd(pool, own, mv[:, g, :, 1], rstd[:, g, :], mem.minus_half,
                                  TOK_EPS, s["rstd"], 2 * j + g + 1)
                    if j == 0:
                        pool.wait_ge(s["rows_in"], 16)
                        for g in range(GROUPS):
                            pool.wait_ge(s["z"], TILES * (g + 1))
                            pool.tensor_tensor(tiles_of(g), tiles_of(g), spread(rows[:, 1, :], 1, TILES),
                                               ALU.add).then_inc(s["bo_added"], 1)
                            pool.wait_ge(s["bo_added"], g + 1)

            @block.vector
            def _(v):
                own = Steps(v, s["v_own"])

                def norm(j):
                    for g in range(GROUPS):
                        norm_stats(v, own, tiles_of(g), stats[:, g], mv[:, g], s["stats"])
                    for g in range(GROUPS):
                        v.wait_ge(s["rstd"], 2 * j + g + 1)
                        norm_apply(v, tiles_of(g), mv[:, g], rstd[:, g], z[:, g], s["z"])

                norm(0)
                v.wait_ge(s["cols_in"], 16)
                for g in range(GROUPS):
                    for m in range(DT):
                        v.wait_ge(s["k_sum"], DT * g + m + 1)
                        v.tensor_scalar(kT[:, g, m, :], ps[:, 4 * g + m, :], cols[:, 6 + m:7 + m], None,
                                        ALU.add).then_inc(s["k"], 1)
                v.wait_ge(s["rows_in"], 16)
                for g in range(GROUPS):
                    for b in range(2):
                        v.wait_ge(s["v_sum"], 2 * g + b + 1)
                        v.tensor_tensor(val[:, g, 2 * b:2 * b + 2, :], two_tiles(g, 2 + b),
                                        spread(rows[:, 0, :], 1, 2), ALU.add).then_inc(s["v"], 1)
                for g in range(GROUPS):
                    v.wait_ge(s["s_sum"], g + 1)
                    rows32 = sc[:, g].rearrange("p r (j k) -> p (r j) k", k=32)
                    own.step(v.tensor_tensor(
                        sc[:, g].rearrange("p r (j k) -> p r j k", k=32),
                        ps[:, 4 * g:4 * g + 4, 0:256].rearrange("p r (j k) -> p r j k", k=32),
                        spread(spread(mem.same_seq, 1, 8), 1, 4), ALU.add))
                    own.settle()
                    own.step(v.tensor_reduce(small[:, g, 0, :], rows32, AX, ALU.max))
                    own.settle()
                    v.tensor_tensor(rows32, rows32, spread(small[:, g, 0, :], 2, 32),
                                    ALU.subtract).then_inc(s["s_ready"], 1)
                for g in range(GROUPS):
                    v.wait_ge(s["e"], g + 1)
                    rows32 = sc[:, g].rearrange("p r (j k) -> p (r j) k", k=32)
                    own.step(v.tensor_reduce(small[:, g, 1, :], rows32, AX, ALU.add))
                    own.settle()
                    own.step(v.reciprocal(small[:, g, 0, :], small[:, g, 1, :]))
                    own.settle()
                    own.step(v.tensor_tensor(rows32, rows32, spread(small[:, g, 0, :], 2, 32), ALU.mult))
                    own.settle()
                    v.transpose(pT[:, g].rearrange("p r c -> p (r c)"),
                                sc[:, g].rearrange("p r c -> p (r c)")).then_inc(s["p"], 1)
                for g in range(GROUPS):
                    v.wait_ge(s["bo_added"], g + 1)
                    for b in range(2):
                        v.wait_ge(s["wo_sum"], 2 * g + b + 1)
                        two = res[:, TILES * g + 2 * b:TILES * g + 2 * b + 2, :]
                        v.tensor_tensor(two, two, two_tiles(g, b), ALU.add).then_inc(s["res1"], 1)
                v.wait_ge(s["res1"], 2 * GROUPS)
                norm(1)
                for g in range(GROUPS):
                    for b in range(2):
                        v.wait_ge(s["f2_sum"], 2 * g + b + 1)
                        two = res[:, TILES * g + 2 * b:TILES * g + 2 * b + 2, :]
                        v.tensor_tensor(two, two, two_tiles(g, 2 + b), ALU.add).then_inc(s["res2"], 1)

            @block.scalar
            def _(act):
                act.wait_ge(s["cols_in"], 16)

                def turned(j, base):
                    for g in range(GROUPS):
                        for f in range(DT):
                            act.wait_ge(s["turned"], GROUPS * DT * j + DT * g + f + 1)
                            act.activation(hT[:, g, f, :], ps[:, 4 * g + 2 * j + f, :], ACT.Identity,
                                           bias=cols[:, base + 2 + f:base + 3 + f],
                                           scale=cols[:, base + f:base + f + 1]).then_inc(s["hT"], 1)

                turned(0, 0)
                for g in range(GROUPS):
                    for m in range(DT):
                        act.wait_ge(s["q_sum"], DT * g + m + 1)
                        act.activation(qT[:, g, m, :], ps[:, 4 * g + 2 + m, :], ACT.Identity,
                                       bias=cols[:, 4 + m:5 + m]).then_inc(s["q"], 1)
                for g in range(GROUPS):
                    act.wait_ge(s["s_ready"], g + 1)
                    both = sc[:, g].rearrange("p r c -> p (r c)")
                    act.activation(both, both, ACT.Exp, scale=SCALE).then_inc(s["e"], 1)
                for g in range(GROUPS):
                    act.wait_ge(s["o_sum"], g + 1)
                    for hh in range(2):
                        act.activation(
                            oT[:, g, hh, :].rearrange("p (t i q) -> p i t q", t=TILES, i=4),
                            ps[:, 4 * g:4 * g + 4, hh * P:(hh + 1) * P].rearrange("p i (t q) -> p i t q", q=32),
                            ACT.Copy).then_inc(s["o"], 1)
                turned(1, 8)
                for g in range(GROUPS):
                    act.wait_ge(s["f_sum"], g + 1)
                    act.activation(fT[0:TOK_FF, g, :], ps[0:TOK_FF, 4 * g, :], ACT.Relu,
                                   bias=cols[0:TOK_FF, 12:13]).then_inc(s["f"], 1)

            @block.tensor
            def _(pe):
                def turn(j):
                    for g in range(GROUPS):
                        if j == 1:
                            pe.wait_ge(s["o"], 2 * (g + 1))
                        pe.wait_ge(s["z"], GROUPS * TILES * j + TILES * (g + 1))
                        turn_tiles(pe, z[:, g], mem.ident, ps[:, 4 * g + 2 * j:4 * g + 2 * j + 2, :], s["turned"])

                def columns(g, bank, w, at, done):
                    for m in range(DT):
                        for k in range(DT):
                            ins = pe.matmul(ps[:, bank + m, :], w[:, k, at + m * P:at + (m + 1) * P],
                                            hT[:, g, k, :], start=(k == 0), stop=(k == DT - 1))
                        ins.then_inc(done, 1)

                def tokens(bank, src, w, done, K=DT):
                    for t in range(TILES):
                        for k in range(K):
                            ins = pe.matmul(ps[:, bank + t // 2, (t % 2) * D:(t % 2 + 1) * D],
                                            src(k)[:, t * P:(t + 1) * P], w(k),
                                            start=(k == 0), stop=(k == K - 1))
                        if t % 2:
                            ins.then_inc(done, 1)

                turn(0)
                pe.wait_ge(s["qkv_in"], 16)
                for g in range(GROUPS):
                    pe.wait_ge(s["hT"], DT * (g + 1))
                    columns(g, 4 * g + 2, wqkv, 0, s["q_sum"])
                    columns(g, 4 * g, wqkv, D, s["k_sum"])
                for g in range(GROUPS):
                    pe.wait_ge(s["q"], DT * (g + 1))
                    tokens(4 * g + 2, lambda k: hT[:, g, k, :], lambda k: wqkv[:, k, 2 * D:3 * D], s["v_sum"])
                for g in range(GROUPS):
                    pe.wait_ge(s["k"], DT * (g + 1))
                    pe.wait_ge(s["v"], 2 * (g + 1))
                    for t in range(TILES):
                        for hh in range(2):
                            for i in range(4):
                                for r in range(4):
                                    at = slice(t * P + 32 * i, t * P + 32 * i + 32)
                                    ins = pe.matmul(ps[32 * i:32 * i + 32, 4 * g + r, (2 * t + hh) * 32:(2 * t + hh + 1) * 32],
                                                    qT[32 * r:32 * r + 32, g, hh, at],
                                                    kT[32 * r:32 * r + 32, g, hh, at],
                                                    start=True, stop=True)
                    ins.then_inc(s["s_sum"], 1)
                for g in range(GROUPS):
                    pe.wait_ge(s["p"], g + 1)
                    for hh in range(2):
                        for t in range(TILES):
                            for r in range(4):
                                for i in range(4):
                                    rows_i = slice(32 * i, 32 * i + 32)
                                    ins = pe.matmul(ps[32 * r:32 * r + 32, 4 * g + i, hh * P + t * 32:hh * P + (t + 1) * 32],
                                                    val[rows_i, g, t, (4 * hh + r) * 32:(4 * hh + r + 1) * 32],
                                                    pT[rows_i, g, r, (2 * t + hh) * 32:(2 * t + hh + 1) * 32],
                                                    start=True, stop=True)
                    ins.then_inc(s["o_sum"], 1)
                pe.wait_ge(s["wo_in"], 16)
                for g in range(GROUPS):
                    pe.wait_ge(s["o"], 2 * (g + 1))
                    tokens(4 * g, lambda k: oT[:, g, k, :], lambda k: wo[:, k, :], s["wo_sum"])
                turn(1)
                pe.wait_ge(s["ff_in"], 32)
                for g in range(GROUPS):
                    pe.wait_ge(s["res1"], 2 * (g + 1))
                    pe.wait_ge(s["hT"], DT * GROUPS + DT * (g + 1))
                    for k in range(DT):
                        ins = pe.matmul(ps[0:TOK_FF, 4 * g, :], ff1[:, k, :], hT[:, g, k, :],
                                        start=(k == 0), stop=(k == DT - 1))
                    ins.then_inc(s["f_sum"], 1)
                pe.wait_ge(s["p_own"], 1)
                for g in range(GROUPS):
                    pe.wait_ge(s["f"], g + 1)
                    tokens(4 * g + 2, lambda k: fT[:, g, :], lambda k: ff2, s["f2_sum"], K=1)
        end_block(nc, mem)


def absolute_max(v, own, out, src):
    own.step(v.tensor_reduce(out, src, AX, ALU.max, apply_absolute_value=True))


def quantiser(v, own, most, scale, inverse):
    own.step(v.tensor_scalar(scale, most, 1e-6, 1.0 / 127.0, ALU.max, ALU.mult))
    own.settle()
    own.step(v.reciprocal(inverse, scale))
    own.settle()


def quantise(v, own, src, inverse, shifted, out, done):
    own.step(v.tensor_scalar(shifted, src, inverse, ROUND, ALU.mult, ALU.add))
    own.settle()
    v.tensor_scalar(out, shifted, -ROUND, None, ALU.add).then_inc(done, 1)


def latent_attention_and_ffn(nc, ctx, mem, dram):
    s = named(mem, """mla_in ffn_in stats rstd z turned hT
        m1_sum m1 keff_sum keff veff_sum veff d_sum d c_sum c q_sum q k_sum k v_sum v
        s_sum s_ready e p o_sum res1 w_most w_all w1_q w2_q x_most x_all x_q x_scale
        a_sum a a_most a_all a_q a_scale b2_added f_sum res2 v_own p_own""")
    a = mem.fresh()
    w = a.take(2048)
    dq = w[:, 0:256].rearrange("p (f n) -> p f n", f=DT)
    dq_rows = w[:, 256:512]
    uq = w[:, 512:768]
    uk = w[:, 768:1024].rearrange("p (f n) -> p f n", f=DT)
    dkv = w[:, 1024:1280].rearrange("p (f n) -> p f n", f=DT)
    uv = w[:, 1280:1536].rearrange("p (f n) -> p f n", f=DT)
    wo = w[:, 1536:2048].rearrange("p (f n) -> p f n", f=DT)
    m1, keff, veff = a.take(DT, D), a.take(D), a.take(D)
    stats, mv, rstd = a.take(GROUPS, TILES, 6), a.take(GROUPS, TILES, 2), a.take(GROUPS, TILES)
    z, hT = a.take(GROUPS, TILES, D), a.take(GROUPS, DT, GROUP)
    dT, cT = a.take(GROUPS, GROUP), a.take(GROUPS, GROUP)
    qT = a.take(GROUPS, DT, GROUP)
    kT = a.take(GROUPS, 2, DT, GROUP)
    val = a.take(GROUPS, TILES, D)
    sc, pT = a.take(GROUPS, 4, 512), a.take(GROUPS, 4, 512)
    small = a.take(GROUPS, 2, 64)
    w1, w2 = a.take(DT, FFN), a.take(FFN // P, D)
    w1q, w2q = a.take(DT, FFN, dtype=BF16), a.take(FFN // P, D, dtype=BF16)
    b1, b1s, b2 = a.take(FFN // P), a.take(FFN // P), a.take(D)
    most, alls, scale, inverse = a.take(4), a.take(4), a.take(4), a.take(4)
    parts = a.take(4)
    prod = a.take(2)
    xq = a.take(GROUPS, DT, GROUP, dtype=BF16)
    shifted = a.take(2048)
    hidden = a.take(GROUPS, FFN // P, GROUP)
    hq = a.take(GROUPS, FFN // P, GROUP, dtype=BF16)
    ps, res, h = mem.ps, mem.res, mem.h
    SCALE = MLA_HS ** -0.5
    M = FFN // P

    def flat(ap):
        return ap.rearrange("p a b -> p (a b)")

    def tiles_of(g):
        return res[:, TILES * g:TILES * (g + 1), :]

    def two_tiles(g, b):
        return ps[:, 4 * g + b, :].rearrange("p (t d) -> p t d", t=2)

    with nc.Block() as block:
        @block.sync
        def _(sp):
            sp.dma_start(w, dram["mla"]).then_inc(s["mla_in"], 16)
            sp.dma_start(w1, dram["ffn_w1"]).then_inc(s["ffn_in"], 16)
            sp.dma_start(w2, dram["ffn_w2"]).then_inc(s["ffn_in"], 16)
            sp.dma_start(b1, dram["ffn_b1"]).then_inc(s["ffn_in"], 16)
            sp.dma_start(b2, dram["ffn_b2"]).then_inc(s["ffn_in"], 16)

        @block.gpsimd
        def _(pool):
            own = Steps(pool, s["p_own"])
            for g in range(GROUPS):
                pool.wait_ge(s["stats"], g + 1)
                norm_rstd(pool, own, mv[:, g, :, 1], rstd[:, g, :], mem.minus_half, EPS, s["rstd"], g + 1)
            for n in range(2):
                pool.wait_ge(s["w_most"], n + 1)
                pool.partition_all_reduce(alls[:, n:n + 1], most[:, n:n + 1], P, RMAX).then_inc(s["w_all"], 1)
                pool.wait_ge(s["w_all"], n + 1)
            for g in range(GROUPS):
                n = GROUPS + g + 1
                pool.wait_ge(s["stats"], n)
                norm_rstd(pool, own, mv[:, g, :, 1], rstd[:, g, :], mem.minus_half, EPS, s["rstd"], n)
            pool.wait_ge(s["x_most"], 1)
            pool.partition_all_reduce(alls[:, 2:3], most[:, 2:3], P, RMAX).then_inc(s["x_all"], 1)
            pool.wait_ge(s["x_all"], 1)
            pool.wait_ge(s["a_most"], 1)
            pool.partition_all_reduce(alls[:, 3:4], most[:, 3:4], P, RMAX).then_inc(s["a_all"], 1)
            pool.wait_ge(s["a_all"], 1)
            pool.wait_ge(s["a_scale"], 1)
            own.step(pool.tensor_scalar(b2, b2, prod[:, 1:2], 1.0, ALU.mult, ALU.mult))
            for g in range(GROUPS):
                own.settle()
                if g:
                    pool.wait_ge(s["b2_added"], g)
                pool.tensor_tensor(tiles_of(g), tiles_of(g), spread(b2, 1, TILES), ALU.add).then_inc(s["b2_added"], 1)
            pool.wait_ge(s["b2_added"], GROUPS)
            for g in range(GROUPS):
                n = 2 * GROUPS + g + 1
                pool.wait_ge(s["stats"], n)
                norm_rstd(pool, own, mv[:, g, :, 1], rstd[:, g, :], mem.minus_half, EPS, s["rstd"], n)

        @block.vector
        def _(v):
            own = Steps(v, s["v_own"])

            def statistics():
                for g in range(GROUPS):
                    norm_stats(v, own, tiles_of(g), stats[:, g], mv[:, g], s["stats"])

            def apply(j, out):
                for g in range(GROUPS):
                    v.wait_ge(s["rstd"], GROUPS * j + g + 1)
                    norm_apply(v, tiles_of(g), mv[:, g], rstd[:, g], out(g), s["z"])

            statistics()
            v.wait_ge(s["ffn_in"], 64)
            for n, x in enumerate((w1, w2)):
                v.tensor_reduce(most[:, n:n + 1], flat(x), AX, ALU.max,
                                apply_absolute_value=True).then_inc(s["w_most"], 1)
            apply(0, lambda g: z[:, g])
            for n, (x, q, done) in enumerate(((w1, w1q, s["w1_q"]), (w2, w2q, s["w2_q"]))):
                v.wait_ge(s["w_all"], n + 1)
                quantiser(v, own, alls[:, n:n + 1], scale[:, n:n + 1], inverse[:, n:n + 1])
                if n:
                    v.wait_ge(s["w1_q"], 1)
                quantise(v, own, flat(x), inverse[:, n:n + 1], shifted, flat(q), done)
            for g in range(GROUPS):
                v.wait_ge(s["c_sum"], g + 1)
                v.tensor_copy(cT[:, g, :], ps[:, 4 * g + 3, :]).then_inc(s["c"], 1)
            for g in range(GROUPS):
                v.wait_ge(s["k_sum"], DT * (g + 1))
                for e in range(2):
                    v.tensor_scalar(kT[:, g, e, 1, :], ps[:, 4 * g + 3, :], mem.parity[:, e:e + 1], None,
                                    ALU.mult).then_inc(s["k"], 1)
            for g in range(GROUPS):
                for b in range(2):
                    v.wait_ge(s["v_sum"], 2 * g + b + 1)
                    v.tensor_copy(val[:, g, 2 * b:2 * b + 2, :], two_tiles(g, b)).then_inc(s["v"], 1)
            for g in range(GROUPS):
                v.wait_ge(s["s_sum"], g + 1)
                rows32 = sc[:, g].rearrange("p r (j k) -> p (r j) k", k=32)
                own.step(v.tensor_tensor(
                    sc[:, g].rearrange("p r (j k) -> p r j k", k=32),
                    ps[:, 4 * g:4 * g + 4, :].rearrange("p r (j k) -> p r j k", k=32),
                    spread(spread(mem.causal, 1, 16), 1, 4), ALU.add))
                own.settle()
                own.step(v.tensor_reduce(small[:, g, 0, :], rows32, AX, ALU.max))
                own.settle()
                v.tensor_tensor(rows32, rows32, spread(small[:, g, 0, :], 2, 32),
                                ALU.subtract).then_inc(s["s_ready"], 1)
            for g in range(GROUPS):
                v.wait_ge(s["e"], g + 1)
                rows32 = sc[:, g].rearrange("p r (j k) -> p (r j) k", k=32)
                own.step(v.tensor_reduce(small[:, g, 1, :], rows32, AX, ALU.add))
                own.settle()
                own.step(v.reciprocal(small[:, g, 0, :], small[:, g, 1, :]))
                own.settle()
                own.step(v.tensor_tensor(rows32, rows32, spread(small[:, g, 0, :], 2, 32), ALU.mult))
                own.settle()
                v.transpose(flat(pT[:, g]), flat(sc[:, g])).then_inc(s["p"], 1)
            for pair in range(2):
                for g in range(GROUPS):
                    v.wait_ge(s["o_sum"], GROUPS * pair + g + 1)
                    for i in range(4):
                        rows_i = slice(32 * i, 32 * i + 32)
                        t = TILES * g + 2 * pair
                        two = res[rows_i, t:t + 2, :]
                        v.tensor_tensor(two, two, ps[rows_i, 4 * g + i, :].rearrange("p (t d) -> p t d", t=2),
                                        ALU.add).then_inc(s["res1"], 1)
            v.wait_ge(s["res1"], 4 * GROUPS * 2)
            statistics()
            apply(1, lambda g: z[:, g])
            v.wait_ge(s["z"], 2 * GROUPS * TILES)
            absolute_max(v, own, parts[:, 0:1], z.rearrange("p g t d -> p (g t d)"))
            own.settle()
            v.tensor_copy(most[:, 2:3], parts[:, 0:1]).then_inc(s["x_most"], 1)
            v.wait_ge(s["x_all"], 1)
            quantiser(v, own, alls[:, 2:3], scale[:, 2:3], inverse[:, 2:3])
            own.step(v.tensor_tensor(prod[:, 0:1], scale[:, 0:1], scale[:, 2:3], ALU.mult))
            own.settle()
            v.tensor_scalar(b1s, b1, prod[:, 0:1], None, ALU.mult).then_inc(s["x_scale"], 1)
            for g in range(GROUPS):
                v.wait_ge(s["hT"], DT * GROUPS + DT * (g + 1))
                quantise(v, own, flat(hT[:, g]), inverse[:, 2:3], flat(hT[:, g]), flat(xq[:, g]), s["x_q"])
            for g in range(GROUPS):
                for b in range(2):
                    v.wait_ge(s["a"], M * g + 4 * b + 4)
                    n = 2 * g + b
                    absolute_max(v, own, parts[:, n:n + 1], flat(hidden[:, g, 4 * b:4 * b + 4, :]))
            own.settle()
            v.tensor_reduce(most[:, 3:4], parts, AX, ALU.max).then_inc(s["a_most"], 1)
            v.wait_ge(s["a_all"], 1)
            quantiser(v, own, alls[:, 3:4], scale[:, 3:4], inverse[:, 3:4])
            v.tensor_tensor(prod[:, 1:2], scale[:, 1:2], scale[:, 3:4], ALU.mult).then_inc(s["a_scale"], 1)
            for g in range(GROUPS):
                quantise(v, own, flat(hidden[:, g]), inverse[:, 3:4], flat(hidden[:, g]), flat(hq[:, g]), s["a_q"])
            v.wait_ge(s["a_scale"], 1)
            for g in range(GROUPS):
                v.wait_ge(s["b2_added"], g + 1)
                for b in range(2):
                    v.wait_ge(s["f_sum"], 2 * g + b + 1)
                    t = TILES * g + 2 * b
                    two = res[:, t:t + 2, :]
                    v.scalar_tensor_tensor(two, two_tiles(g, b), prod[:, 1:2], two, ALU.mult,
                                           ALU.add).then_inc(s["res2"], 1)
            v.wait_ge(s["res2"], 2 * GROUPS)
            statistics()
            apply(2, lambda g: h[:, TILES * g:TILES * (g + 1), :])

        @block.scalar
        def _(act):
            act.wait_ge(s["m1_sum"], 1)
            act.activation(flat(m1), ps[:, 6, :], ACT.Copy).then_inc(s["m1"], 1)
            act.wait_ge(s["veff_sum"], 1)
            act.activation(veff, ps[:, 7, 0:D], ACT.Copy).then_inc(s["veff"], 1)
            act.wait_ge(s["keff_sum"], 1)
            act.activation(keff, ps[:, 6, 0:D], ACT.Copy).then_inc(s["keff"], 1)

            def turned(j):
                for g in range(GROUPS):
                    for f in range(DT):
                        act.wait_ge(s["turned"], GROUPS * DT * j + DT * g + f + 1)
                        act.activation(hT[:, g, f, :], ps[:, 4 * g + f, :], ACT.Copy).then_inc(s["hT"], 1)

            turned(0)
            for g in range(GROUPS):
                act.wait_ge(s["d_sum"], g + 1)
                act.activation(dT[:, g, :], ps[:, 4 * g + 2, :], ACT.Copy).then_inc(s["d"], 1)
            for g in range(GROUPS):
                for m in range(DT):
                    act.wait_ge(s["q_sum"], DT * g + m + 1)
                    act.activation(qT[:, g, m, :], ps[:, 4 * g + m, :], ACT.Copy).then_inc(s["q"], 1)
            for g in range(GROUPS):
                act.wait_ge(s["k_sum"], DT * g + 1)
                for e in range(2):
                    act.activation(kT[:, g, e, 0, :], ps[:, 4 * g + 2, :], ACT.Identity, bias=0.0,
                                   scale=mem.parity[:, e:e + 1]).then_inc(s["k"], 1)
            for g in range(GROUPS):
                act.wait_ge(s["s_ready"], g + 1)
                act.activation(flat(sc[:, g]), flat(sc[:, g]), ACT.Exp, scale=SCALE).then_inc(s["e"], 1)
            turned(1)
            act.wait_ge(s["x_scale"], 1)
            for g in range(GROUPS):
                for m in range(M):
                    act.wait_ge(s["a_sum"], M * g + m + 1)
                    act.activation(hidden[:, g, m, :], ps[:, 4 * g + m % 4, :], ACT.Gelu,
                                   bias=b1s[:, m:m + 1], scale=prod[:, 0:1]).then_inc(s["a"], 1)

        @block.tensor
        def _(pe):
            pe.wait_ge(s["mla_in"], 16)
            for f in range(DT):
                ins = pe.matmul(ps[:, 6, f * D:(f + 1) * D], uq[:, f * P:(f + 1) * P], dq_rows,
                                start=True, stop=True)
            ins.then_inc(s["m1_sum"], 1)
            for f in range(DT):
                ins = pe.matmul(ps[:, 7, 0:D], uv[:, f, :], wo[:, f, :], start=(f == 0), stop=(f == DT - 1))
            ins.then_inc(s["veff_sum"], 1)
            pe.wait_ge(s["m1"], 1)
            for f in range(DT):
                ins = pe.matmul(ps[:, 6, 0:D], uk[:, f, :], m1[:, f, :], start=(f == 0), stop=(f == DT - 1))
            ins.then_inc(s["keff_sum"], 1)

            def turn(j):
                for g in range(GROUPS):
                    pe.wait_ge(s["z"], GROUPS * TILES * j + TILES * (g + 1))
                    turn_tiles(pe, z[:, g], mem.ident, ps[:, 4 * g:4 * g + 2, :], s["turned"])

            turn(0)
            pe.wait_ge(s["veff"], 1)
            pe.wait_ge(s["keff"], 1)
            for g in range(GROUPS):
                pe.wait_ge(s["hT"], DT * (g + 1))
                for w_in, bank, done in ((dq, 2, s["d_sum"]), (dkv, 3, s["c_sum"])):
                    for k in range(DT):
                        ins = pe.matmul(ps[:, 4 * g + bank, :], w_in[:, k, :], hT[:, g, k, :],
                                        start=(k == 0), stop=(k == DT - 1))
                    ins.then_inc(done, 1)
            for g in range(GROUPS):
                pe.wait_ge(s["d"], g + 1)
                for m in range(DT):
                    pe.matmul(ps[:, 4 * g + m, :], uq[:, m * P:(m + 1) * P], dT[:, g, :],
                              start=True, stop=True).then_inc(s["q_sum"], 1)
                pe.wait_ge(s["c"], g + 1)
                for m in range(DT):
                    pe.matmul(ps[:, 4 * g + 2 + m, :], keff[:, m * P:(m + 1) * P], cT[:, g, :],
                              start=True, stop=True).then_inc(s["k_sum"], 1)
            for g in range(GROUPS):
                pe.wait_ge(s["q"], DT * (g + 1))
                for t in range(TILES):
                    ins = pe.matmul(ps[:, 4 * g + t // 2, (t % 2) * D:(t % 2 + 1) * D],
                                    cT[:, g, t * P:(t + 1) * P], veff, start=True, stop=True)
                    if t % 2:
                        ins.then_inc(s["v_sum"], 1)
            pe.wait_ge(s["k"], 4 * GROUPS)
            for g in range(GROUPS):
                pe.wait_ge(s["v"], 2 * (g + 1))
                for t in range(TILES):
                    for f in range(DT):
                        for e in range(2):
                            col = t * P + (2 * f + e) * 32
                            for i in range(4):
                                for r in range(4):
                                    at = slice(t * P + 32 * i, t * P + 32 * i + 32)
                                    ins = pe.matmul(ps[32 * i:32 * i + 32, 4 * g + r, col:col + 32],
                                                    qT[32 * r:32 * r + 32, g, f, at],
                                                    kT[32 * r:32 * r + 32, g, e, f, at],
                                                    start=True, stop=True)
                ins.then_inc(s["s_sum"], 1)
            for pair in range(2):
                for g in range(GROUPS):
                    pe.wait_ge(s["p"], g + 1)
                    if pair:
                        pe.wait_ge(s["res1"], 4 * (g + 1))
                    for t in (2 * pair, 2 * pair + 1):
                        for f in range(DT):
                            for e in range(2):
                                col = t * P + (2 * f + e) * 32
                                for r in range(4):
                                    head = 8 * f + 2 * r + e
                                    for i in range(4):
                                        rows_i = slice(32 * i, 32 * i + 32)
                                        out_at = (t % 2) * D + head * MLA_HS
                                        ins = pe.matmul(ps[rows_i, 4 * g + i, out_at:out_at + MLA_HS],
                                                        pT[rows_i, g, r, col:col + 32],
                                                        val[rows_i, g, t, head * MLA_HS:(head + 1) * MLA_HS],
                                                        start=True, stop=True)
                    ins.then_inc(s["o_sum"], 1)
            turn(1)
            pe.wait_ge(s["w1_q"], 1)
            for g in range(GROUPS):
                pe.wait_ge(s["x_q"], g + 1)
                for m in range(M):
                    if m >= 4:
                        pe.wait_ge(s["a"], M * g + m - 3)
                    for k in range(DT):
                        ins = pe.matmul(ps[:, 4 * g + m % 4, :], w1q[:, k, m * P:(m + 1) * P], xq[:, g, k, :],
                                        start=(k == 0), stop=(k == DT - 1))
                    ins.then_inc(s["a_sum"], 1)
            pe.wait_ge(s["w2_q"], 1)
            for g in range(GROUPS):
                pe.wait_ge(s["a_q"], g + 1)
                for t in range(TILES):
                    for k in range(M):
                        ins = pe.matmul(ps[:, 4 * g + t // 2, (t % 2) * D:(t % 2 + 1) * D],
                                        hq[:, g, k, t * P:(t + 1) * P], w2q[:, k, :],
                                        start=(k == 0), stop=(k == M - 1))
                    if t % 2:
                        ins.then_inc(s["f_sum"], 1)
    end_block(nc, mem)


def mamba_plan():
    SCANS, C = LAYERS * GROUPS, CHUNKS
    jobs = []
    for n in range(SCANS):
        base = C * (n - 1)
        at = {"norm": 4, "xs0": 5, "xs1": 6, "conv0": 7, "conv1": 8, "gate0": 9, "xproj": 10, "gate1": 11,
              "dt0": 12, "dt1": 12}
        first = {"norm": 0, "xs0": 1, "xs1": 2, "conv0": 3, "conv1": 4, "gate0": 5, "xproj": 6, "gate1": 7,
                 "dt0": 8, "dt1": 9}
        for what, p in at.items():
            where = base + p if n else first[what] - 100
            jobs.append((where, 0, (what.rstrip("01"), n, int(what[-1]) if what[-1] in "01" else 0)))
        jobs.append((C * (n + 1) + 1, 0, ("out", n, 0)))
        for part in range(NC):
            q = NC * n + part
            start = KT * q
            for r, lead in enumerate((4, 3, 2, 1)):
                jobs.append((start - lead if q else -50, 1 + r, ("rows", q, r)))
    jobs.sort()
    slot = {job: k % 2 for k, (_, _, job) in enumerate(jobs)}
    order = [job for _, _, job in jobs]
    place = {job: p for p, _, job in jobs}

    def with_chunks(items):
        items = items + [(c, 10 ** 9, ("chunk", c, 0)) for c in range(C * SCANS)]
        return [job for _, _, job in sorted(items)]

    def later(p, by):
        return p if p < 0 else p + by

    tensor = with_chunks([(p, k, job) for k, (p, _, job) in enumerate(jobs)])
    scalar, vector = [], []
    for k, job in enumerate(order):
        p, (what, n, _) = place[job], job
        if what == "norm":
            scalar.append((later(p, 1), k - 1, ("square", n, 0)))
            vector.append((p, k, ("z", n, 0)))
        if what == "dt" and job[2] == 1:
            vector.append((later(p, 2), k, ("delta", n, 0)))
        if what in ("xproj", "out"):
            vector.append((later(p, 1 if what == "xproj" else 2), k, job))
        else:
            scalar.append((later(p, 2), k, job))
    for n in range(SCANS):
        vector.append((C * (n + 1) + (1 if n < SCANS - 1 else 0), -1, ("y", n, 0)))
    return tensor, with_chunks(scalar), with_chunks(vector), slot, order


def mamba_layers(nc, ctx, mem, dram):
    s = named(mem, """cols_in in_in x_in dt_in out_in sel_in zeroed diag a_exp a_neg squares rstd z
        turned hT xs_sum xs gate_sum gate conv_sum u x_sum x bc3 dt_sum dt_free soft delta du bc_sum bc
        decay scanned weighted reduced y_free y o_sum bo_added h_out v_own p_own""")
    PAD = (CONV - 1) // 2
    SEQ = GROUP // T
    SCANS = LAYERS * GROUPS
    a = mem.fresh()
    w_in = a.take(DT, 2 * INNER)
    w_conv = a.take(KT * CONV, P)
    w_x = a.take(KT, RANK + 2 * STATE)
    w_dt = a.take(INNER, rows=RANK)
    w_out = a.take(KT, D)
    cols = a.take(LAYERS, 48)
    decay_rate = a.take(LAYERS, KT, STATE)
    b_out = a.take(LAYERS, D)
    squares, rstd = a.take(SCANS, TILES), a.take(SCANS, TILES)
    select = a.take(2 * STATE, P, dtype=BF16, rows=96)
    zh = a.take(4, GROUP)
    z = zh[:, 0:2, :].rearrange("p a (t d) -> p (a t) d", d=D)
    hT = zh[:, 2:4, :]
    soft = zh
    padded = a.take(KT, SEQ, T + 2 * PAD)
    u, gate = a.take(2, KT, GROUP), a.take(2, KT, GROUP)
    delta, du = a.take(2, KT, GROUP), a.take(2, KT, GROUP)
    xd = a.take(GROUP, rows=96)
    bc3 = a.take(2, GROUP, dtype=BF16, rows=96)
    rest = a.take(GROUP, rows=96)
    middle = a.take(GROUP, dtype=BF16, rows=96)
    bc = a.take(2, 2 * CH, GROUP)
    decay, work = a.take(2, CH, GROUP), a.take(2, CH, GROUP)
    ps, h = mem.ps, mem.h
    for_tensor, for_scalar, for_vector, slot, jobs = mamba_plan()

    def flat(ap):
        return ap.rearrange("p a b -> p (a b)")

    def steps_of(ap):
        return ap.rearrange("p (b t) -> p b t", t=T)

    def tiles_of(n):
        g = n % GROUPS
        return h[:, TILES * g:TILES * (g + 1), :]

    def banks(job):
        return ps[:, 4 + 2 * slot[job]:6 + 2 * slot[job], :]

    def column(n, at):
        return cols[:, n // GROUPS, at:at + 1]

    B_IN, B_CONV, B_DT, SKIP, W_NORM, TAPS = 0, 8, 12, 16, 20, 24

    def emptied(job):
        what, n, half = job
        return {"norm": (s["hT"], DT * (n + 1)), "xs": (s["xs"], KT * n + 2 * half + 2),
                "gate": (s["gate"], KT * n + 2 * half + 2), "conv": (s["u"], KT * n + 2 * half + 2),
                "xproj": (s["x"], n + 1), "dt": (s["dt_free"], KT * n + 2 * half + 2),
                "rows": (s["bc"], CH * n + half + 1), "out": (s["h_out"], 2 * (n + 1))}[what]

    with nc.Block() as block:
        @block.sync
        def _(sp):
            sp.dma_start(cols, dram["mam_cols"].rearrange("l p c -> p l c")).then_inc(s["cols_in"], 16)
            sp.dma_start(decay_rate.rearrange("p l m s -> p l (m s)"),
                         dram["mam_alog"].rearrange("l p m s -> p l (m s)")).then_inc(s["cols_in"], 16)
            sp.dma_start(b_out, dram["mam_bo"].rearrange("l p d -> p l d")).then_inc(s["cols_in"], 16)
            for l in range(LAYERS):
                last = GROUPS * l
                if l == 0:
                    sp.dma_start(w_in, dram["mam_in"][l, :, :, :]).then_inc(s["in_in"], 16)
                    sp.dma_start(select, dram["select"]).then_inc(s["sel_in"], 16)
                if l:
                    sp.wait_ge(s["x_sum"], last)
                sp.dma_start(w_x, dram["mam_x"][l, :, :, :]).then_inc(s["x_in"], 16)
                if l:
                    sp.wait_ge(s["dt_sum"], KT * last)
                sp.dma_start(w_dt, dram["mam_dt"][l, :, :]).then_inc(s["dt_in"], 16)
                if l:
                    sp.wait_ge(s["gate_sum"], KT * last)
                    sp.wait_ge(s["xs_sum"], KT * last)
                    sp.dma_start(w_in, dram["mam_in"][l, :, :, :]).then_inc(s["in_in"], 16)
                    sp.wait_ge(s["o_sum"], 2 * last)
                sp.dma_start(w_out, dram["mam_out"][l, :, :, :]).then_inc(s["out_in"], 16)

        @block.gpsimd
        def _(pool):
            own = Steps(pool, s["p_own"])

            def scale_rows(n):
                pool.wait_ge(s["squares"], TILES * (n + 1))
                own.step(pool.tensor_scalar(rstd[:, n], squares[:, n], 1.0 / D, EPS, ALU.mult, ALU.add))
                own.settle()
                pool.tensor_tensor(rstd[:, n], rstd[:, n], mem.minus_half, ALU.pow).then_inc(s["rstd"], 1)
                pool.wait_ge(s["rstd"], n + 1)

            def diagonals(l):
                pool.wait_ge(s["cols_in"], 48)
                pool.tensor_tensor(w_conv, spread(mem.ident, 1, KT * CONV),
                                   spread(cols[:, l, TAPS:TAPS + KT * CONV], 2, P), ALU.mult).then_inc(s["diag"], 1)
                pool.wait_ge(s["diag"], l + 1)

            for n in range(SCANS):
                scale_rows(n)
                if n == 0:
                    own.step(pool.memset(padded, 0.0))
                    own.settle()
                    diagonals(0)
                    own.step(pool.memset(decay, 0.0))
                    own.settle()
                if n % GROUPS == GROUPS - 1 and n < SCANS - 1:
                    pool.wait_ge(s["conv_sum"], KT * (n + 1))
                    diagonals(n // GROUPS + 1)
                pool.wait_ge(s["z"], TILES * (n + 1))
                pool.tensor_tensor(tiles_of(n), tiles_of(n), spread(b_out[:, n // GROUPS, :], 1, TILES),
                                   ALU.add).then_inc(s["bo_added"], 1)
                pool.wait_ge(s["bo_added"], n + 1)

        @block.scalar
        def _(act):
            act.wait_ge(s["cols_in"], 48)
            for job in for_scalar:
                what, n, half = job
                b = n % 2
                if what == "square":
                    if n >= 2:
                        act.wait_ge(s["h_out"], 2 * (n - 1))
                    if n:
                        act.wait_ge(s["delta"], n)
                    for t in range(TILES):
                        act.activation(z[:, t, :], tiles_of(n)[:, t, :], ACT.Square,
                                       accum_out=squares[:, n, t:t + 1]).then_inc(s["squares"], 1)
                if what == "norm":
                    act.wait_ge(s["turned"], DT * (n + 1))
                    for f in range(DT):
                        act.activation(hT[:, f, :], banks(job)[:, f, :], ACT.Identity, bias=0.0,
                                       scale=column(n, W_NORM + f)).then_inc(s["hT"], 1)
                if what == "xs":
                    act.wait_ge(s["p_own"], 2)
                    for i in range(2):
                        m = 2 * half + i
                        act.wait_ge(s["xs_sum"], KT * n + m + 1)
                        act.activation(padded[:, m, :, PAD:PAD + T], steps_of(banks(job)[:, i, :]), ACT.Identity,
                                       bias=column(n, B_IN + m)).then_inc(s["xs"], 1)
                if what == "gate":
                    for i in range(2):
                        m = 2 * half + i
                        act.wait_ge(s["gate_sum"], KT * n + m + 1)
                        act.activation(gate[:, b, m, :], banks(job)[:, i, :], ACT.Silu,
                                       bias=column(n, B_IN + KT + m)).then_inc(s["gate"], 1)
                if what == "conv":
                    for i in range(2):
                        m = 2 * half + i
                        act.wait_ge(s["conv_sum"], KT * n + m + 1)
                        act.activation(u[:, b, m, :], banks(job)[:, i, :], ACT.Silu,
                                       bias=column(n, B_CONV + m)).then_inc(s["u"], 1)
                if what == "dt":
                    if half == 0:
                        act.wait_ge(s["gate_sum"], KT * (n + 1))
                    if half == 0 and n % GROUPS == 0:
                        l = n // GROUPS
                        act.activation(flat(decay_rate[:, l]), flat(decay_rate[:, l]), ACT.Exp).then_inc(s["a_exp"], 1)
                    for i in range(2):
                        m = 2 * half + i
                        act.wait_ge(s["dt_sum"], KT * n + m + 1)
                        act.activation(soft[:, m, :], banks(job)[:, i, :], ACT.Abs, bias=column(n, B_DT + m))\
                           .then_inc(s["soft"], 1)
                        act.activation(delta[:, b, m, :], banks(job)[:, i, :], ACT.Relu,
                                       bias=column(n, B_DT + m)).then_inc(s["dt_free"], 1)
                    if half == 1:
                        act.wait_ge(s["soft"], (KT + 2) * n + KT)
                        act.activation(flat(soft), flat(soft), ACT.Exp, scale=-1.0).then_inc(s["soft"], 1)
                        act.wait_ge(s["soft"], (KT + 2) * n + KT + 1)
                        act.activation(flat(soft), flat(soft), ACT.Ln, bias=1.0).then_inc(s["soft"], 1)
                if what == "rows":
                    if n >= 2:
                        act.wait_ge(s["weighted"], KT * (n - 1))
                    act.wait_ge(s["bc_sum"], CH * n + half + 1)
                    act.activation(bc[:, n % 2, 2 * half:2 * half + 2, :], banks(job), ACT.Copy).then_inc(s["bc"], 1)
                if what == "chunk":
                    g, part, m = n // CHUNKS, n % CHUNKS // KT, n % KT
                    act.wait_ge(s["delta"], g + 1)
                    act.wait_ge(s["a_neg"], g // GROUPS + 1)
                    if n == 0:
                        act.wait_ge(s["p_own"], 3)
                    if n >= 2:
                        act.wait_ge(s["scanned"], n - 1)
                    for j in range(CH):
                        state = CH * part + j
                        act.activation(steps_of(decay[:, n % 2, j, :])[:, :, 1:T],
                                       steps_of(delta[:, g % 2, m, :])[:, :, 1:T], ACT.Exp,
                                       scale=decay_rate[:, g // GROUPS, m, state:state + 1]).then_inc(s["decay"], 1)

        @block.vector
        def _(v):
            own = Steps(v, s["v_own"])
            for job in for_vector:
                what, n, _ = job
                b = n % 2
                if what == "z":
                    v.wait_ge(s["rstd"], n + 1)
                    for t in range(TILES):
                        v.tensor_scalar(z[:, t, :], tiles_of(n)[:, t, :], rstd[:, n, t:t + 1], None,
                                        ALU.mult).then_inc(s["z"], 1)
                if what == "xproj":
                    lo, mid, hi = slice(0, 32), slice(32, 64), slice(64, 96)
                    v.wait_ge(s["x_sum"], n + 1)
                    v.tensor_copy(xd, banks(job)[0:96, 0, :]).then_inc(s["x"], 1)
                    v.wait_ge(s["x"], n + 1)
                    own.step(v.tensor_copy(bc3[hi, b, :], xd[hi, :]))
                    own.settle()
                    own.step(v.tensor_tensor(rest[hi, :], xd[hi, :], bc3[hi, b, :], ALU.subtract))
                    own.settle()
                    own.step(v.tensor_copy(middle[hi, :], rest[hi, :]))
                    own.settle()
                    own.step(v.tensor_tensor(rest[hi, :], rest[hi, :], middle[hi, :], ALU.subtract))
                    own.step(v.tensor_copy(bc3[mid, b, :], middle[hi, :]))
                    own.settle()
                    v.tensor_copy(bc3[lo, b, :], rest[hi, :]).then_inc(s["bc3"], 1)
                if what == "delta":
                    if n % GROUPS == 0:
                        l = n // GROUPS
                        v.wait_ge(s["a_exp"], l + 1)
                        v.tensor_scalar(flat(decay_rate[:, l]), flat(decay_rate[:, l]), -1.0, None,
                                        ALU.mult).then_inc(s["a_neg"], 1)
                    v.wait_ge(s["soft"], (KT + 2) * (n + 1))
                    v.wait_ge(s["dt_free"], KT * (n + 1))
                    v.tensor_tensor(flat(delta[:, b]), flat(delta[:, b]), flat(soft), ALU.add).then_inc(s["delta"], 1)
                    v.wait_ge(s["delta"], n + 1)
                    v.wait_ge(s["u"], KT * (n + 1))
                    v.tensor_tensor(flat(du[:, b]), flat(delta[:, b]), flat(u[:, b]), ALU.mult).then_inc(s["du"], 1)
                    v.wait_ge(s["du"], n + 1)
                if what == "chunk":
                    g, q, m = n // CHUNKS, n // KT, n % KT
                    rows = bc[:, q % 2]
                    w = work[:, n % 2]
                    v.wait_ge(s["bc"], CH * q + CH // 2)
                    if n >= 2:
                        v.wait_ge(s["reduced"], n - 1)
                    own.step(v.tensor_tensor(w, spread(du[:, g % 2, m, :], 1, CH), rows[:, 0:CH, :], ALU.mult))
                    v.wait_ge(s["decay"], CH * (n + 1))
                    own.settle()
                    v.tensor_tensor_scan(flat(w), flat(decay[:, n % 2]), flat(w), 0.0, ALU.mult,
                                         ALU.add).then_inc(s["scanned"], 1)
                    v.wait_ge(s["scanned"], n + 1)
                    v.wait_ge(s["bc"], CH * (q + 1))
                    v.tensor_tensor(w, w, rows[:, CH:2 * CH, :], ALU.mult).then_inc(s["weighted"], 1)
                if what == "y":
                    v.wait_ge(s["reduced"], CHUNKS * (n + 1))
                    v.wait_ge(s["gate"], KT * (n + 1))
                    v.wait_ge(s["cols_in"], 48)
                    for m in range(KT):
                        v.scalar_tensor_tensor(du[:, b, m, :], u[:, b, m, :], column(n, SKIP + m), ps[:, m, :],
                                               ALU.mult, ALU.add).then_inc(s["y_free"], 1)
                    for m in range(KT):
                        v.wait_ge(s["y_free"], KT * n + m + 1)
                        v.tensor_tensor(du[:, b, m, :], du[:, b, m, :], gate[:, b, m, :], ALU.mult)\
                         .then_inc(s["y"], 1)
                if what == "out":
                    v.wait_ge(s["bo_added"], n + 1)
                    for i in range(2):
                        v.wait_ge(s["o_sum"], 2 * n + i + 1)
                        two = tiles_of(n)[:, 2 * i:2 * i + 2, :]
                        v.tensor_tensor(two, two, banks(job)[:, i, :].rearrange("p (t d) -> p t d", t=2),
                                        ALU.add).then_inc(s["h_out"], 1)

        @block.tensor
        def _(pe):
            for job in for_tensor:
                what, n, half = job
                b, l = n % 2, n // GROUPS
                if what != "chunk" and jobs.index(job) >= 2:
                    pe.wait_ge(*emptied(jobs[jobs.index(job) - 2]))
                if what == "norm":
                    pe.wait_ge(s["z"], TILES * (n + 1))
                    turn_tiles(pe, z, mem.ident, banks(job), s["turned"])
                if what in ("xs", "gate"):
                    pe.wait_ge(s["in_in"], 16 * (l + 1))
                    pe.wait_ge(s["hT"], DT * (n + 1))
                    for i in range(2):
                        at = (2 * half + i) * P + (0 if what == "xs" else INNER)
                        for k in range(DT):
                            ins = pe.matmul(banks(job)[:, i, :], w_in[:, k, at:at + P],
                                            hT[:, k, :], start=(k == 0), stop=(k == DT - 1))
                        ins.then_inc(s["xs_sum"] if what == "xs" else s["gate_sum"], 1)
                if what == "conv":
                    pe.wait_ge(s["diag"], l + 1)
                    pe.wait_ge(s["xs"], KT * n + 2 * half + 2)
                    for i in range(2):
                        m = 2 * half + i
                        for k in range(CONV):
                            ins = pe.matmul(banks(job)[:, i, :], w_conv[:, CONV * m + k, :],
                                            padded[:, m, :, k:k + T], start=(k == 0), stop=(k == CONV - 1))
                        ins.then_inc(s["conv_sum"], 1)
                if what == "xproj":
                    pe.wait_ge(s["x_in"], 16 * (l + 1))
                    pe.wait_ge(s["u"], KT * (n + 1))
                    for k in range(KT):
                        ins = pe.matmul(banks(job)[0:96, 0, :], w_x[:, k, :], u[:, b, k, :],
                                        start=(k == 0), stop=(k == KT - 1))
                    ins.then_inc(s["x_sum"], 1)
                if what == "dt":
                    pe.wait_ge(s["dt_in"], 16 * (l + 1))
                    pe.wait_ge(s["x"], n + 1)
                    for i in range(2):
                        m = 2 * half + i
                        pe.matmul(banks(job)[:, i, :], w_dt[:, m * P:(m + 1) * P], xd[0:RANK, :],
                                  start=True, stop=True).then_inc(s["dt_sum"], 1)
                if what == "rows":
                    g, part = n // NC, n % NC
                    pe.wait_ge(s["sel_in"], 16)
                    pe.wait_ge(s["bc3"], g + 1)
                    for i in range(2):
                        j = 2 * half + i
                        row = (j // CH) * STATE + CH * part + j % CH
                        ins = pe.matmul(banks(job)[:, i, :], select[:, row, :], bc3[:, g % 2, :],
                                        start=True, stop=True)
                    ins.then_inc(s["bc_sum"], 1)
                if what == "chunk":
                    g, part, m = n // CHUNKS, n % CHUNKS // KT, n % KT
                    if g and part == 0:
                        pe.wait_ge(s["y_free"], KT * (g - 1) + m + 1)
                    pe.wait_ge(s["weighted"], n + 1)
                    for j in range(CH):
                        ins = pe.matmul(ps[:, m, :], mem.ident, work[:, n % 2, j, :],
                                        start=(part == 0 and j == 0), stop=(part == NC - 1 and j == CH - 1))
                    ins.then_inc(s["reduced"], 1)
                if what == "out":
                    pe.wait_ge(s["out_in"], 16 * (l + 1))
                    pe.wait_ge(s["y"], KT * (n + 1))
                    for t in range(TILES):
                        for k in range(KT):
                            ins = pe.matmul(banks(job)[:, t // 2, (t % 2) * D:(t % 2 + 1) * D],
                                            du[:, b, k, t * P:(t + 1) * P], w_out[:, k, :],
                                            start=(k == 0), stop=(k == KT - 1))
                        if t % 2:
                            ins.then_inc(s["o_sum"], 1)
    end_block(nc, mem)


def mixture_of_depths(nc, ctx, mem, dram):
    s = named(mem, """small_in w1_in w2_in squares rstd first stats rstd2 z turned hT
        score spread_in score_sum minus expo weight x_added a_sum a f_sum biased done stored v_own p_own""")
    M = FFN // P
    a = mem.fresh()
    w1, w2 = a.take(DT, FFN), a.take(M, D)
    b1 = a.take(M)
    rows = a.take(3, D)
    squares, rstd = a.take(GROUPS, TILES), a.take(GROUPS, TILES)
    stats, mv = a.take(GROUPS, TILES, 6), a.take(GROUPS, TILES, 2)
    first, z, hT = a.take(GROUPS, TILES, D), a.take(GROUPS, TILES, D), a.take(GROUPS, DT, GROUP)
    score = a.take(GROUPS, TILES)
    each, seen, tmp, tied = (a.take(GROUPS, TILES, T) for _ in range(4))
    mine, rank, expo, weight = (a.take(GROUPS, TILES) for _ in range(4))
    hidden = a.take(GROUPS, M, GROUP)
    biased = a.take(GROUPS, TILES, D)
    ps, res, h = mem.ps, mem.res, mem.h

    def tiles_of(x, g):
        return x[:, TILES * g:TILES * (g + 1), :]

    with nc.Block() as block:
        @block.sync
        def _(sp):
            sp.dma_start(rows, dram["mod_rows"]).then_inc(s["small_in"], 16)
            sp.dma_start(b1, dram["mod_b1"]).then_inc(s["small_in"], 16)
            sp.dma_start(w1, dram["mod_w1"]).then_inc(s["w1_in"], 16)
            sp.dma_start(w2, dram["mod_w2"]).then_inc(s["w2_in"], 16)
            for g in range(GROUPS):
                sp.wait_ge(s["done"], TILES * (g + 1))
                out = dram["out"][g * GROUP:(g + 1) * GROUP, :].rearrange("(t p) d -> p t d", p=P)
                sp.dma_start(out, tiles_of(res, g)).then_inc(s["stored"], 16)
            sp.wait_ge(s["stored"], 16 * GROUPS)

        @block.gpsimd
        def _(pool):
            own = Steps(pool, s["p_own"])
            for g in range(GROUPS):
                pool.wait_ge(s["squares"], TILES * (g + 1))
                own.settle()
                own.step(pool.tensor_scalar(rstd[:, g], squares[:, g], 1.0 / D, EPS, ALU.mult, ALU.add))
                own.settle()
                pool.tensor_tensor(rstd[:, g], rstd[:, g], mem.minus_half, ALU.pow).then_inc(s["rstd"], 1)
                pool.wait_ge(s["rstd"], g + 1)
            for g in range(GROUPS):
                pool.wait_ge(s["stats"], g + 1)
                norm_rstd(pool, own, mv[:, g, :, 1], rstd[:, g, :], mem.minus_half, EPS, s["rstd2"], g + 1)
            for g in range(GROUPS):
                pool.wait_ge(s["z"], TILES * (g + 1))
                pool.tensor_tensor(tiles_of(res, g), tiles_of(res, g), z[:, g], ALU.add).then_inc(s["x_added"], 1)
                pool.wait_ge(s["x_added"], g + 1)

        @block.scalar
        def _(act):
            for g in range(GROUPS):
                for t in range(TILES):
                    act.activation(z[:, g, t, :], h[:, TILES * g + t, :], ACT.Square,
                                   accum_out=squares[:, g, t:t + 1]).then_inc(s["squares"], 1)
            for g in range(GROUPS):
                for f in range(DT):
                    act.wait_ge(s["turned"], DT * g + f + 1)
                    act.activation(hT[:, g, f, :], ps[:, 4 * g + f, :], ACT.Copy).then_inc(s["hT"], 1)
            for g in range(GROUPS):
                act.wait_ge(s["minus"], g + 1)
                act.activation(expo[:, g], mine[:, g], ACT.Exp, scale=-1.0).then_inc(s["expo"], 1)
            act.wait_ge(s["small_in"], 32)
            for g in range(GROUPS):
                for m in range(M):
                    act.wait_ge(s["a_sum"], M * g + m + 1)
                    act.activation(hidden[:, g, m, :], ps[:, 4 * g + m % 4, :], ACT.Gelu_apprx_tanh,
                                   bias=b1[:, m:m + 1]).then_inc(s["a"], 1)

        @block.vector
        def _(v):
            own = Steps(v, s["v_own"])
            v.wait_ge(s["small_in"], 32)
            for g in range(GROUPS):
                v.wait_ge(s["rstd"], g + 1)
                for t in range(TILES):
                    v.scalar_tensor_tensor(first[:, g, t, :], h[:, TILES * g + t, :], rstd[:, g, t:t + 1],
                                           rows[:, 0, :], ALU.mult, ALU.mult).then_inc(s["first"], 1)
                v.wait_ge(s["first"], TILES * (g + 1))
                own.step(v.tensor_tensor(tiles_of(res, g), tiles_of(res, g), first[:, g], ALU.add))
                own.settle()
                norm_stats(v, own, tiles_of(res, g), stats[:, g], mv[:, g], s["stats"])
            for g in range(GROUPS):
                v.wait_ge(s["rstd2"], g + 1)
                norm_apply(v, tiles_of(res, g), mv[:, g], rstd[:, g], z[:, g], s["z"])
            for g in range(GROUPS):
                v.wait_ge(s["z"], TILES * (g + 1))
                for t in range(TILES):
                    own.step(v.tensor_tensor_reduce(first[:, g, t, :], z[:, g, t, :], rows[:, 1, :], 1.0, 0.0,
                                                    ALU.mult, ALU.add, score[:, g, t:t + 1]))
                own.settle()
                v.tensor_tensor(each[:, g], spread(mem.slot, 1, TILES), spread(score[:, g], 2, T),
                                ALU.mult).then_inc(s["spread_in"], 1)
            for g in range(GROUPS):
                v.wait_ge(s["score_sum"], g + 1)
                own.step(v.tensor_copy(seen[:, g], ps[:, 4 * g + 2, 0:TILES * T].rearrange("p (t j) -> p t j", j=T)))
                own.settle()
                own.step(v.tensor_tensor(tmp[:, g], seen[:, g], spread(mem.slot, 1, TILES), ALU.mult))
                own.settle()
                v.tensor_reduce(mine[:, g], tmp[:, g], AX, ALU.add).then_inc(s["minus"], 1)
                v.wait_ge(s["minus"], g + 1)
                own.step(v.tensor_tensor(tied[:, g], seen[:, g], spread(mine[:, g], 2, T), ALU.is_equal))
                own.step(v.tensor_tensor(tmp[:, g], seen[:, g], spread(mine[:, g], 2, T), ALU.is_gt))
                own.settle()
                own.step(v.tensor_tensor(tied[:, g], tied[:, g], spread(mem.before, 1, TILES), ALU.mult))
                own.settle()
                own.step(v.tensor_tensor(tmp[:, g], tmp[:, g], tied[:, g], ALU.add))
                own.settle()
                own.step(v.tensor_reduce(rank[:, g], tmp[:, g], AX, ALU.add))
                v.wait_ge(s["expo"], g + 1)
                own.step(v.tensor_scalar(weight[:, g], expo[:, g], 1.0, None, ALU.add))
                own.settle()
                own.step(v.reciprocal(weight[:, g], weight[:, g]))
                own.step(v.tensor_scalar(rank[:, g], rank[:, g], TOP - 0.5, None, ALU.is_lt))
                own.settle()
                v.tensor_tensor(weight[:, g], weight[:, g], rank[:, g], ALU.mult).then_inc(s["weight"], 1)
            for g in range(GROUPS):
                v.wait_ge(s["weight"], g + 1)
                v.wait_ge(s["x_added"], g + 1)
                for b in range(2):
                    v.wait_ge(s["f_sum"], 2 * g + b + 1)
                    v.tensor_tensor(biased[:, g, 2 * b:2 * b + 2, :],
                                    ps[:, 4 * g + b, :].rearrange("p (t d) -> p t d", t=2),
                                    spread(rows[:, 2, :], 1, 2), ALU.add).then_inc(s["biased"], 1)
                    v.wait_ge(s["biased"], 2 * g + b + 1)
                    for t in (2 * b, 2 * b + 1):
                        tile = res[:, TILES * g + t, :]
                        v.scalar_tensor_tensor(tile, biased[:, g, t, :], weight[:, g, t:t + 1], tile,
                                               ALU.mult, ALU.add).then_inc(s["done"], 1)

        @block.tensor
        def _(pe):
            for g in range(GROUPS):
                pe.wait_ge(s["z"], TILES * (g + 1))
                turn_tiles(pe, z[:, g], mem.ident, ps[:, 4 * g:4 * g + 2, :], s["turned"])
            for g in range(GROUPS):
                pe.wait_ge(s["spread_in"], g + 1)
                pe.matmul(ps[:, 4 * g + 2, 0:TILES * T], mem.seq_block,
                          each[:, g].rearrange("p t j -> p (t j)"), start=True, stop=True).then_inc(s["score_sum"], 1)
            pe.wait_ge(s["w1_in"], 16)
            for g in range(GROUPS):
                pe.wait_ge(s["hT"], DT * (g + 1))
                pe.wait_ge(s["minus"], g + 1)
                for m in range(M):
                    if m >= 4:
                        pe.wait_ge(s["a"], M * g + m - 3)
                    for k in range(DT):
                        ins = pe.matmul(ps[:, 4 * g + m % 4, :], w1[:, k, m * P:(m + 1) * P], hT[:, g, k, :],
                                        start=(k == 0), stop=(k == DT - 1))
                    ins.then_inc(s["a_sum"], 1)
            pe.wait_ge(s["w2_in"], 16)
            for g in range(GROUPS):
                pe.wait_ge(s["a"], M * (g + 1))
                for t in range(TILES):
                    for k in range(M):
                        ins = pe.matmul(ps[:, 4 * g + t // 2, (t % 2) * D:(t % 2 + 1) * D],
                                        hidden[:, g, k, t * P:(t + 1) * P], w2[:, k, :],
                                        start=(k == 0), stop=(k == M - 1))
                    if t % 2:
                        ins.then_inc(s["f_sum"], 1)


BLOCKS = [token_mlp, attention_layers, latent_attention_and_ffn, mamba_layers, mixture_of_depths]


def audio_tower(nc, dram):
    with ExitStack() as ctx:
        size = 53200
        tensor = ctx.enter_context(nc.sbuf_tensor("arena", [P, size], F32))
        ps = ctx.enter_context(nc.psum_tensor("banks", [P, 8, 512], F32))
        a = Arena(tensor, size)
        consts = a.take(CONSTS)
        mem = Memory()
        mem.ps, mem.consts = ps, consts
        mem.res = a.take(GROUPS * TILES, D)
        mem.h = a.take(GROUPS * TILES, D)
        at = 0
        parts = []
        for n in CONST_PARTS:
            parts.append(consts[:, at:at + n])
            at += n
        mem.ident, mem.same_seq, mem.causal, mem.parity, mem.minus_half, mem.seq_block, mem.slot, mem.before = parts
        start = a.at

        def fresh():
            b = Arena(tensor, size)
            b.at = start
            return b

        mem.fresh = fresh
        mem.pool = [ctx.enter_context(nc.semaphore(f"count{n}")) for n in range(SEMAPHORES)]
        mem.numbers = range(mem.pool[0].num, mem.pool[-1].num + 1)
        assert len(mem.numbers) == SEMAPHORES
        for block in BLOCKS:
            block(nc, ctx, mem, dram)


CONST_PARTS = [P, 32, 32, 2, TILES, P, T, T]
CONSTS = sum(CONST_PARTS)


def constants(np):
    p = np.arange(P)[:, None]
    k = np.arange(32)[None, :]
    same = (p % 32) // T == k // T
    causal = same & (k % T <= p % T)
    far = np.float32(-1e30)
    step = np.arange(T)[None, :]
    parts = [
        np.eye(P),
        np.where(same, 0, far),
        np.where(causal, 0, far),
        (p // MLA_HS) % 2 == np.arange(2)[None, :],
        np.full((P, TILES), -0.5),
        p // T == np.arange(P)[None, :] // T,
        p % T == step,
        step < p % T,
    ]
    return np.concatenate([np.asarray(x, np.float32) for x in parts], axis=1)


def by_rows(np, w):
    K, M = w.shape
    return w.reshape(K // P, P, M).transpose(1, 0, 2)


def by_partition(np, b):
    return b.reshape(-1, P).T


def every_token(np, b):
    return np.broadcast_to(b, (P, *b.shape))


def laid_out(np, i):
    x = np.pad(i["x"], ((0, 0), (0, T * MLP_IN // 128 - i["x"].shape[1]), (0, 0)))
    x = x.reshape(TOKENS, MLP_IN)
    a = {"consts": constants(np)}
    a["tok_x"] = by_rows(np, x.T)
    a["tok_w1"] = by_rows(np, i["L0_tok_w1"].T)
    a["tok_w2"] = by_rows(np, i["L0_tok_w2"].T)
    a["tok_b1"] = by_partition(np, i["L0_tok_b1"])
    a["tok_b2"] = every_token(np, i["L0_tok_b2"])
    e = {n[7:]: v for n, v in i.items() if n.startswith("L0_tok_")}
    layers = range(LAYERS)
    a["enc_wqkv"] = np.stack([by_rows(np, np.concatenate([e["wq"][l], e["wk"][l], e["wv"][l]]).T) for l in layers])
    a["enc_wo"] = np.stack([by_rows(np, e["wo"][l].T) for l in layers])
    a["enc_ff1"] = np.stack([by_rows(np, e["ffw1"][l].T) for l in layers])
    a["enc_ff2"] = np.stack([np.concatenate([e["ffw2"][l].T, e["ffb2"][l][None]]) for l in layers])
    a["enc_rows"] = np.stack([every_token(np, np.stack([e["bv"][l], e["bo"][l]])) for l in layers])
    a["enc_cols"] = np.stack([np.concatenate(
        [by_partition(np, e[n][l]) for n in ("ln1_s", "ln1_b", "bq", "bk", "ln2_s", "ln2_b")]
        + [np.pad(e["ffb1"][l], (0, P - TOK_FF))[:, None], np.zeros((P, 3), np.float32)], axis=1) for l in layers])
    m = {n[8:]: v for n, v in i.items() if n.startswith("L0_attn_")}

    def side(w):
        return by_rows(np, w).reshape(P, -1)

    a["mla"] = np.concatenate([side(m["W_dq"].T), m["W_dq"], m["W_uq"].T, side(m["W_uk"]), side(m["W_dkv"].T),
                               side(m["W_uv"]), side(m["W_o"].T)], axis=1)
    a["ffn_w1"] = by_rows(np, i["L0_ffn_w1"].T)
    a["ffn_w2"] = by_rows(np, i["L0_ffn_w2"].T)
    a["ffn_b1"] = by_partition(np, i["L0_ffn_b1"])
    a["ffn_b2"] = every_token(np, i["L0_ffn_b2"])
    q = {n[8:]: v for n, v in i.items() if n.startswith("L1_attn_")}
    a["mam_in"] = np.stack([by_rows(np, q["in_proj_w"][l].T) for l in layers])
    a["mam_x"] = np.stack([by_rows(np, q["x_proj_w"][l].T) for l in layers])
    a["mam_dt"] = np.stack([q["dt_proj_w"][l].T for l in layers])
    a["mam_out"] = np.stack([by_rows(np, q["out_proj_w"][l].T) for l in layers])
    a["mam_bo"] = np.stack([every_token(np, q["out_proj_b"][l]) for l in layers])
    a["mam_alog"] = np.stack([by_rows(np, q["A_log"][l]) for l in layers])
    a["mam_cols"] = np.stack([np.concatenate(
        [by_partition(np, q[n][l]) for n in ("in_proj_b", "conv_b", "dt_proj_b", "D", "norm_w")]
        + [np.zeros((P, 2), np.float32), by_rows(np, q["conv_w"][l][:, 0, :]).reshape(P, -1),
           np.zeros((P, 4), np.float32)], axis=1) for l in layers])
    a["select"] = np.broadcast_to((np.arange(96)[:, None] % 32 == np.arange(32)[None, :])[:, :, None],
                                  (96, 32, P)).astype(mybir.dt.np(BF16))
    f = {n[7:]: v for n, v in i.items() if n.startswith("L1_ffn_")}
    a["mod_rows"] = every_token(np, np.stack([q["norm_f_w"], f["w_router"], f["b2"]]))
    a["mod_b1"] = by_partition(np, f["b1"])
    a["mod_w1"] = by_rows(np, f["W1"])
    a["mod_w2"] = by_rows(np, f["W2"])
    return a


def kernel(**inputs):
    import numpy as np
    import concourse.bacc as bacc
    from concourse.bass_utils import run_bass_kernel_spmd

    arrays = {n: np.ascontiguousarray(v) for n, v in laid_out(np, {n: np.asarray(v) for n, v in inputs.items()}).items()}
    nc = bacc.Bacc("TRN2", target_bir_lowering=False, num_devices=1)
    handles = {n: nc.dram_tensor(n, v.shape, mybir.dt.from_np(v.dtype), kind="ExternalInput").ap()
               for n, v in arrays.items()}
    handles["out"] = nc.dram_tensor("out", (TOKENS, D), F32, kind="ExternalOutput").ap()
    audio_tower(nc, handles)
    got = run_bass_kernel_spmd(nc, [arrays], core_ids=[0])
    return got.results[0]["out"].reshape(SEQS, T, D)
```

```python
from contextlib import ExitStack

import concourse.bass as bass
from concourse import mybir

F32 = mybir.dt.float32
BF16 = mybir.dt.bfloat16
ALU = mybir.AluOpType
ACT = mybir.ActivationFunctionType
AX = mybir.AxisListType.X
RMAX = bass.bass_isa.ReduceOp.max

P = 128
SEQS, T, D = 64, 16, 256
TOKENS = SEQS * T
GROUP = 512
GROUPS = TOKENS // GROUP
TILES = GROUP // P
DT = D // P
EPS = 1e-5
TOK_EPS = 1e-12
LAYERS = 2
MLP_IN, MLP_HID = 1024, 512
TOK_HEADS, TOK_DK = 8, 32
TOK_FF = D // 4
MLA_HEADS, MLA_HS, LATENT = 16, 16, 128
FFN = 1024
SEMAPHORES = 72
ROUND = 12582912.0
INNER, STATE, RANK, CONV = 512, 16, 64, 5
KT = INNER // P
CH, NC = 4, STATE // 4
CHUNKS = NC * KT
TOP = 8


class Memory:
    pass


class Steps:

    def __init__(self, eng, sem):
        self.eng, self.sem, self.n = eng, sem, 0

    def step(self, ins):
        ins.then_inc(self.sem, 1)
        self.n += 1
        return self.n

    def settle(self):
        if self.n:
            self.eng.wait_ge(self.sem, self.n)


def named(mem, names):
    names = names.split()
    return dict(zip(names, mem.pool[:len(names)], strict=True))


def end_block(nc, mem):
    nc.gpsimd.sem_clear(mem.numbers)
    nc.all_engine_barrier()


class Arena:

    def __init__(self, tensor, size):
        self.tensor, self.size, self.at = tensor, size, 0

    def take(self, *shape, dtype=F32, rows=P):
        n = 1
        for x in shape:
            n *= x
        words = n if dtype == F32 else (n + 1) // 2
        view = self.tensor[0:rows, self.at:self.at + words]
        self.at += words
        assert self.at <= self.size, (self.at, self.size)
        if dtype != F32:
            view = view.bitcast(dtype)
        if len(shape) > 1:
            names = " ".join(f"d{i}" for i in range(len(shape)))
            sizes = {f"d{i}": x for i, x in enumerate(shape) if i}
            view = view.rearrange(f"p ({names}) -> p {names}", **sizes)
        return view


def spread(ap, axis, n):
    shape = list(ap.shape)
    shape.insert(axis, n)
    return ap.unsqueeze(axis).broadcast_to(shape)


def norm_stats(v, own, src, stats, mv, stats_ready):
    for t in range(TILES):
        own.step(v.bn_stats(stats[:, t, :], src[:, t, :]))
    own.settle()
    for t in range(TILES):
        ins = v.bn_aggr(mv[:, t, :], stats[:, t, :])
        if t < TILES - 1:
            own.step(ins)
    own.settle()
    ins.then_inc(stats_ready, 1)


def norm_rstd(pool, own, var, rstd, minus_half, eps, rstd_ready, n):
    own.settle()
    own.step(pool.tensor_scalar(rstd, var, 1.0, eps, ALU.mult, ALU.add))
    own.settle()
    pool.tensor_tensor(rstd, rstd, minus_half, ALU.pow).then_inc(rstd_ready, 1)
    pool.wait_ge(rstd_ready, n)


def norm_apply(v, src, mv, rstd, z, z_ready):
    for t in range(TILES):
        v.tensor_scalar(z[:, t, :], src[:, t, :], mv[:, t, 0:1], rstd[:, t:t + 1],
                        ALU.subtract, ALU.mult).then_inc(z_ready, 1)


def turn_tiles(pe, z, ident, banks, turned):
    for f in range(DT):
        for t in range(TILES):
            ins = pe.transpose(banks[:, f, t * P:(t + 1) * P], z[:, t, f * P:(f + 1) * P], ident)
        ins.then_inc(turned, 1)


def token_mlp(nc, ctx, mem, dram):
    s = named(mem, " ".join(f"slice{k}" for k in range(8)) +
                      " small hid_sum hid_ready out_sum out_ready")
    slices = [s["slice0"], s["slice1"], s["slice2"], s["slice3"], s["slice4"], s["slice5"], s["slice6"], s["slice7"]]
    KT, HT = MLP_IN // P, MLP_HID // P
    a = mem.fresh()
    w1 = a.take(KT, MLP_HID)
    x = a.take(KT, TOKENS)
    w2 = a.take(HT, D)
    b1 = a.take(HT)
    b2 = a.take(D)
    hid = a.take(GROUPS, HT, GROUP)
    ps, res = mem.ps, mem.res

    with nc.Block() as block:
        @block.sync
        def _(sp):
            for k in range(KT):
                sp.dma_start(w1[:, k, :], dram["tok_w1"][:, k, :]).then_inc(slices[k], 16)
                sp.dma_start(x[:, k, :], dram["tok_x"][:, k, :]).then_inc(slices[k], 16)

        @block.scalar
        def _(act):
            act.dma_start(mem.consts, dram["consts"]).then_inc(s["small"], 16)
            act.dma_start(b1, dram["tok_b1"]).then_inc(s["small"], 16)
            act.dma_start(b2, dram["tok_b2"]).then_inc(s["small"], 16)
            act.dma_start(w2, dram["tok_w2"]).then_inc(s["small"], 16)
            act.wait_ge(s["small"], 64)
            for g in range(GROUPS):
                for m in range(HT):
                    act.wait_ge(s["hid_sum"], g * HT + m + 1)
                    act.activation(hid[:, g, m, :], ps[:, 4 * g + m, :], ACT.Relu,
                                   bias=b1[:, m:m + 1]).then_inc(s["hid_ready"], 1)

        @block.tensor
        def _(pe):
            for k in range(KT):
                pe.wait_ge(slices[k], 32)
                for g in range(GROUPS):
                    for m in range(HT):
                        ins = pe.matmul(ps[:, 4 * g + m, :], w1[:, k, m * P:(m + 1) * P],
                                        x[:, k, g * GROUP:(g + 1) * GROUP],
                                        start=(k == 0), stop=(k == KT - 1))
                        if k == KT - 1:
                            ins.then_inc(s["hid_sum"], 1)
            pe.wait_ge(s["small"], 64)
            for g in range(GROUPS):
                pe.wait_ge(s["hid_ready"], (g + 1) * HT)
                for t in range(TILES):
                    for k in range(HT):
                        ins = pe.matmul(ps[:, 4 * g + t // 2, (t % 2) * D:(t % 2 + 1) * D],
                                        hid[:, g, k, t * P:(t + 1) * P], w2[:, k, :],
                                        start=(k == 0), stop=(k == HT - 1))
                    if t % 2:
                        ins.then_inc(s["out_sum"], 1)

        @block.vector
        def _(v):
            v.wait_ge(s["small"], 64)
            for g in range(GROUPS):
                for h in range(2):
                    v.wait_ge(s["out_sum"], 2 * g + h + 1)
                    t = TILES * g + 2 * h
                    v.tensor_tensor(res[:, t:t + 2, :],
                                    ps[:, 4 * g + h, :].rearrange("p (t d) -> p t d", t=2),
                                    spread(b2, 1, 2), ALU.add).then_inc(s["out_ready"], 1)
    end_block(nc, mem)


def attention_layers(nc, ctx, mem, dram):
    s = named(mem, """cols_in qkv_in wo_in ff_in rows_in
        stats rstd z turned hT q_sum q k_sum k v_sum v s_sum s_ready e p o_sum o
        wo_sum bo_added res1 f_sum f f2_sum res2 v_own p_own""")
    a = mem.fresh()
    wqkv = a.take(DT, 3 * D)
    wo = a.take(DT, D)
    ff1 = a.take(DT, TOK_FF)
    ff2 = a.take(D, rows=TOK_FF + 1)
    cols = a.take(16)
    rows = a.take(2, D)
    stats, mv, rstd = a.take(GROUPS, TILES, 6), a.take(GROUPS, TILES, 2), a.take(GROUPS, TILES)
    z, hT = a.take(GROUPS, TILES, D), a.take(GROUPS, DT, GROUP)
    qT, kT = a.take(GROUPS, DT, GROUP), a.take(GROUPS, DT, GROUP)
    val = a.take(GROUPS, TILES, D)
    sc, pT = a.take(GROUPS, 4, 8 * 32), a.take(GROUPS, 4, 8 * 32)
    small = a.take(GROUPS, 2, 32)
    oT = a.take(GROUPS, DT, GROUP)
    fT = a.take(GROUPS, GROUP, rows=TOK_FF + 1)
    ps, res = mem.ps, mem.res
    SCALE = TOK_DK ** -0.5

    def tiles_of(g):
        return res[:, TILES * g:TILES * (g + 1), :]

    def two_tiles(g, b):
        return ps[:, 4 * g + b, :].rearrange("p (t d) -> p t d", t=2)

    with nc.Fori(0, LAYERS) as layer:
        with nc.Block() as block:
            @block.sync
            def _(sp):
                sp.dma_start(cols, dram["enc_cols"][layer, :, :]).then_inc(s["cols_in"], 16)
                sp.dma_start(wqkv, dram["enc_wqkv"][layer, :, :, :]).then_inc(s["qkv_in"], 16)
                sp.dma_start(rows, dram["enc_rows"][layer, :, :, :]).then_inc(s["rows_in"], 16)
                sp.dma_start(wo, dram["enc_wo"][layer, :, :, :]).then_inc(s["wo_in"], 16)
                sp.dma_start(ff1, dram["enc_ff1"][layer, :, :, :]).then_inc(s["ff_in"], 16)
                sp.dma_start(ff2, dram["enc_ff2"][layer, :, :]).then_inc(s["ff_in"], 16)

            @block.gpsimd
            def _(pool):
                own = Steps(pool, s["p_own"])
                own.step(pool.memset(fT[TOK_FF:TOK_FF + 1, :, :], 1.0))
                for j in range(2):
                    for g in range(GROUPS):
                        pool.wait_ge(s["stats"], 2 * j + g + 1)
                        norm_rstd(pool, own, mv[:, g, :, 1], rstd[:, g, :], mem.minus_half,
                                  TOK_EPS, s["rstd"], 2 * j + g + 1)
                    if j == 0:
                        pool.wait_ge(s["rows_in"], 16)
                        for g in range(GROUPS):
                            pool.wait_ge(s["z"], TILES * (g + 1))
                            pool.tensor_tensor(tiles_of(g), tiles_of(g), spread(rows[:, 1, :], 1, TILES),
                                               ALU.add).then_inc(s["bo_added"], 1)
                            pool.wait_ge(s["bo_added"], g + 1)

            @block.vector
            def _(v):
                own = Steps(v, s["v_own"])

                def statistics(g):
                    norm_stats(v, own, tiles_of(g), stats[:, g], mv[:, g], s["stats"])

                def apply(j):
                    for g in range(GROUPS):
                        v.wait_ge(s["rstd"], 2 * j + g + 1)
                        norm_apply(v, tiles_of(g), mv[:, g], rstd[:, g], z[:, g], s["z"])

                for g in range(GROUPS):
                    statistics(g)
                apply(0)
                v.wait_ge(s["cols_in"], 16)
                for g in range(GROUPS):
                    for m in range(DT):
                        v.wait_ge(s["k_sum"], DT * g + m + 1)
                        v.tensor_scalar(kT[:, g, m, :], ps[:, 4 * g + m, :], cols[:, 6 + m:7 + m], None,
                                        ALU.add).then_inc(s["k"], 1)
                v.wait_ge(s["rows_in"], 16)
                for g in range(GROUPS):
                    for b in range(2):
                        v.wait_ge(s["v_sum"], 2 * g + b + 1)
                        v.tensor_tensor(val[:, g, 2 * b:2 * b + 2, :], two_tiles(g, 2 + b),
                                        spread(rows[:, 0, :], 1, 2), ALU.add).then_inc(s["v"], 1)
                for g in range(GROUPS):
                    v.wait_ge(s["s_sum"], g + 1)
                    rows32 = sc[:, g].rearrange("p r (j k) -> p (r j) k", k=32)
                    own.step(v.tensor_tensor(
                        sc[:, g].rearrange("p r (j k) -> p r j k", k=32),
                        ps[:, 4 * g:4 * g + 4, 0:256].rearrange("p r (j k) -> p r j k", k=32),
                        spread(spread(mem.same_seq, 1, 8), 1, 4), ALU.add))
                    own.settle()
                    own.step(v.tensor_reduce(small[:, g, 0, :], rows32, AX, ALU.max))
                    own.settle()
                    v.tensor_tensor(rows32, rows32, spread(small[:, g, 0, :], 2, 32),
                                    ALU.subtract).then_inc(s["s_ready"], 1)
                    v.wait_ge(s["e"], g + 1)
                    own.step(v.tensor_reduce(small[:, g, 1, :], rows32, AX, ALU.add))
                    own.settle()
                    own.step(v.reciprocal(small[:, g, 0, :], small[:, g, 1, :]))
                    own.settle()
                    own.step(v.tensor_tensor(rows32, rows32, spread(small[:, g, 0, :], 2, 32), ALU.mult))
                    own.settle()
                    v.transpose(pT[:, g].rearrange("p r c -> p (r c)"),
                                sc[:, g].rearrange("p r c -> p (r c)")).then_inc(s["p"], 1)
                for g in range(GROUPS):
                    v.wait_ge(s["bo_added"], g + 1)
                    for b in range(2):
                        v.wait_ge(s["wo_sum"], 2 * g + b + 1)
                        two = res[:, TILES * g + 2 * b:TILES * g + 2 * b + 2, :]
                        v.tensor_tensor(two, two, two_tiles(g, b), ALU.add).then_inc(s["res1"], 1)
                    v.wait_ge(s["res1"], 2 * (g + 1))
                    statistics(g)
                apply(1)
                for g in range(GROUPS):
                    for b in range(2):
                        v.wait_ge(s["f2_sum"], 2 * g + b + 1)
                        two = res[:, TILES * g + 2 * b:TILES * g + 2 * b + 2, :]
                        v.tensor_tensor(two, two, two_tiles(g, 2 + b), ALU.add).then_inc(s["res2"], 1)

            @block.scalar
            def _(act):
                act.wait_ge(s["cols_in"], 16)

                def turned(j, base):
                    for g in range(GROUPS):
                        for f in range(DT):
                            act.wait_ge(s["turned"], GROUPS * DT * j + DT * g + f + 1)
                            act.activation(hT[:, g, f, :], ps[:, 4 * g + 2 * j + f, :], ACT.Identity,
                                           bias=cols[:, base + 2 + f:base + 3 + f],
                                           scale=cols[:, base + f:base + f + 1]).then_inc(s["hT"], 1)

                turned(0, 0)
                for g in range(GROUPS):
                    for m in range(DT):
                        act.wait_ge(s["q_sum"], DT * g + m + 1)
                        act.activation(qT[:, g, m, :], ps[:, 4 * g + 2 + m, :], ACT.Identity,
                                       bias=cols[:, 4 + m:5 + m]).then_inc(s["q"], 1)
                for g in range(GROUPS):
                    act.wait_ge(s["s_ready"], g + 1)
                    both = sc[:, g].rearrange("p r c -> p (r c)")
                    act.activation(both, both, ACT.Exp, scale=SCALE).then_inc(s["e"], 1)
                for g in range(GROUPS):
                    act.wait_ge(s["o_sum"], g + 1)
                    for hh in range(2):
                        act.activation(
                            oT[:, g, hh, :].rearrange("p (t i q) -> p i t q", t=TILES, i=4),
                            ps[:, 4 * g:4 * g + 4, hh * P:(hh + 1) * P].rearrange("p i (t q) -> p i t q", q=32),
                            ACT.Copy).then_inc(s["o"], 1)
                turned(1, 8)
                for g in range(GROUPS):
                    act.wait_ge(s["f_sum"], g + 1)
                    act.activation(fT[0:TOK_FF, g, :], ps[0:TOK_FF, 4 * g, :], ACT.Relu,
                                   bias=cols[0:TOK_FF, 12:13]).then_inc(s["f"], 1)

            @block.tensor
            def _(pe):
                def turn(j):
                    for g in range(GROUPS):
                        if j == 1:
                            pe.wait_ge(s["o"], 2 * (g + 1))
                        pe.wait_ge(s["z"], GROUPS * TILES * j + TILES * (g + 1))
                        turn_tiles(pe, z[:, g], mem.ident, ps[:, 4 * g + 2 * j:4 * g + 2 * j + 2, :], s["turned"])

                def columns(g, bank, w, at, done):
                    for m in range(DT):
                        for k in range(DT):
                            ins = pe.matmul(ps[:, bank + m, :], w[:, k, at + m * P:at + (m + 1) * P],
                                            hT[:, g, k, :], start=(k == 0), stop=(k == DT - 1))
                        ins.then_inc(done, 1)

                def tokens(bank, src, w, done, K=DT):
                    for t in range(TILES):
                        for k in range(K):
                            ins = pe.matmul(ps[:, bank + t // 2, (t % 2) * D:(t % 2 + 1) * D],
                                            src(k)[:, t * P:(t + 1) * P], w(k),
                                            start=(k == 0), stop=(k == K - 1))
                        if t % 2:
                            ins.then_inc(done, 1)

                turn(0)
                pe.wait_ge(s["qkv_in"], 16)
                for g in range(GROUPS):
                    pe.wait_ge(s["hT"], DT * (g + 1))
                    columns(g, 4 * g + 2, wqkv, 0, s["q_sum"])
                    columns(g, 4 * g, wqkv, D, s["k_sum"])
                for g in range(GROUPS):
                    pe.wait_ge(s["q"], DT * (g + 1))
                    tokens(4 * g + 2, lambda k: hT[:, g, k, :], lambda k: wqkv[:, k, 2 * D:3 * D], s["v_sum"])
                for g in range(GROUPS):
                    pe.wait_ge(s["k"], DT * (g + 1))
                    pe.wait_ge(s["v"], 2 * (g + 1))
                    for t in range(TILES):
                        for hh in range(2):
                            for i in range(4):
                                for r in range(4):
                                    at = slice(t * P + 32 * i, t * P + 32 * i + 32)
                                    ins = pe.matmul(ps[32 * i:32 * i + 32, 4 * g + r, (2 * t + hh) * 32:(2 * t + hh + 1) * 32],
                                                    qT[32 * r:32 * r + 32, g, hh, at],
                                                    kT[32 * r:32 * r + 32, g, hh, at],
                                                    start=True, stop=True)
                    ins.then_inc(s["s_sum"], 1)
                for g in range(GROUPS):
                    pe.wait_ge(s["p"], g + 1)
                    for hh in range(2):
                        for t in range(TILES):
                            for r in range(4):
                                for i in range(4):
                                    rows_i = slice(32 * i, 32 * i + 32)
                                    ins = pe.matmul(ps[32 * r:32 * r + 32, 4 * g + i, hh * P + t * 32:hh * P + (t + 1) * 32],
                                                    val[rows_i, g, t, (4 * hh + r) * 32:(4 * hh + r + 1) * 32],
                                                    pT[rows_i, g, r, (2 * t + hh) * 32:(2 * t + hh + 1) * 32],
                                                    start=True, stop=True)
                    ins.then_inc(s["o_sum"], 1)
                pe.wait_ge(s["wo_in"], 16)
                for g in range(GROUPS):
                    pe.wait_ge(s["o"], 2 * (g + 1))
                    tokens(4 * g, lambda k: oT[:, g, k, :], lambda k: wo[:, k, :], s["wo_sum"])
                turn(1)
                pe.wait_ge(s["ff_in"], 32)
                for g in range(GROUPS):
                    pe.wait_ge(s["res1"], 2 * (g + 1))
                    pe.wait_ge(s["hT"], DT * GROUPS + DT * (g + 1))
                    for k in range(DT):
                        ins = pe.matmul(ps[0:TOK_FF, 4 * g, :], ff1[:, k, :], hT[:, g, k, :],
                                        start=(k == 0), stop=(k == DT - 1))
                    ins.then_inc(s["f_sum"], 1)
                pe.wait_ge(s["p_own"], 1)
                for g in range(GROUPS):
                    pe.wait_ge(s["f"], g + 1)
                    tokens(4 * g + 2, lambda k: fT[:, g, :], lambda k: ff2, s["f2_sum"], K=1)
        end_block(nc, mem)


def absolute_max(v, own, out, src):
    own.step(v.tensor_reduce(out, src, AX, ALU.max, apply_absolute_value=True))


def quantiser(v, own, most, scale, inverse):
    own.step(v.tensor_scalar(scale, most, 1e-6, 1.0 / 127.0, ALU.max, ALU.mult))
    own.settle()
    own.step(v.reciprocal(inverse, scale))
    own.settle()


def quantise(v, own, src, inverse, shifted, out, done):
    own.step(v.tensor_scalar(shifted, src, inverse, ROUND, ALU.mult, ALU.add))
    own.settle()
    v.tensor_scalar(out, shifted, -ROUND, None, ALU.add).then_inc(done, 1)


def latent_attention_and_ffn(nc, ctx, mem, dram):
    s = named(mem, """mla_in ffn_in stats rstd z turned hT
        m1_sum m1 keff_sum keff veff_sum veff d_sum d c_sum c q_sum q k_sum k v_sum v
        s_sum masked s_ready e p o_sum res1 w_most w_all w1_q w2_q x_most x_all x_q x_scale
        a_sum a a_most a_all a_q a_scale b2_added f_sum res2 v_own p_own""")
    a = mem.fresh()
    w = a.take(2048)
    dq = w[:, 0:256].rearrange("p (f n) -> p f n", f=DT)
    dq_rows = w[:, 256:512]
    uq = w[:, 512:768]
    uk = w[:, 768:1024].rearrange("p (f n) -> p f n", f=DT)
    dkv = w[:, 1024:1280].rearrange("p (f n) -> p f n", f=DT)
    uv = w[:, 1280:1536].rearrange("p (f n) -> p f n", f=DT)
    wo = w[:, 1536:2048].rearrange("p (f n) -> p f n", f=DT)
    m1, keff, veff = a.take(DT, D), a.take(D), a.take(D)
    stats, mv, rstd = a.take(GROUPS, TILES, 6), a.take(GROUPS, TILES, 2), a.take(GROUPS, TILES)
    z, hT = a.take(GROUPS, TILES, D), a.take(GROUPS, DT, GROUP)
    dT, cT = a.take(GROUPS, GROUP), a.take(GROUPS, GROUP)
    qT = a.take(GROUPS, DT, GROUP)
    kT = a.take(GROUPS, 2, DT, GROUP)
    val = a.take(GROUPS, TILES, D)
    PAIRS = [(g, half) for half in range(2) for g in range(GROUPS)]
    sc, pT = a.take(GROUPS, 2, 4, 256), a.take(GROUPS, 2, 4, 256)
    small = a.take(GROUPS, 2, 2, 32)
    w1, w2 = a.take(DT, FFN), a.take(FFN // P, D)
    w1q, w2q = a.take(DT, FFN, dtype=BF16), a.take(FFN // P, D, dtype=BF16)
    b1, b1s, b2 = a.take(FFN // P), a.take(FFN // P), a.take(D)
    most, alls, scale, inverse = a.take(4), a.take(4), a.take(4), a.take(4)
    parts = a.take(5)
    prod = a.take(2)
    xq = a.take(GROUPS, DT, GROUP, dtype=BF16)
    shifted = a.take(2048)
    hidden = a.take(GROUPS, FFN // P, GROUP)
    hq = a.take(GROUPS, FFN // P, GROUP, dtype=BF16)
    ps, res, h = mem.ps, mem.res, mem.h
    SCALE = MLA_HS ** -0.5
    M = FFN // P

    def flat(ap):
        return ap.rearrange("p a b -> p (a b)")

    def tiles_of(g):
        return res[:, TILES * g:TILES * (g + 1), :]

    def scores(g, half):
        return ps[:, 4 * g:4 * g + 4, 256 * half:256 * (half + 1)]

    def two_tiles(g, b):
        return ps[:, 4 * g + b, :].rearrange("p (t d) -> p t d", t=2)

    with nc.Block() as block:
        @block.sync
        def _(sp):
            sp.dma_start(w, dram["mla"]).then_inc(s["mla_in"], 16)
            sp.dma_start(w1, dram["ffn_w1"]).then_inc(s["ffn_in"], 16)
            sp.dma_start(w2, dram["ffn_w2"]).then_inc(s["ffn_in"], 16)
            sp.dma_start(b1, dram["ffn_b1"]).then_inc(s["ffn_in"], 16)
            sp.dma_start(b2, dram["ffn_b2"]).then_inc(s["ffn_in"], 16)

        @block.gpsimd
        def _(pool):
            own = Steps(pool, s["p_own"])
            for g in range(GROUPS):
                pool.wait_ge(s["stats"], g + 1)
                norm_rstd(pool, own, mv[:, g, :, 1], rstd[:, g, :], mem.minus_half, EPS, s["rstd"], g + 1)
            for n in range(2):
                pool.wait_ge(s["w_most"], n + 1)
                pool.partition_all_reduce(alls[:, n:n + 1], most[:, n:n + 1], P, RMAX).then_inc(s["w_all"], 1)
                pool.wait_ge(s["w_all"], n + 1)
            for g in range(GROUPS):
                n = GROUPS + g + 1
                pool.wait_ge(s["stats"], n)
                norm_rstd(pool, own, mv[:, g, :, 1], rstd[:, g, :], mem.minus_half, EPS, s["rstd"], n)
            pool.wait_ge(s["x_most"], 1)
            pool.partition_all_reduce(alls[:, 2:3], most[:, 2:3], P, RMAX).then_inc(s["x_all"], 1)
            pool.wait_ge(s["x_all"], 1)
            pool.wait_ge(s["a_most"], 1)
            pool.partition_all_reduce(alls[:, 3:4], most[:, 3:4], P, RMAX).then_inc(s["a_all"], 1)
            pool.wait_ge(s["a_all"], 1)
            pool.wait_ge(s["a_scale"], 1)
            own.step(pool.tensor_scalar(b2, b2, prod[:, 1:2], 1.0, ALU.mult, ALU.mult))
            for g in range(GROUPS):
                own.settle()
                if g:
                    pool.wait_ge(s["b2_added"], g)
                pool.tensor_tensor(tiles_of(g), tiles_of(g), spread(b2, 1, TILES), ALU.add).then_inc(s["b2_added"], 1)
            pool.wait_ge(s["b2_added"], GROUPS)
            for g in range(GROUPS):
                n = 2 * GROUPS + g + 1
                pool.wait_ge(s["stats"], n)
                norm_rstd(pool, own, mv[:, g, :, 1], rstd[:, g, :], mem.minus_half, EPS, s["rstd"], n)

        @block.vector
        def _(v):
            own = Steps(v, s["v_own"])

            def statistics(g):
                norm_stats(v, own, tiles_of(g), stats[:, g], mv[:, g], s["stats"])

            def apply(j, out):
                for g in range(GROUPS):
                    v.wait_ge(s["rstd"], GROUPS * j + g + 1)
                    norm_apply(v, tiles_of(g), mv[:, g], rstd[:, g], out(g), s["z"])

            for g in range(GROUPS):
                statistics(g)
            apply(0, lambda g: z[:, g])
            for g in range(GROUPS):
                v.wait_ge(s["c_sum"], g + 1)
                v.tensor_copy(cT[:, g, :], ps[:, 4 * g + 3, :]).then_inc(s["c"], 1)
            for g in range(GROUPS):
                v.wait_ge(s["k_sum"], DT * (g + 1))
                for e in range(2):
                    v.tensor_scalar(kT[:, g, e, 1, :], ps[:, 4 * g + 3, :], mem.parity[:, e:e + 1], None,
                                    ALU.mult).then_inc(s["k"], 1)
            for g in range(GROUPS):
                for b in range(2):
                    v.wait_ge(s["v_sum"], 2 * g + b + 1)
                    v.tensor_copy(val[:, g, 2 * b:2 * b + 2, :], two_tiles(g, b)).then_inc(s["v"], 1)
            for n, (g, half) in enumerate(PAIRS):
                v.wait_ge(s["s_sum"], n + 1)
                most_of, sum_of = small[:, g, half, 0], small[:, g, half, 1]
                rows32 = sc[:, g, half].rearrange("p r (j k) -> p (r j) k", k=32)
                v.tensor_tensor(sc[:, g, half].rearrange("p r (j k) -> p r j k", k=32),
                                scores(g, half).rearrange("p r (j k) -> p r j k", k=32),
                                spread(spread(mem.causal, 1, 8), 1, 4), ALU.add).then_inc(s["masked"], 1)
                v.wait_ge(s["masked"], n + 1)
                own.step(v.tensor_reduce(most_of, rows32, AX, ALU.max))
                own.settle()
                v.tensor_tensor(rows32, rows32, spread(most_of, 2, 32), ALU.subtract).then_inc(s["s_ready"], 1)
                v.wait_ge(s["e"], n + 1)
                own.step(v.tensor_reduce(sum_of, rows32, AX, ALU.add))
                own.settle()
                own.step(v.reciprocal(most_of, sum_of))
                own.settle()
                own.step(v.tensor_tensor(rows32, rows32, spread(most_of, 2, 32), ALU.mult))
                own.settle()
                v.transpose(flat(pT[:, g, half]), flat(sc[:, g, half])).then_inc(s["p"], 1)
            v.wait_ge(s["ffn_in"], 64)
            for n, x in enumerate((w1, w2)):
                v.tensor_reduce(most[:, n:n + 1], flat(x), AX, ALU.max,
                                apply_absolute_value=True).then_inc(s["w_most"], 1)
            for n, (x, q, done) in enumerate(((w1, w1q, s["w1_q"]), (w2, w2q, s["w2_q"]))):
                v.wait_ge(s["w_all"], n + 1)
                quantiser(v, own, alls[:, n:n + 1], scale[:, n:n + 1], inverse[:, n:n + 1])
                if n:
                    v.wait_ge(s["w1_q"], 1)
                quantise(v, own, flat(x), inverse[:, n:n + 1], shifted, flat(q), done)
            for n, (g, half) in enumerate(PAIRS):
                v.wait_ge(s["o_sum"], n + 1)
                two = res[:, TILES * g + 2 * half:TILES * g + 2 * half + 2, :]
                v.tensor_tensor(two, two, two_tiles(g, half), ALU.add).then_inc(s["res1"], 1)
                if half == 1:
                    v.wait_ge(s["res1"], n + 1)
                    statistics(g)
            apply(1, lambda g: z[:, g])
            v.wait_ge(s["z"], 2 * GROUPS * TILES)
            absolute_max(v, own, parts[:, 0:1], z.rearrange("p g t d -> p (g t d)"))
            own.settle()
            v.tensor_copy(most[:, 2:3], parts[:, 0:1]).then_inc(s["x_most"], 1)
            v.wait_ge(s["x_all"], 1)
            quantiser(v, own, alls[:, 2:3], scale[:, 2:3], inverse[:, 2:3])
            own.step(v.tensor_tensor(prod[:, 0:1], scale[:, 0:1], scale[:, 2:3], ALU.mult))
            own.settle()
            v.tensor_scalar(b1s, b1, prod[:, 0:1], None, ALU.mult).then_inc(s["x_scale"], 1)
            for g in range(GROUPS):
                v.wait_ge(s["hT"], DT * GROUPS + DT * (g + 1))
                quantise(v, own, flat(hT[:, g]), inverse[:, 2:3], flat(hT[:, g]), flat(xq[:, g]), s["x_q"])
            for n, (g, upto, tiles) in enumerate(((0, 4, 4), (0, 8, 4), (1, 4, 4), (1, 6, 2), (1, 8, 2))):
                v.wait_ge(s["a"], M * g + upto)
                absolute_max(v, own, parts[:, n:n + 1], flat(hidden[:, g, upto - tiles:upto, :]))
            own.settle()
            v.tensor_reduce(most[:, 3:4], parts, AX, ALU.max).then_inc(s["a_most"], 1)
            v.wait_ge(s["a_all"], 1)
            quantiser(v, own, alls[:, 3:4], scale[:, 3:4], inverse[:, 3:4])
            v.tensor_tensor(prod[:, 1:2], scale[:, 1:2], scale[:, 3:4], ALU.mult).then_inc(s["a_scale"], 1)
            for g in range(GROUPS):
                for b in range(2):
                    some = slice(b * GROUP // 2, (b + 1) * GROUP // 2)
                    quantise(v, own, hidden[:, g, :, some], inverse[:, 3:4], hidden[:, g, :, some],
                             hq[:, g, :, some], s["a_q"])
            for g in range(GROUPS):
                v.wait_ge(s["b2_added"], g + 1)
                for b in range(2):
                    v.wait_ge(s["f_sum"], 2 * g + b + 1)
                    t = TILES * g + 2 * b
                    two = res[:, t:t + 2, :]
                    v.scalar_tensor_tensor(two, two_tiles(g, b), prod[:, 1:2], two, ALU.mult,
                                           ALU.add).then_inc(s["res2"], 1)
                v.wait_ge(s["res2"], 2 * (g + 1))
                statistics(g)
            apply(2, lambda g: h[:, TILES * g:TILES * (g + 1), :])

        @block.scalar
        def _(act):
            act.wait_ge(s["m1_sum"], 1)
            act.activation(flat(m1), ps[:, 6, :], ACT.Copy).then_inc(s["m1"], 1)
            act.wait_ge(s["veff_sum"], 1)
            act.activation(veff, ps[:, 7, 0:D], ACT.Copy).then_inc(s["veff"], 1)
            act.wait_ge(s["keff_sum"], 1)
            act.activation(keff, ps[:, 6, 0:D], ACT.Copy).then_inc(s["keff"], 1)

            def turned(j):
                for g in range(GROUPS):
                    for f in range(DT):
                        act.wait_ge(s["turned"], GROUPS * DT * j + DT * g + f + 1)
                        act.activation(hT[:, g, f, :], ps[:, 4 * g + f, :], ACT.Copy).then_inc(s["hT"], 1)

            turned(0)
            for g in range(GROUPS):
                act.wait_ge(s["d_sum"], g + 1)
                act.activation(dT[:, g, :], ps[:, 4 * g + 2, :], ACT.Copy).then_inc(s["d"], 1)
            for g in range(GROUPS):
                for m in range(DT):
                    act.wait_ge(s["q_sum"], DT * g + m + 1)
                    act.activation(qT[:, g, m, :], ps[:, 4 * g + m, :], ACT.Copy).then_inc(s["q"], 1)
            for g in range(GROUPS):
                act.wait_ge(s["k_sum"], DT * g + 1)
                for e in range(2):
                    act.activation(kT[:, g, e, 0, :], ps[:, 4 * g + 2, :], ACT.Identity, bias=0.0,
                                   scale=mem.parity[:, e:e + 1]).then_inc(s["k"], 1)
            for n, (g, half) in enumerate(PAIRS):
                act.wait_ge(s["s_ready"], n + 1)
                act.activation(flat(sc[:, g, half]), flat(sc[:, g, half]), ACT.Exp, scale=SCALE).then_inc(s["e"], 1)
            turned(1)
            act.wait_ge(s["x_scale"], 1)
            for g in range(GROUPS):
                for m in range(M):
                    act.wait_ge(s["a_sum"], M * g + m + 1)
                    act.activation(hidden[:, g, m, :], ps[:, 4 * g + m % 4, :], ACT.Gelu,
                                   bias=b1s[:, m:m + 1], scale=prod[:, 0:1]).then_inc(s["a"], 1)

        @block.tensor
        def _(pe):
            pe.wait_ge(s["mla_in"], 16)
            for f in range(DT):
                ins = pe.matmul(ps[:, 6, f * D:(f + 1) * D], uq[:, f * P:(f + 1) * P], dq_rows,
                                start=True, stop=True)
            ins.then_inc(s["m1_sum"], 1)
            for f in range(DT):
                ins = pe.matmul(ps[:, 7, 0:D], uv[:, f, :], wo[:, f, :], start=(f == 0), stop=(f == DT - 1))
            ins.then_inc(s["veff_sum"], 1)
            pe.wait_ge(s["m1"], 1)
            for f in range(DT):
                ins = pe.matmul(ps[:, 6, 0:D], uk[:, f, :], m1[:, f, :], start=(f == 0), stop=(f == DT - 1))
            ins.then_inc(s["keff_sum"], 1)

            def turn(j):
                for g in range(GROUPS):
                    pe.wait_ge(s["z"], GROUPS * TILES * j + TILES * (g + 1))
                    turn_tiles(pe, z[:, g], mem.ident, ps[:, 4 * g:4 * g + 2, :], s["turned"])

            turn(0)
            pe.wait_ge(s["veff"], 1)
            pe.wait_ge(s["keff"], 1)
            for g in range(GROUPS):
                pe.wait_ge(s["hT"], DT * (g + 1))
                for w_in, bank, done in ((dq, 2, s["d_sum"]), (dkv, 3, s["c_sum"])):
                    for k in range(DT):
                        ins = pe.matmul(ps[:, 4 * g + bank, :], w_in[:, k, :], hT[:, g, k, :],
                                        start=(k == 0), stop=(k == DT - 1))
                    ins.then_inc(done, 1)
            for g in range(GROUPS):
                pe.wait_ge(s["d"], g + 1)
                for m in range(DT):
                    pe.matmul(ps[:, 4 * g + m, :], uq[:, m * P:(m + 1) * P], dT[:, g, :],
                              start=True, stop=True).then_inc(s["q_sum"], 1)
                pe.wait_ge(s["c"], g + 1)
                for m in range(DT):
                    pe.matmul(ps[:, 4 * g + 2 + m, :], keff[:, m * P:(m + 1) * P], cT[:, g, :],
                              start=True, stop=True).then_inc(s["k_sum"], 1)
            for g in range(GROUPS):
                pe.wait_ge(s["q"], DT * (g + 1))
                for t in range(TILES):
                    ins = pe.matmul(ps[:, 4 * g + t // 2, (t % 2) * D:(t % 2 + 1) * D],
                                    cT[:, g, t * P:(t + 1) * P], veff, start=True, stop=True)
                    if t % 2:
                        ins.then_inc(s["v_sum"], 1)
            pe.wait_ge(s["k"], 4 * GROUPS)
            pe.wait_ge(s["v"], 2 * GROUPS)
            for n, (g, half) in enumerate(PAIRS):
                if half == 1:
                    pe.wait_ge(s["masked"], n + 1 - GROUPS)
                for t in range(2):
                    for f in range(DT):
                        col = t * P + 2 * f * 32
                        for i in range(4):
                            for r in range(4):
                                at = slice((2 * half + t) * P + 32 * i, (2 * half + t) * P + 32 * i + 32)
                                ins = pe.matmul(scores(g, half)[32 * i:32 * i + 32, r, col:col + 64],
                                                qT[32 * r:32 * r + 32, g, f, at],
                                                kT[32 * r:32 * r + 32, g, :, f, at],
                                                start=True, stop=True)
                ins.then_inc(s["s_sum"], 1)
            for n, (g, half) in enumerate(PAIRS):
                pe.wait_ge(s["p"], n + 1)
                pe.wait_ge(s["masked"], GROUPS + g + 1)
                for t in range(2):
                    for f in range(DT):
                        for e in range(2):
                            col = t * P + (2 * f + e) * 32
                            for r in range(4):
                                head = 8 * f + 2 * r + e
                                for i in range(4):
                                    rows_i = slice(32 * i, 32 * i + 32)
                                    out_at = t * D + head * MLA_HS
                                    ins = pe.matmul(ps[rows_i, 4 * g + half, out_at:out_at + MLA_HS],
                                                    pT[rows_i, g, half, r, col:col + 32],
                                                    val[rows_i, g, 2 * half + t, head * MLA_HS:(head + 1) * MLA_HS],
                                                    start=True, stop=True)
                ins.then_inc(s["o_sum"], 1)
            turn(1)
            pe.wait_ge(s["w1_q"], 1)
            for g in range(GROUPS):
                pe.wait_ge(s["x_q"], g + 1)
                for m in range(M):
                    if m >= 4:
                        pe.wait_ge(s["a"], M * g + m - 3)
                    for k in range(DT):
                        ins = pe.matmul(ps[:, 4 * g + m % 4, :], w1q[:, k, m * P:(m + 1) * P], xq[:, g, k, :],
                                        start=(k == 0), stop=(k == DT - 1))
                    ins.then_inc(s["a_sum"], 1)
            pe.wait_ge(s["w2_q"], 1)
            for g in range(GROUPS):
                for t in range(TILES):
                    pe.wait_ge(s["a_q"], 2 * g + t // 2 + 1)
                    for k in range(M):
                        ins = pe.matmul(ps[:, 4 * g + t // 2, (t % 2) * D:(t % 2 + 1) * D],
                                        hq[:, g, k, t * P:(t + 1) * P], w2q[:, k, :],
                                        start=(k == 0), stop=(k == M - 1))
                    if t % 2:
                        ins.then_inc(s["f_sum"], 1)
    end_block(nc, mem)


def scan_plan():
    SCANS, C = LAYERS * GROUPS, CHUNKS
    EARLY = 0.5
    jobs = []
    for n in range(SCANS):
        base = C * (n - 1)
        at = {"norm": 4, "xs0": 5, "xs1": 5, "conv0": 7, "conv1": 9, "xproj": 11, "dt0": 11.5, "dt1": 14.5,
              "gate0": C + 2, "gate1": C + 3}
        first = {"norm": 0, "xs0": 1, "xs1": 2, "conv0": 3, "gate0": 3.2, "gate1": 3.4, "conv1": 4, "xproj": 5,
                 "dt0": 6, "dt1": 80}
        for what, p in at.items():
            if (what, n) == ("conv1", 0):
                continue
            where = first[what] - 100 if n == 0 else base + p - (EARLY if n == 1 and p < C else 0)
            jobs.append((where, 0, (what.rstrip("01"), n, int(what[-1]) if what[-1] in "01" else 0)))
        jobs.append((C * (n + 1) + 1, 0, ("out", n, 0)))
        for part in range(NC):
            q = NC * n + part
            start = KT * q
            for r, lead in enumerate((4, 3, 2, 1)):
                jobs.append((start - lead if q else -50, 1 + r, ("rows", q, r)))
    for g in range(GROUPS):
        base = C * (SCANS - GROUPS + g + 1)
        for what, half, p in (("score", 0, 6), ("gather", 0, 7), ("up", 0, 9), ("up", 1, 11), ("down", 0, 11.5),
                              ("back", 0, 13.5)):
            jobs.append((base + p, 0, (what, g, half)))
    jobs.sort()
    slot = {job: k % 2 for k, (_, _, job) in enumerate(jobs)}
    order = [job for _, _, job in jobs]
    place = {job: p for p, _, job in jobs}

    def with_chunks(items, *part):
        items = items + [(c, 10 ** 9, ("chunk", c, 0, *part)) for c in range(C * SCANS)]
        return [job for _, _, job in sorted(items)]

    def later(p, by):
        return p if p < -20 else max(p, -1) + by

    two_parts = ("xs", "conv", "gate", "dt", "out")
    tensor = []
    for k, (p, _, job) in enumerate(jobs):
        tensor.append((p, k, (*job, 0)))
        if job[0] in two_parts and job != ("conv", 0, 0):
            tensor.append((p, k, (*job, 1)))
    tensor = with_chunks(tensor, 0)
    scalar = [(-100 + 4, -1, ("tapped", 0, m, 0)) for m in range(1, KT)]
    vector = [(-100 + 4, -1, ("taps", 0, 1))]
    for k, job in enumerate(order):
        p, (what, n, _) = place[job], job
        if what == "norm":
            scalar.append((later(p, -1), k - 1, ("square", n, 0, 0)))
            scalar.append((later(p, 1), k - 0.5, ("z", n, 0, 0)))
        if what == "dt":
            vector.append((later(p, 2), k, ("delta", n, job[2])))
        if what == "score":
            scalar.append((p - 3, k - 1, ("mix_square", n, 0, 0)))
            vector.append((p - 2, k - 1, ("mix_first", n, 0)))
            vector.append((p - 1, k - 1, ("mix_norm", n, 0)))
        if what in ("down", "back"):
            vector.append((later(p, 2), k, job))
        elif what in ("xproj", "out", "score"):
            vector.append((later(p, 1), k, job))
        else:
            for i in range(2 if what in two_parts and job != ("conv", 0, 0) else 1):
                scalar.append((later(p, 2), k, (*job, i)))
    for n in range(SCANS):
        for m in range(KT):
            vector.append((C * (n + 1) - KT + 2 + m, -1, ("y", n, m)))
    return tensor, with_chunks(scalar, 0), with_chunks(vector), slot, order


def mamba_and_mixture(nc, ctx, mem, dram):
    s = named(mem, """cols_in in_in x_in dt_in out_in gate_in sel_in diag a_exp a_neg squares rstd z
        turned hT xs_sum xs gate_sum gate conv_sum tapped u x_sum x bc3 dt_sum dt_free soft delta du bc_sum bc
        input decay scanned weighted reduced skip_diag y o_sum bo_added h_out v_own p_own
        mix_in up_in down_in mix_squares mix_rstd mix_first stats rstd2 mix_z spread_in score_sum seen minus expo
        pick gathered mix_hT place_sum place a_sum a f_sum biased back_sum x_added done stored""")
    PAD = (CONV - 1) // 2
    WORKS = 3
    SEQ = GROUP // T
    SCANS = LAYERS * GROUPS
    a = mem.fresh()
    w_in = a.take(DT, 2 * INNER)
    w_conv = a.take(KT * CONV, P)
    w_skip = a.take(KT, P)
    w_x = a.take(KT, RANK + 2 * STATE)
    w_dt = a.take(INNER, rows=RANK)
    w_out = a.take(KT, D)
    cols = a.take(LAYERS, 48)
    decay_rate = a.take(LAYERS, KT, STATE)
    b_out = a.take(LAYERS, D)
    squares, rstd = a.take(SCANS, TILES), a.take(SCANS, TILES)
    select = a.take(2 * STATE, P, dtype=BF16, rows=96)
    z, hT = a.take(TILES, D), a.take(DT, GROUP)
    padded = a.take(KT, SEQ, T + 2 * PAD)
    soft = padded.rearrange("p m s t -> p (m s) t")[:, :, PAD:PAD + T]
    u, gate = a.take(2, KT, GROUP), a.take(KT, GROUP)
    delta, du = a.take(2, KT, GROUP), a.take(2, KT, GROUP)
    xd = a.take(GROUP, rows=96)
    bc3 = a.take(2, GROUP, dtype=BF16, rows=96)
    bc = a.take(2, 2 * CH, GROUP)
    decay, work = a.take(2, CH, GROUP), a.take(WORKS, CH, GROUP)
    ps, h, res = mem.ps, mem.h, mem.res
    for_tensor, for_scalar, for_vector, slot, jobs = scan_plan()

    def flat(ap):
        return ap.rearrange("p a b -> p (a b)")

    def steps_of(ap):
        return ap.rearrange("p (b t) -> p b t", t=T)

    def tiles_of(n, stream=h):
        g = n % GROUPS
        return stream[:, TILES * g:TILES * (g + 1), :]

    M = FFN // P
    SLOTS = P // T * TOP
    PICKED = TILES * SLOTS
    w_up = flat(u[:, 0]).rearrange("p (k n) -> p k n", k=DT)
    w_down = flat(delta[:, 0]).rearrange("p (k n) -> p k n", k=M)
    hidden = padded.rearrange("p m s t -> p (m s t)")[:, 0:M * PICKED].rearrange("p (m n) -> p m n", m=M)
    x, xT = z, hT.rearrange("p f n -> p (f n)")[:, 0:DT * PICKED].rearrange("p (f n) -> p f n", f=DT)
    d = Arena(flat(du[:, 0]), KT * GROUP)
    first, biased = d.take(TILES, D), d.take(2, D)
    pick = d.take(TILES, SLOTS)
    place = d.take(2, P)
    d = Arena(flat(w_conv), KT * CONV * P)
    mix_rows = d.take(3, D)
    b1 = d.take(M)
    stats, mv = d.take(TILES, 6), d.take(TILES, 2)
    mix_squares, mix_rstd, score, mine, rank, expo, weight = (d.take(TILES) for _ in range(7))
    each, seen, tmp, tied = (d.take(TILES, T) for _ in range(4))

    def banks(job):
        return ps[:, 4 + 2 * slot[job]:6 + 2 * slot[job], :]

    def column(n, at):
        return cols[:, n // GROUPS, at:at + 1]

    B_IN, B_CONV, B_DT, SKIP, W_NORM, TAPS = 0, 8, 12, 16, 20, 24

    def conv_sums(n, m):
        return KT * n + m + 1 - (KT - 1 if n else 0)

    def emptied(job):
        what, n, half = job
        return {"norm": (s["hT"], DT * (n + 1)), "xs": (s["xs"], KT * n + 2 * half + 2),
                "gate": (s["gate"], KT * n + 2 * half + 2), "conv": (s["u"], KT * n + 2 * half + 2 if n else 1),
                "xproj": (s["x"], n + 1), "dt": (s["dt_free"], KT * n + 2 * half + 2),
                "rows": (s["bc"], CH * n + half + 1), "out": (s["h_out"], 2 * (n + 1)),
                "score": (s["seen"], n + 1), "gather": (s["place"], n + 1),
                "up": (s["a"], M * n + 4 * half + 4), "down": (s["biased"], 2 * (n + 1)),
                "back": (s["done"], TILES * (n + 1))}[what]

    def up_bank(job, m):
        return banks(job)[:, m // 2 % 2, (m % 2) * PICKED:(m % 2 + 1) * PICKED]

    def back_bank(job, t):
        return banks(job)[:, t % 2, (t // 2) * D:(t // 2 + 1) * D]

    with nc.Block() as block:
        @block.sync
        def _(sp):
            sp.dma_start(cols, dram["mam_cols"].rearrange("l p c -> p l c")).then_inc(s["cols_in"], 16)
            sp.dma_start(decay_rate.rearrange("p l m s -> p l (m s)"),
                         dram["mam_alog"].rearrange("l p m s -> p l (m s)")).then_inc(s["cols_in"], 16)
            sp.dma_start(b_out, dram["mam_bo"].rearrange("l p d -> p l d")).then_inc(s["cols_in"], 16)
            for l in range(LAYERS):
                last = GROUPS * l
                if l:
                    sp.wait_ge(s["xs_sum"], KT * last)
                sp.dma_start(w_in[:, :, 0:INNER], dram["mam_in"][l, :, :, 0:INNER]).then_inc(s["in_in"], 16)
                if l == 0:
                    sp.dma_start(select, dram["select"]).then_inc(s["sel_in"], 16)
                if l:
                    sp.wait_ge(s["x_sum"], last)
                sp.dma_start(w_x, dram["mam_x"][l, :, :, :]).then_inc(s["x_in"], 16)
                if l:
                    sp.wait_ge(s["dt_sum"], KT * last)
                sp.dma_start(w_dt, dram["mam_dt"][l, :, :]).then_inc(s["dt_in"], 16)
                if l:
                    sp.wait_ge(s["gate_sum"], KT * last)
                sp.dma_start(w_in[:, :, INNER:2 * INNER],
                             dram["mam_in"][l, :, :, INNER:2 * INNER]).then_inc(s["gate_in"], 16)
                if l:
                    sp.wait_ge(s["o_sum"], 2 * last)
                sp.dma_start(w_out, dram["mam_out"][l, :, :, :]).then_inc(s["out_in"], 16)
            first_group = SCANS - GROUPS
            sp.wait_ge(s["du"], 2 * (first_group + 1))
            sp.wait_ge(s["reduced"], CHUNKS * first_group + KT)
            sp.dma_start(w_up, dram["mod_w1"]).then_inc(s["up_in"], 16)
            sp.wait_ge(s["conv_sum"], conv_sums(SCANS - 1, KT - 1))
            sp.dma_start(mix_rows, dram["mod_rows"]).then_inc(s["mix_in"], 16)
            sp.dma_start(b1, dram["mod_b1"]).then_inc(s["mix_in"], 16)
            sp.wait_ge(s["decay"], CH * CHUNKS * (first_group + 1))
            sp.dma_start(w_down, dram["mod_w2"]).then_inc(s["down_in"], 16)
            for g in range(GROUPS):
                sp.wait_ge(s["done"], TILES * (g + 1))
                out = dram["out"][g * GROUP:(g + 1) * GROUP, :].rearrange("(t p) d -> p t d", p=P)
                sp.dma_start(out, tiles_of(g, res)).then_inc(s["stored"], 16)
            sp.wait_ge(s["stored"], 16 * GROUPS)

        @block.gpsimd
        def _(pool):
            own = Steps(pool, s["p_own"])

            def scale_rows(n):
                pool.wait_ge(s["squares"], TILES * (n + 1))
                own.step(pool.tensor_scalar(rstd[:, n], squares[:, n], 1.0 / D, EPS, ALU.mult, ALU.add))
                own.settle()
                pool.tensor_tensor(rstd[:, n], rstd[:, n], mem.minus_half, ALU.pow).then_inc(s["rstd"], 1)
                pool.wait_ge(s["rstd"], n + 1)

            def diagonals(l):
                pool.wait_ge(s["cols_in"], 48)
                pool.tensor_tensor(w_conv, spread(mem.ident, 1, KT * CONV),
                                   spread(cols[:, l, TAPS:TAPS + KT * CONV], 2, P), ALU.mult).then_inc(s["diag"], 1)
                pool.wait_ge(s["diag"], l + 1)

            def skip_diagonals(l):
                pool.wait_ge(s["cols_in"], 48)
                pool.tensor_tensor(w_skip, spread(mem.ident, 1, KT), spread(cols[:, l, SKIP:SKIP + KT], 2, P),
                                   ALU.mult).then_inc(s["skip_diag"], 1)
                pool.wait_ge(s["skip_diag"], l + 1)

            for n in range(SCANS):
                scale_rows(n)
                if n == 0:
                    own.step(pool.memset(padded, 0.0))
                    own.settle()
                    diagonals(0)
                    own.step(pool.memset(decay, 0.0))
                    own.settle()
                    skip_diagonals(0)
                if n % GROUPS == GROUPS - 1 and n < SCANS - 1:
                    pool.wait_ge(s["conv_sum"], conv_sums(n, KT - 1))
                    diagonals(n // GROUPS + 1)
                if n and n % GROUPS == 0:
                    pool.wait_ge(s["reduced"], CHUNKS * (n - 1) + KT)
                    skip_diagonals(n // GROUPS)
                pool.wait_ge(s["z"], TILES * (n + 1))
                pool.tensor_tensor(tiles_of(n), tiles_of(n), spread(b_out[:, n // GROUPS, :], 1, TILES),
                                   ALU.add).then_inc(s["bo_added"], 1)
                pool.wait_ge(s["bo_added"], n + 1)
            for g in range(GROUPS):
                pool.wait_ge(s["mix_squares"], TILES * (g + 1))
                own.step(pool.tensor_scalar(mix_rstd, mix_squares, 1.0 / D, EPS, ALU.mult, ALU.add))
                own.settle()
                pool.tensor_tensor(mix_rstd, mix_rstd, mem.minus_half, ALU.pow).then_inc(s["mix_rstd"], 1)
                pool.wait_ge(s["mix_rstd"], g + 1)
                pool.wait_ge(s["stats"], g + 1)
                norm_rstd(pool, own, mv[:, :, 1], mix_rstd, mem.minus_half, EPS, s["rstd2"], g + 1)
                pool.wait_ge(s["mix_z"], TILES * (g + 1))
                pool.tensor_tensor(tiles_of(g, res), tiles_of(g, res), x, ALU.add).then_inc(s["x_added"], 1)
                pool.wait_ge(s["x_added"], g + 1)

        @block.scalar
        def _(act):
            for what, n, half, i in for_scalar:
                job = (what, n, half)
                b = n % 2
                if job == ("norm", 0, 0):
                    act.wait_ge(s["cols_in"], 48)
                if what == "square":
                    if n >= GROUPS:
                        act.wait_ge(s["h_out"], 2 * (n - GROUPS + 1))
                    if n:
                        act.wait_ge(s["turned"], DT * n)
                    for t in range(TILES):
                        act.activation(z[:, t, :], tiles_of(n)[:, t, :], ACT.Square,
                                       accum_out=squares[:, n, t:t + 1]).then_inc(s["squares"], 1)
                if what == "z":
                    act.wait_ge(s["rstd"], n + 1)
                    for t in range(TILES):
                        act.activation(z[:, t, :], tiles_of(n)[:, t, :], ACT.Identity, bias=0.0,
                                       scale=rstd[:, n, t:t + 1]).then_inc(s["z"], 1)
                if what == "norm":
                    act.wait_ge(s["turned"], DT * (n + 1))
                    if n:
                        act.wait_ge(s["gate_sum"], KT * n)
                    for f in range(DT):
                        act.activation(hT[:, f, :], banks(job)[:, f, :], ACT.Identity, bias=0.0,
                                       scale=column(n, W_NORM + f)).then_inc(s["hT"], 1)
                if what == "xs":
                    act.wait_ge(s["p_own"], 2)
                    if n:
                        act.wait_ge(s["delta"], 2 * n)
                    m = 2 * half + i
                    act.wait_ge(s["xs_sum"], KT * n + m + 1)
                    act.activation(padded[:, m, :, PAD:PAD + T], steps_of(banks(job)[:, i, :]), ACT.Identity,
                                   bias=column(n, B_IN + m)).then_inc(s["xs"], 1)
                if what == "gate":
                    if n:
                        act.wait_ge(s["y"], KT * n)
                    m = 2 * half + i
                    act.wait_ge(s["gate_sum"], KT * n + m + 1)
                    act.activation(gate[:, m, :], banks(job)[:, i, :], ACT.Silu,
                                   bias=column(n, B_IN + KT + m)).then_inc(s["gate"], 1)
                if what == "tapped":
                    m = half
                    act.wait_ge(s["tapped"], m)
                    act.activation(u[:, 0, m, :], u[:, 0, m, :], ACT.Silu, bias=column(0, B_CONV + m)).then_inc(s["u"], 1)
                if what == "conv":
                    m = 2 * half + i
                    act.wait_ge(s["conv_sum"], conv_sums(n, m))
                    act.activation(u[:, b, m, :], banks(job)[:, i, :], ACT.Silu,
                                   bias=column(n, B_CONV + m)).then_inc(s["u"], 1)
                if what == "dt":
                    if half == i == 0 and n % GROUPS == 0:
                        every = flat(decay_rate[:, n // GROUPS])
                        act.activation(every, every, ACT.Exp).then_inc(s["a_exp"], 1)
                    m = 2 * half + i
                    act.wait_ge(s["dt_sum"], KT * n + m + 1)
                    act.activation(soft[:, SEQ * m:SEQ * (m + 1), :], steps_of(banks(job)[:, i, :]), ACT.Abs,
                                   bias=column(n, B_DT + m)).then_inc(s["soft"], 1)
                    act.activation(delta[:, b, m, :], banks(job)[:, i, :], ACT.Relu,
                                   bias=column(n, B_DT + m)).then_inc(s["dt_free"], 1)
                    if i == 1:
                        of_half = soft[:, 2 * SEQ * half:2 * SEQ * (half + 1), :]
                        act.wait_ge(s["soft"], 4 * (2 * n + half) + 2)
                        act.activation(of_half, of_half, ACT.Exp, scale=-1.0).then_inc(s["soft"], 1)
                        act.wait_ge(s["soft"], 4 * (2 * n + half) + 3)
                        act.activation(of_half, of_half, ACT.Ln, bias=1.0).then_inc(s["soft"], 1)
                if what == "mix_square":
                    if n:
                        act.wait_ge(s["x_added"], n)
                    for t in range(TILES):
                        act.wait_ge(s["h_out"], 2 * (SCANS - GROUPS + n) + t // 2 + 1)
                        act.activation(x[:, t, :], tiles_of(n)[:, t, :], ACT.Square,
                                       accum_out=mix_squares[:, t:t + 1]).then_inc(s["mix_squares"], 1)
                if what == "gather":
                    if n:
                        act.wait_ge(s["done"], TILES * n)
                    act.wait_ge(s["minus"], n + 1)
                    act.activation(expo, mine, ACT.Exp, scale=-1.0).then_inc(s["expo"], 1)
                    act.wait_ge(s["gathered"], n + 1)
                    act.activation(flat(xT), banks(job)[:, 0, :], ACT.Copy).then_inc(s["mix_hT"], 1)
                    act.wait_ge(s["place_sum"], n + 1)
                    act.activation(flat(place), banks(job)[:, 1, 0:2 * P], ACT.Copy).then_inc(s["place"], 1)
                if what == "up":
                    act.wait_ge(s["mix_in"], 32)
                    for m in range(4 * half, 4 * half + 4):
                        act.wait_ge(s["a_sum"], M // 2 * n + m // 2 + 1)
                        act.activation(hidden[:, m, :], up_bank(job, m), ACT.Gelu_apprx_tanh,
                                       bias=b1[:, m:m + 1]).then_inc(s["a"], 1)
                if what == "rows":
                    if n >= 2:
                        act.wait_ge(s["weighted"], KT * (n - 1))
                    act.wait_ge(s["bc_sum"], CH * n + half + 1)
                    act.activation(bc[:, n % 2, 2 * half:2 * half + 2, :], banks(job), ACT.Copy).then_inc(s["bc"], 1)
                if what == "chunk":
                    g, part, m = n // CHUNKS, n % CHUNKS // KT, n % KT
                    act.wait_ge(s["delta"], 2 * g + m // 2 + 1)
                    act.wait_ge(s["a_neg"], g // GROUPS + 1)
                    if n == 0:
                        act.wait_ge(s["p_own"], 3)
                    if n >= 2:
                        act.wait_ge(s["scanned"], n - 1)
                    for j in range(CH):
                        state = CH * part + j
                        act.activation(steps_of(decay[:, n % 2, j, :])[:, :, 1:T],
                                       steps_of(delta[:, g % 2, m, :])[:, :, 1:T], ACT.Exp,
                                       scale=decay_rate[:, g // GROUPS, m, state:state + 1]).then_inc(s["decay"], 1)

        @block.vector
        def _(v):
            own = Steps(v, s["v_own"])

            def chunk_input(n):
                g, q, m = n // CHUNKS, n // KT, n % KT
                v.wait_ge(s["du"], 2 * g + m // 2 + 1)
                v.wait_ge(s["bc"], CH * q + CH // 2)
                if n >= WORKS:
                    v.wait_ge(s["reduced"], n - WORKS + 1)
                v.tensor_tensor(work[:, n % WORKS], spread(du[:, g % 2, m, :], 1, CH), bc[:, q % 2, 0:CH, :],
                                ALU.mult).then_inc(s["input"], 1)

            for job in for_vector:
                what, n, half = job
                b = n % 2
                if what == "taps":
                    v.wait_ge(s["cols_in"], 48)
                    for k in range(CONV):
                        for m in range(1, KT):
                            shifted, out = padded[:, m, :, k:k + T], steps_of(u[:, 0, m, :])
                            tap = column(0, TAPS + CONV * m + k)
                            if k == 0:
                                v.wait_ge(s["xs"], m + 1)
                                ins = v.tensor_scalar(out, shifted, tap, None, ALU.mult)
                            else:
                                v.wait_ge(s["v_own"], (k - 1) * (KT - 1) + m)
                                ins = v.scalar_tensor_tensor(out, shifted, tap, out, ALU.mult, ALU.add)
                            if k == CONV - 1:
                                ins.then_inc(s["tapped"], 1)
                            else:
                                own.step(ins)
                if what == "xproj":
                    lo, mid, hi = slice(0, 32), slice(32, 64), slice(64, 96)
                    rest, middle = du[:, b, 0, :], du[:, b, 1, 0:GROUP // 2].bitcast(BF16)
                    v.wait_ge(s["x_sum"], n + 1)
                    v.tensor_copy(xd, banks(job)[0:96, 0, :]).then_inc(s["x"], 1)
                    v.wait_ge(s["x"], n + 1)
                    own.step(v.tensor_copy(bc3[hi, b, :], xd[hi, :]))
                    own.settle()
                    own.step(v.tensor_tensor(rest[hi, :], xd[hi, :], bc3[hi, b, :], ALU.subtract))
                    own.settle()
                    own.step(v.tensor_copy(middle[hi, :], rest[hi, :]))
                    own.settle()
                    own.step(v.tensor_tensor(rest[hi, :], rest[hi, :], middle[hi, :], ALU.subtract))
                    own.step(v.tensor_copy(bc3[mid, b, :], middle[hi, :]))
                    own.settle()
                    v.tensor_copy(bc3[lo, b, :], rest[hi, :]).then_inc(s["bc3"], 1)
                if what == "delta":
                    if half == 0 and n % GROUPS == 0:
                        l = n // GROUPS
                        v.wait_ge(s["a_exp"], l + 1)
                        v.tensor_scalar(flat(decay_rate[:, l]), flat(decay_rate[:, l]), -1.0, None,
                                        ALU.mult).then_inc(s["a_neg"], 1)
                    two = slice(2 * half, 2 * half + 2)
                    v.wait_ge(s["soft"], 4 * (2 * n + half + 1))
                    v.wait_ge(s["dt_free"], KT * n + 2 * half + 2)
                    both = steps_of(flat(delta[:, b, two]))
                    v.tensor_tensor(both, both, soft[:, 2 * SEQ * half:2 * SEQ * (half + 1), :],
                                    ALU.add).then_inc(s["delta"], 1)
                    v.wait_ge(s["delta"], 2 * n + half + 1)
                    v.wait_ge(s["u"], KT * (n + 1))
                    v.tensor_tensor(flat(du[:, b, two]), flat(delta[:, b, two]), flat(u[:, b, two]),
                                    ALU.mult).then_inc(s["du"], 1)
                if what == "chunk":
                    q = n // KT
                    rows = bc[:, q % 2]
                    w = work[:, n % WORKS]
                    if n == 0:
                        chunk_input(0)
                    v.wait_ge(s["decay"], CH * (n + 1))
                    v.wait_ge(s["input"], n + 1)
                    v.tensor_tensor_scan(flat(w), flat(decay[:, n % 2]), flat(w), 0.0, ALU.mult,
                                         ALU.add).then_inc(s["scanned"], 1)
                    if n + 1 < CHUNKS * SCANS:
                        chunk_input(n + 1)
                    v.wait_ge(s["scanned"], n + 1)
                    v.wait_ge(s["bc"], CH * (q + 1))
                    v.tensor_tensor(w, w, rows[:, CH:2 * CH, :], ALU.mult).then_inc(s["weighted"], 1)
                if what == "y":
                    m = half
                    v.wait_ge(s["reduced"], CHUNKS * (n + 1) - KT + m + 1)
                    v.wait_ge(s["gate"], KT * n + m + 1)
                    v.tensor_tensor(du[:, b, m, :], ps[:, m, :], gate[:, m, :], ALU.mult).then_inc(s["y"], 1)
                if what == "mix_first":
                    v.wait_ge(s["mix_in"], 32)
                    v.wait_ge(s["mix_rstd"], n + 1)
                    for t in range(TILES):
                        v.scalar_tensor_tensor(first[:, t, :], tiles_of(n)[:, t, :], mix_rstd[:, t:t + 1],
                                               mix_rows[:, 0, :], ALU.mult, ALU.mult).then_inc(s["mix_first"], 1)
                    v.wait_ge(s["mix_first"], TILES * (n + 1))
                    own.step(v.tensor_tensor(tiles_of(n, res), tiles_of(n, res), first, ALU.add))
                    own.settle()
                    norm_stats(v, own, tiles_of(n, res), stats, mv, s["stats"])
                if what == "mix_norm":
                    v.wait_ge(s["rstd2"], n + 1)
                    norm_apply(v, tiles_of(n, res), mv, mix_rstd, x, s["mix_z"])
                    v.wait_ge(s["mix_z"], TILES * (n + 1))
                    for t in range(TILES):
                        own.step(v.tensor_tensor_reduce(first[:, t, :], x[:, t, :], mix_rows[:, 1, :], 1.0, 0.0,
                                                        ALU.mult, ALU.add, score[:, t:t + 1]))
                    own.settle()
                    v.tensor_tensor(each, spread(mem.slot, 1, TILES), spread(score, 2, T),
                                    ALU.mult).then_inc(s["spread_in"], 1)
                if what == "score":
                    v.wait_ge(s["score_sum"], n + 1)
                    v.tensor_copy(seen, banks(job)[:, 0, 0:TILES * T].rearrange("p (t j) -> p t j", j=T))\
                     .then_inc(s["seen"], 1)
                    v.wait_ge(s["seen"], n + 1)
                    own.step(v.tensor_tensor(tmp, seen, spread(mem.slot, 1, TILES), ALU.mult))
                    own.settle()
                    v.tensor_reduce(mine, tmp, AX, ALU.add).then_inc(s["minus"], 1)
                    v.wait_ge(s["minus"], n + 1)
                    own.step(v.tensor_tensor(tied, seen, spread(mine, 2, T), ALU.is_equal))
                    own.step(v.tensor_tensor(tmp, seen, spread(mine, 2, T), ALU.is_gt))
                    own.settle()
                    own.step(v.tensor_tensor(tied, tied, spread(mem.before, 1, TILES), ALU.mult))
                    own.settle()
                    own.step(v.tensor_tensor(tmp, tmp, tied, ALU.add))
                    own.settle()
                    own.step(v.tensor_reduce(rank, tmp, AX, ALU.add))
                    own.settle()
                    v.tensor_tensor(pick, spread(rank, 2, SLOTS), spread(mem.slot_rank, 1, TILES),
                                    ALU.is_equal).then_inc(s["pick"], 1)
                if what == "down":
                    v.wait_ge(s["expo"], n + 1)
                    own.step(v.tensor_scalar(weight, expo, 1.0, None, ALU.add))
                    own.settle()
                    own.step(v.reciprocal(weight, weight))
                    v.wait_ge(s["f_sum"], n + 1)
                    for b in range(2):
                        v.tensor_tensor(biased[:, b, :], banks(job)[:, 0, b * D:(b + 1) * D], mix_rows[:, 2, :],
                                        ALU.add).then_inc(s["biased"], 1)
                if what == "back":
                    own.settle()
                    v.wait_ge(s["x_added"], n + 1)
                    v.wait_ge(s["back_sum"], 2 * (n + 1))
                    for t in range(TILES):
                        tile = tiles_of(n, res)[:, t, :]
                        v.scalar_tensor_tensor(tile, back_bank(job, t), weight[:, t:t + 1], tile, ALU.mult,
                                               ALU.add).then_inc(s["done"], 1)
                if what == "out":
                    v.wait_ge(s["bo_added"], n + 1)
                    for i in range(2):
                        v.wait_ge(s["o_sum"], 2 * n + i + 1)
                        two = tiles_of(n)[:, 2 * i:2 * i + 2, :]
                        v.tensor_tensor(two, two, banks(job)[:, i, :].rearrange("p (t d) -> p t d", t=2),
                                        ALU.add).then_inc(s["h_out"], 1)

        @block.tensor
        def _(pe):
            for what, n, half, i in for_tensor:
                job = (what, n, half)
                b, l = n % 2, n // GROUPS
                if what != "chunk" and i == 0 and jobs.index(job) >= 2:
                    pe.wait_ge(*emptied(jobs[jobs.index(job) - 2]))
                if what == "norm":
                    pe.wait_ge(s["z"], TILES * (n + 1))
                    turn_tiles(pe, z, mem.ident, banks(job), s["turned"])
                if what in ("xs", "gate"):
                    pe.wait_ge(s["in_in"] if what == "xs" else s["gate_in"], 16 * (l + 1))
                    pe.wait_ge(s["hT"], DT * (n + 1))
                    at = (2 * half + i) * P + (0 if what == "xs" else INNER)
                    for k in range(DT):
                        ins = pe.matmul(banks(job)[:, i, :], w_in[:, k, at:at + P],
                                        hT[:, k, :], start=(k == 0), stop=(k == DT - 1))
                    ins.then_inc(s["xs_sum"] if what == "xs" else s["gate_sum"], 1)
                if what == "conv":
                    pe.wait_ge(s["diag"], l + 1)
                    m = 2 * half + i
                    pe.wait_ge(s["xs"], KT * n + m + 1)
                    for k in range(CONV):
                        ins = pe.matmul(banks(job)[:, i, :], w_conv[:, CONV * m + k, :],
                                        padded[:, m, :, k:k + T], start=(k == 0), stop=(k == CONV - 1))
                    ins.then_inc(s["conv_sum"], 1)
                if what == "xproj":
                    pe.wait_ge(s["x_in"], 16 * (l + 1))
                    pe.wait_ge(s["u"], KT * (n + 1))
                    for k in range(KT):
                        ins = pe.matmul(banks(job)[0:96, 0, :], w_x[:, k, :], u[:, b, k, :],
                                        start=(k == 0), stop=(k == KT - 1))
                    ins.then_inc(s["x_sum"], 1)
                if what == "dt":
                    pe.wait_ge(s["dt_in"], 16 * (l + 1))
                    pe.wait_ge(s["x"], n + 1)
                    m = 2 * half + i
                    pe.matmul(banks(job)[:, i, :], w_dt[:, m * P:(m + 1) * P], xd[0:RANK, :],
                              start=True, stop=True).then_inc(s["dt_sum"], 1)
                if what == "rows":
                    g, part = n // NC, n % NC
                    pe.wait_ge(s["sel_in"], 16)
                    pe.wait_ge(s["bc3"], g + 1)
                    for i in range(2):
                        j = 2 * half + i
                        row = (j // CH) * STATE + CH * part + j % CH
                        ins = pe.matmul(banks(job)[:, i, :], select[:, row, :], bc3[:, g % 2, :],
                                        start=True, stop=True)
                    ins.then_inc(s["bc_sum"], 1)
                if what == "chunk":
                    g, part, m = n // CHUNKS, n % CHUNKS // KT, n % KT
                    if g and part == 0:
                        pe.wait_ge(s["y"], KT * (g - 1) + m + 1)
                    if part == 0:
                        pe.wait_ge(s["skip_diag"], g // GROUPS + 1)
                        pe.wait_ge(s["u"], KT * (g + 1))
                        pe.matmul(ps[:, m, :], w_skip[:, m, :], u[:, g % 2, m, :], start=True, stop=False)
                    pe.wait_ge(s["weighted"], n + 1)
                    for j in range(CH):
                        ins = pe.matmul(ps[:, m, :], mem.ident, work[:, n % WORKS, j, :],
                                        start=False, stop=(part == NC - 1 and j == CH - 1))
                    ins.then_inc(s["reduced"], 1)
                if what == "out":
                    pe.wait_ge(s["out_in"], 16 * (l + 1))
                    pe.wait_ge(s["y"], KT * (n + 1))
                    for t in (2 * i, 2 * i + 1):
                        for k in range(KT):
                            ins = pe.matmul(banks(job)[:, i, (t % 2) * D:(t % 2 + 1) * D],
                                            du[:, b, k, t * P:(t + 1) * P], w_out[:, k, :],
                                            start=(k == 0), stop=(k == KT - 1))
                    ins.then_inc(s["o_sum"], 1)
                if what == "score":
                    pe.wait_ge(s["spread_in"], n + 1)
                    pe.matmul(banks(job)[:, 0, 0:TILES * T], mem.seq_block, each.rearrange("p t j -> p (t j)"),
                              start=True, stop=True).then_inc(s["score_sum"], 1)
                if what == "gather":
                    pe.wait_ge(s["pick"], n + 1)
                    for f in range(DT):
                        for t in range(TILES):
                            at = f * PICKED + t * SLOTS
                            ins = pe.matmul(banks(job)[:, 0, at:at + SLOTS], x[:, t, f * P:(f + 1) * P],
                                            pick[:, t, :], start=True, stop=True)
                    ins.then_inc(s["gathered"], 1)
                    for k in range(2):
                        ins = pe.transpose(banks(job)[:, 1, k * P:(k + 1) * P],
                                           pick[:, 2 * k:2 * k + 2, :].rearrange("p t n -> p (t n)"), mem.ident)
                    ins.then_inc(s["place_sum"], 1)
                if what == "up":
                    pe.wait_ge(s["up_in"], 16)
                    pe.wait_ge(s["mix_hT"], n + 1)
                    for m in range(4 * half, 4 * half + 4):
                        for k in range(DT):
                            ins = pe.matmul(up_bank(job, m), w_up[:, k, m * P:(m + 1) * P], xT[:, k, :],
                                            start=(k == 0), stop=(k == DT - 1))
                        if m % 2:
                            ins.then_inc(s["a_sum"], 1)
                if what == "down":
                    pe.wait_ge(s["down_in"], 16)
                    pe.wait_ge(s["a"], M * (n + 1))
                    for k in range(2):
                        for m in range(M):
                            ins = pe.matmul(banks(job)[:, 0, k * D:(k + 1) * D], hidden[:, m, k * P:(k + 1) * P],
                                            w_down[:, m, :], start=(m == 0), stop=(m == M - 1))
                    ins.then_inc(s["f_sum"], 1)
                if what == "back":
                    pe.wait_ge(s["place"], n + 1)
                    pe.wait_ge(s["biased"], 2 * (n + 1))
                    for t in range(TILES):
                        mine_in = slice((t % 2) * SLOTS, (t % 2 + 1) * SLOTS)
                        ins = pe.matmul(back_bank(job, t), place[mine_in, t // 2, :], biased[mine_in, t // 2, :],
                                        start=True, stop=True)
                        if t >= 2:
                            ins.then_inc(s["back_sum"], 1)


BLOCKS = [token_mlp, attention_layers, latent_attention_and_ffn, mamba_and_mixture]


def audio_tower(nc, dram):
    with ExitStack() as ctx:
        size = 53200
        tensor = ctx.enter_context(nc.sbuf_tensor("arena", [P, size], F32))
        ps = ctx.enter_context(nc.psum_tensor("banks", [P, 8, 512], F32))
        a = Arena(tensor, size)
        consts = a.take(CONSTS)
        mem = Memory()
        mem.ps, mem.consts = ps, consts
        mem.res = a.take(GROUPS * TILES, D)
        mem.h = a.take(GROUPS * TILES, D)
        at = 0
        parts = []
        for n in CONST_PARTS:
            parts.append(consts[:, at:at + n])
            at += n
        mem.ident, mem.same_seq, mem.causal, mem.parity, mem.minus_half, mem.seq_block, mem.slot, mem.before, mem.slot_rank = parts
        start = a.at

        def fresh():
            b = Arena(tensor, size)
            b.at = start
            return b

        mem.fresh = fresh
        mem.pool = [ctx.enter_context(nc.semaphore(f"count{n}")) for n in range(SEMAPHORES)]
        mem.numbers = range(mem.pool[0].num, mem.pool[-1].num + 1)
        assert len(mem.numbers) == SEMAPHORES
        for block in BLOCKS:
            block(nc, ctx, mem, dram)


CONST_PARTS = [P, 32, 32, 2, TILES, P, T, T, P // T * TOP]
CONSTS = sum(CONST_PARTS)


def constants(np):
    p = np.arange(P)[:, None]
    k = np.arange(32)[None, :]
    same = (p % 32) // T == k // T
    causal = same & (k % T <= p % T)
    far = np.float32(-1e30)
    step = np.arange(T)[None, :]
    slots = np.arange(P // T * TOP)[None, :]
    parts = [
        np.eye(P),
        np.where(same, 0, far),
        np.where(causal, 0, far),
        (p // MLA_HS) % 2 == np.arange(2)[None, :],
        np.full((P, TILES), -0.5),
        p // T == np.arange(P)[None, :] // T,
        p % T == step,
        step < p % T,
        np.where(slots // TOP == p // T, slots % TOP, 2 * T),
    ]
    return np.concatenate([np.asarray(x, np.float32) for x in parts], axis=1)


def by_rows(np, w):
    K, M = w.shape
    return w.reshape(K // P, P, M).transpose(1, 0, 2)


def by_partition(np, b):
    return b.reshape(-1, P).T


def every_token(np, b):
    return np.broadcast_to(b, (P, *b.shape))


def laid_out(np, i):
    x = np.pad(i["x"], ((0, 0), (0, T * MLP_IN // 128 - i["x"].shape[1]), (0, 0)))
    x = x.reshape(TOKENS, MLP_IN)
    a = {"consts": constants(np)}
    a["tok_x"] = by_rows(np, x.T)
    a["tok_w1"] = by_rows(np, i["L0_tok_w1"].T)
    a["tok_w2"] = by_rows(np, i["L0_tok_w2"].T)
    a["tok_b1"] = by_partition(np, i["L0_tok_b1"])
    a["tok_b2"] = every_token(np, i["L0_tok_b2"])
    e = {n[7:]: v for n, v in i.items() if n.startswith("L0_tok_")}
    layers = range(LAYERS)
    a["enc_wqkv"] = np.stack([by_rows(np, np.concatenate([e["wq"][l], e["wk"][l], e["wv"][l]]).T) for l in layers])
    a["enc_wo"] = np.stack([by_rows(np, e["wo"][l].T) for l in layers])
    a["enc_ff1"] = np.stack([by_rows(np, e["ffw1"][l].T) for l in layers])
    a["enc_ff2"] = np.stack([np.concatenate([e["ffw2"][l].T, e["ffb2"][l][None]]) for l in layers])
    a["enc_rows"] = np.stack([every_token(np, np.stack([e["bv"][l], e["bo"][l]])) for l in layers])
    a["enc_cols"] = np.stack([np.concatenate(
        [by_partition(np, e[n][l]) for n in ("ln1_s", "ln1_b", "bq", "bk", "ln2_s", "ln2_b")]
        + [np.pad(e["ffb1"][l], (0, P - TOK_FF))[:, None], np.zeros((P, 3), np.float32)], axis=1) for l in layers])
    m = {n[8:]: v for n, v in i.items() if n.startswith("L0_attn_")}

    def side(w):
        return by_rows(np, w).reshape(P, -1)

    a["mla"] = np.concatenate([side(m["W_dq"].T), m["W_dq"], m["W_uq"].T, side(m["W_uk"]), side(m["W_dkv"].T),
                               side(m["W_uv"]), side(m["W_o"].T)], axis=1)
    a["ffn_w1"] = by_rows(np, i["L0_ffn_w1"].T)
    a["ffn_w2"] = by_rows(np, i["L0_ffn_w2"].T)
    a["ffn_b1"] = by_partition(np, i["L0_ffn_b1"])
    a["ffn_b2"] = every_token(np, i["L0_ffn_b2"])
    q = {n[8:]: v for n, v in i.items() if n.startswith("L1_attn_")}
    a["mam_in"] = np.stack([by_rows(np, q["in_proj_w"][l].T) for l in layers])
    a["mam_x"] = np.stack([by_rows(np, q["x_proj_w"][l].T) for l in layers])
    a["mam_dt"] = np.stack([q["dt_proj_w"][l].T for l in layers])
    a["mam_out"] = np.stack([by_rows(np, q["out_proj_w"][l].T) for l in layers])
    a["mam_bo"] = np.stack([every_token(np, q["out_proj_b"][l]) for l in layers])
    a["mam_alog"] = np.stack([by_rows(np, q["A_log"][l]) for l in layers])
    a["mam_cols"] = np.stack([np.concatenate(
        [by_partition(np, q[n][l]) for n in ("in_proj_b", "conv_b", "dt_proj_b", "D", "norm_w")]
        + [np.zeros((P, 2), np.float32), by_rows(np, q["conv_w"][l][:, 0, :]).reshape(P, -1),
           np.zeros((P, 4), np.float32)], axis=1) for l in layers])
    a["select"] = np.broadcast_to((np.arange(96)[:, None] % 32 == np.arange(32)[None, :])[:, :, None],
                                  (96, 32, P)).astype(mybir.dt.np(BF16))
    f = {n[7:]: v for n, v in i.items() if n.startswith("L1_ffn_")}
    a["mod_rows"] = every_token(np, np.stack([q["norm_f_w"], f["w_router"], f["b2"]]))
    a["mod_b1"] = by_partition(np, f["b1"])
    a["mod_w1"] = by_rows(np, f["W1"])
    a["mod_w2"] = by_rows(np, f["W2"])
    return a


def kernel(**inputs):
    import numpy as np
    import concourse.bacc as bacc
    from concourse.bass_utils import run_bass_kernel_spmd

    arrays = {n: np.ascontiguousarray(v) for n, v in laid_out(np, {n: np.asarray(v) for n, v in inputs.items()}).items()}
    nc = bacc.Bacc("TRN2", target_bir_lowering=False, num_devices=1)
    handles = {n: nc.dram_tensor(n, v.shape, mybir.dt.from_np(v.dtype), kind="ExternalInput").ap()
               for n, v in arrays.items()}
    handles["out"] = nc.dram_tensor("out", (TOKENS, D), F32, kind="ExternalOutput").ap()
    audio_tower(nc, handles)
    got = run_bass_kernel_spmd(nc, [arrays], core_ids=[0])
    return got.results[0]["out"].reshape(SEQS, T, D)
```
